# Optimizing a Trainium2 kernel written in Bass

```python
import numpy as np
import jax
import jax.numpy as jnp

def _softmax(x, axis=-1):
    return jax.nn.softmax(x, axis=axis)

def _gelu(x):
    return jax.nn.gelu(x, approximate=True)

def _silu(x):
    return jax.nn.silu(x)

def _sigmoid(x):
    return jax.nn.sigmoid(x)

def _layernorm(x, axis=-1, eps=1e-05):
    m = jnp.mean(x, axis=axis, keepdims=True)
    v = jnp.var(x, axis=axis, keepdims=True)
    return (x - m) / jnp.sqrt(v + eps)

def _scatter_add(tgt, idx, src, axis=0):
    return tgt.at[idx].add(src)

def _segment_sum(src, seg, n):
    return jax.ops.segment_sum(src, seg, n)
kernel_name = 'mk_vit_tower_postln_d1_tok_img1024_r4_9bffa8'

def setup_inputs(seed: int=0):
    np.random.seed(seed)
    _w = jnp.asarray

    def _rec_inputs():
        import jax
        import jax.numpy as jnp
        _rk = jax.random.key(seed)
        x = jax.random.uniform(jax.random.fold_in(_rk, 1), (32, 3, 256, 256), jnp.float32, 0.0, 1)
        return x
    x = _rec_inputs()

    def _L0_tok_setup():
        import jax, jax.numpy as jnp
        import numpy as np
        _GRAY_W = (0.2989, 0.587, 0.114)
        key = jax.random.key(seed)
        x = jax.random.uniform(key, (32, 3, 256, 256), dtype=jnp.float32)
        sx = jnp.array([[-3.0, 0.0, 3.0], [-10.0, 0.0, 10.0], [-3.0, 0.0, 3.0]], dtype=jnp.float32)
        scharr = jnp.stack([sx, sx.T])[:, None, :, :]
        return {'x': x, 'scharr': scharr}
    _L0_tok_all = _L0_tok_setup()
    _L0_tok_in = {k: v for k, v in _L0_tok_all.items() if k in ('scharr',)}
    del _L0_tok_all

    def _L0_attn_setup():
        import jax, jax.numpy as jnp
        import numpy as np
        N_BITS = 8
        QMAX = 2 ** N_BITS - 1

        def fake_quant(x, axis=None):
            if axis is None:
                mn = jnp.min(x)
                mx = jnp.max(x)
            else:
                red = tuple((i for i in range(x.ndim) if i != axis % x.ndim))
                mn = jnp.min(x, axis=red, keepdims=True)
                mx = jnp.max(x, axis=red, keepdims=True)
            mn = jnp.minimum(mn, 0.0)
            mx = jnp.maximum(mx, 0.0)
            scale = jnp.maximum((mx - mn) / QMAX, 1e-08)
            zp = jnp.round(-mn / scale)
            q = jnp.clip(jnp.round(x / scale) + zp, 0.0, QMAX)
            dq = (q - zp) * scale
            return x + jax.lax.stop_gradient(dq - x)
        key = jax.random.key(seed)
        ks = jax.random.split(key, 5)
        B, N, C = (32, 577, 256)
        return {'x': jax.random.normal(ks[0], (B, N, C), dtype=jnp.float32), 'qkv_w': jax.random.normal(ks[1], (3 * C, C), dtype=jnp.float32) * 0.02, 'qkv_b': jax.random.normal(ks[2], (3 * C,), dtype=jnp.float32) * 0.02, 'proj_w': jax.random.normal(ks[3], (C, C), dtype=jnp.float32) * 0.02, 'proj_b': jax.random.normal(ks[4], (C,), dtype=jnp.float32) * 0.02}
    _L0_attn_all = _L0_attn_setup()
    _L0_attn_in = {k: v for k, v in _L0_attn_all.items() if k in ('qkv_w', 'qkv_b', 'proj_w', 'proj_b')}
    del _L0_attn_all

    def _L0_ffn_setup():
        import jax, jax.numpy as jnp
        import numpy as np
        B, S, H = (1, 512, 256)
        E, K = (16, 4)
        G, TG = (4, 2)
        I_MOE = 128
        N_SH = 2
        SCALE = 2.5

        def _mlp(x, gw, uw, dw):
            return jax.nn.silu(x @ gw.T) * (x @ uw.T) @ dw.T

        def _route(x2d, router_weight, e_bias):
            T = x2d.shape[0]
            scores = jax.nn.sigmoid(x2d @ router_weight.T)
            sc = scores + e_bias[None, :]
            group_scores = jnp.sum(jax.lax.top_k(sc.reshape(T, G, E // G), 2)[0], axis=-1)
            _, gidx = jax.lax.top_k(group_scores, TG)
            gmask = jnp.zeros((T, G), sc.dtype).at[jnp.arange(T)[:, None], gidx].set(1.0)
            smask = jnp.repeat(gmask, E // G, axis=1)
            masked = jnp.where(smask > 0, sc, 0.0)
            _, tidx = jax.lax.top_k(masked, K)
            tw = jnp.take_along_axis(scores, tidx, axis=1)
            tw = tw / (jnp.sum(tw, axis=-1, keepdims=True) + 1e-20)
            tw = tw * SCALE
            return (tidx, tw)

        def _moe_forward(hidden_states, router_weight, e_bias, gate_w, up_w, down_w, sh_gate_w, sh_up_w, sh_down_w):
            orig_shape = hidden_states.shape
            x = hidden_states.reshape(-1, H)
            T = x.shape[0]
            tidx, tw = _route(x, router_weight, e_bias)
            g = jnp.einsum('th,eih->tei', x, gate_w)
            u = jnp.einsum('th,eih->tei', x, up_w)
            h = jax.nn.silu(g) * u
            yo = jnp.einsum('tei,ehi->teh', h, down_w)
            combine = jnp.zeros((T, E), tw.dtype).at[jnp.arange(T)[:, None], tidx].add(tw)
            routed = jnp.einsum('te,teh->th', combine, yo)
            shared = _mlp(hidden_states.reshape(-1, H), sh_gate_w, sh_up_w, sh_down_w)
            return (routed + shared).reshape(orig_shape)
        key = jax.random.key(seed)
        ks = jax.random.split(key, 9)
        s = 0.02
        return {'hidden_states': jax.random.normal(ks[0], (B, S, H), jnp.float32), 'router_weight': jax.random.normal(ks[1], (E, H), jnp.float32) * s, 'e_bias': jnp.zeros((E,), jnp.float32), 'gate_w': jax.random.normal(ks[2], (E, I_MOE, H), jnp.float32) * s, 'up_w': jax.random.normal(ks[3], (E, I_MOE, H), jnp.float32) * s, 'down_w': jax.random.normal(ks[4], (E, H, I_MOE), jnp.float32) * s, 'sh_gate_w': jax.random.normal(ks[5], (N_SH * I_MOE, H), jnp.float32) * s, 'sh_up_w': jax.random.normal(ks[6], (N_SH * I_MOE, H), jnp.float32) * s, 'sh_down_w': jax.random.normal(ks[7], (H, N_SH * I_MOE), jnp.float32) * s}
    _L0_ffn_all = _L0_ffn_setup()
    _L0_ffn_in = {k: v for k, v in _L0_ffn_all.items() if k in ('router_weight', 'e_bias', 'gate_w', 'up_w', 'down_w', 'sh_gate_w', 'sh_up_w', 'sh_down_w')}
    del _L0_ffn_all
    return {'x': x, 'L0_tok_scharr': _L0_tok_in['scharr'], 'L0_attn_qkv_w': _L0_attn_in['qkv_w'], 'L0_attn_qkv_b': _L0_attn_in['qkv_b'], 'L0_attn_proj_w': _L0_attn_in['proj_w'], 'L0_attn_proj_b': _L0_attn_in['proj_b'], 'L0_ffn_router_weight': _L0_ffn_in['router_weight'], 'L0_ffn_e_bias': _L0_ffn_in['e_bias'], 'L0_ffn_gate_w': _L0_ffn_in['gate_w'], 'L0_ffn_up_w': _L0_ffn_in['up_w'], 'L0_ffn_down_w': _L0_ffn_in['down_w'], 'L0_ffn_sh_gate_w': _L0_ffn_in['sh_gate_w'], 'L0_ffn_sh_up_w': _L0_ffn_in['sh_up_w'], 'L0_ffn_sh_down_w': _L0_ffn_in['sh_down_w']}

def reference(x, L0_tok_scharr, L0_attn_qkv_w, L0_attn_qkv_b, L0_attn_proj_w, L0_attn_proj_b, L0_ffn_router_weight, L0_ffn_e_bias, L0_ffn_gate_w, L0_ffn_up_w, L0_ffn_down_w, L0_ffn_sh_gate_w, L0_ffn_sh_up_w, L0_ffn_sh_down_w):
    import jax
    import jax.numpy as jnp

    def _L0_tok_ref(x, scharr):
        import jax, jax.numpy as jnp
        import numpy as np
        _GRAY_W = (0.2989, 0.587, 0.114)
        w = jnp.asarray(_GRAY_W, dtype=x.dtype)
        gray = jnp.einsum('bchw,c->bhw', x, w)[:, None]
        edges = jax.lax.conv_general_dilated(gray, scharr, window_strides=(1, 1), padding='SAME', dimension_numbers=('NCHW', 'OIHW', 'NCHW'))
        abs_edges = jnp.sqrt(jnp.square(edges))
        edge = abs_edges.sum(axis=1) / 2
        return edge

    def _L0_attn_ref(x, qkv_w, qkv_b, proj_w, proj_b):
        import jax, jax.numpy as jnp
        import numpy as np
        N_BITS = 8
        QMAX = 2 ** N_BITS - 1

        def fake_quant(x, axis=None):
            if axis is None:
                mn = jnp.min(x)
                mx = jnp.max(x)
            else:
                red = tuple((i for i in range(x.ndim) if i != axis % x.ndim))
                mn = jnp.min(x, axis=red, keepdims=True)
                mx = jnp.max(x, axis=red, keepdims=True)
            mn = jnp.minimum(mn, 0.0)
            mx = jnp.maximum(mx, 0.0)
            scale = jnp.maximum((mx - mn) / QMAX, 1e-08)
            zp = jnp.round(-mn / scale)
            q = jnp.clip(jnp.round(x / scale) + zp, 0.0, QMAX)
            dq = (q - zp) * scale
            return x + jax.lax.stop_gradient(dq - x)
        B, N, C = x.shape
        H = 16
        D = C // H
        scale = 1.0 / jnp.sqrt(jnp.float32(D))
        xq = fake_quant(x, axis=-1)
        wq = fake_quant(qkv_w, axis=0)
        qkv = xq @ wq.T + qkv_b
        qkv = qkv.reshape(B, N, 3, H, D).transpose(2, 0, 3, 1, 4)
        q, k, v = (qkv[0], qkv[1], qkv[2])
        attn = jnp.einsum('bhnd,bhmd->bhnm', fake_quant(q), fake_quant(k)) * scale
        attn = jax.nn.softmax(attn, axis=-1)
        out = jnp.einsum('bhnm,bhmd->bhnd', attn, fake_quant(v))
        out = out.transpose(0, 2, 1, 3).reshape(B, N, C)
        oq = fake_quant(out)
        pw = fake_quant(proj_w, axis=0)
        return oq @ pw.T + proj_b

    def _L0_ffn_ref(hidden_states, router_weight, e_bias, gate_w, up_w, down_w, sh_gate_w, sh_up_w, sh_down_w):
        import jax, jax.numpy as jnp
        import numpy as np
        B, S, H = (1, 512, 256)
        E, K = (16, 4)
        G, TG = (4, 2)
        I_MOE = 128
        N_SH = 2
        SCALE = 2.5

        def _mlp(x, gw, uw, dw):
            return jax.nn.silu(x @ gw.T) * (x @ uw.T) @ dw.T

        def _route(x2d, router_weight, e_bias):
            T = x2d.shape[0]
            scores = jax.nn.sigmoid(x2d @ router_weight.T)
            sc = scores + e_bias[None, :]
            group_scores = jnp.sum(jax.lax.top_k(sc.reshape(T, G, E // G), 2)[0], axis=-1)
            _, gidx = jax.lax.top_k(group_scores, TG)
            gmask = jnp.zeros((T, G), sc.dtype).at[jnp.arange(T)[:, None], gidx].set(1.0)
            smask = jnp.repeat(gmask, E // G, axis=1)
            masked = jnp.where(smask > 0, sc, 0.0)
            _, tidx = jax.lax.top_k(masked, K)
            tw = jnp.take_along_axis(scores, tidx, axis=1)
            tw = tw / (jnp.sum(tw, axis=-1, keepdims=True) + 1e-20)
            tw = tw * SCALE
            return (tidx, tw)

        def _moe_forward(hidden_states, router_weight, e_bias, gate_w, up_w, down_w, sh_gate_w, sh_up_w, sh_down_w):
            orig_shape = hidden_states.shape
            x = hidden_states.reshape(-1, H)
            T = x.shape[0]
            tidx, tw = _route(x, router_weight, e_bias)
            g = jnp.einsum('th,eih->tei', x, gate_w)
            u = jnp.einsum('th,eih->tei', x, up_w)
            h = jax.nn.silu(g) * u
            yo = jnp.einsum('tei,ehi->teh', h, down_w)
            combine = jnp.zeros((T, E), tw.dtype).at[jnp.arange(T)[:, None], tidx].add(tw)
            routed = jnp.einsum('te,teh->th', combine, yo)
            shared = _mlp(hidden_states.reshape(-1, H), sh_gate_w, sh_up_w, sh_down_w)
            return (routed + shared).reshape(orig_shape)
        return _moe_forward(hidden_states, router_weight, e_bias, gate_w, up_w, down_w, sh_gate_w, sh_up_w, sh_down_w)
    h = _L0_tok_ref(x, L0_tok_scharr)
    h = _layernorm(h + _L0_attn_ref(h, L0_attn_qkv_w, L0_attn_qkv_b, L0_attn_proj_w, L0_attn_proj_b), axis=-1)
    h = _layernorm(h + _L0_ffn_ref(h, L0_ffn_router_weight, L0_ffn_e_bias, L0_ffn_gate_w, L0_ffn_up_w, L0_ffn_down_w, L0_ffn_sh_gate_w, L0_ffn_sh_up_w, L0_ffn_sh_down_w), axis=-1)
    return h

_drawn_inputs = setup_inputs


def setup_inputs(seed=0):
    import zlib

    import numpy as np

    out = dict(_drawn_inputs(seed))
    spreads = {'L0_ffn_e_bias': (0.0, 0.507)}
    factors = {'L0_attn_qkv_b': 8.0,
     'L0_attn_proj_b': 3.71,
     'L0_ffn_router_weight': 7.449,
     'L0_ffn_gate_w': 3.812,
     'L0_ffn_up_w': 3.753,
     'L0_ffn_down_w': 3.753,
     'L0_ffn_sh_gate_w': 3.403,
     'L0_ffn_sh_up_w': 3.356,
     'L0_ffn_sh_down_w': 3.376}
    for name, (base, spread) in spreads.items():
        noise = np.random.default_rng([zlib.crc32(name.encode()), seed]).standard_normal(out[name].shape)
        drawn = base * np.exp(spread * noise) if base else spread * noise
        out[name] = jnp.asarray(drawn.astype(out[name].dtype))
    for name, factor in factors.items():
        out[name] = (out[name] * factor).astype(out[name].dtype)
    return out
```

```python
import concourse.bass as bass
from concourse import mybir
from contextlib import ExitStack

F32 = mybir.dt.float32
F32R = mybir.dt.float32r
BF16 = mybir.dt.bfloat16
ALU = mybir.AluOpType
ACT = mybir.ActivationFunctionType
AXX = mybir.AxisListType.X
RMAX = bass.bass_isa.ReduceOp.max

P = 128
B = 32
N = 256
C = 256
KC = C // P
T = B * N
H, D = 16, 16
G, J = 4, 4
E, I = 16, 128
NE = E + 2
CH = 512
NCH = T // CH
NT = CH // P
QMAX = 255.0
MAGIC = 12582912.0
GRAY = (0.2989 * 0.5, 0.587 * 0.5, 0.114 * 0.5)
LN_EPS = 1e-5
BW = 131


class Chain:

    def __init__(self, eng, sem, i=0, per=0, base=0):
        self.eng, self.sem, self.start, self.n, self.per = eng, sem, i * per + base, 0, per

    def __call__(self, ins):
        self.n += 1
        ins.then_inc(self.sem, 1)
        self.eng.wait_ge(self.sem, self.start + self.n)

    def close(self):
        assert self.n == self.per, (self.n, self.per)


def wait_apart(eng, sem, value, tick):
    eng.wait_ge(sem, value)
    eng.sem_inc(tick, 1)


def quant_scalars(dve, link, mx, mn, scale, inv, top, tmp):
    nc = dve.bass
    link(nc.vector.tensor_scalar(mx, mx, 0.0, None, ALU.max))
    link(nc.vector.tensor_scalar(mn, mn, 0.0, None, ALU.min))
    link(nc.vector.tensor_tensor(tmp, mx, mn, ALU.subtract))
    link(nc.vector.tensor_scalar(scale, tmp, 1.0 / QMAX, 1e-8, ALU.mult, ALU.max))
    link(nc.vector.reciprocal(inv, scale))
    link(nc.vector.tensor_tensor(tmp, mn, inv, ALU.mult))
    link(nc.vector.tensor_scalar(tmp, tmp, MAGIC, None, ALU.add))
    link(nc.vector.tensor_scalar(top, tmp, QMAX, None, ALU.add))


def build(nc, x, scharr, qkv_w, qkv_b, qkv_b_col, proj_w, proj_b_col, router_t, e_bias, gate_t, up_t, down_t, out):
    hs = nc.dram_tensor("edges_scratch", (P, KC, T), F32).ap()
    qk_s = nc.dram_tensor("qk_scratch", (4 * P, T), F32).ap()
    at_s = nc.dram_tensor("attn_scratch", (P, T // P, C), F32).ap()
    v_s = nc.dram_tensor("v_scratch", (T, C), F32).ap()

    with ExitStack() as whole:
        def sem(name):
            return whole.enter_context(nc.semaphore(name))

        def keep(name, shape, dt=F32):
            return whole.enter_context(nc.sbuf_tensor(name, shape, dt))

        link_sem = sem("dve_link")
        ident = keep("ident", [P, P])
        identb = keep("identb", [P, P], BF16)
        magic = keep("magic", [P, 1])
        pint = keep("proj_int_T", [P, KC, C], BF16)
        pscale = keep("proj_scale", [P, KC])
        pb = keep("proj_bias", [P, KC])
        omx = keep("attn_max", [P, B])
        omn = keep("attn_min", [P, B])
        mx = keep("qkv_max", [P, 3, NCH])
        mn = keep("qkv_min", [P, 3, NCH])
        s_tick = sem("waits_apart")
        links = [0]

        def linker(dve):
            c = Chain(dve, link_sem, base=links[0])
            return c

        def linked(c):
            links[0] += c.n

        with ExitStack() as ab:
            def sb(name, shape, dt=F32):
                return ab.enter_context(nc.sbuf_tensor(name, shape, dt))
            hT = sb("edges_T", [P, KC, T])
            cmax = sb("cmax", [P, KC, NCH])
            wdq = sb("wdq", [P, 6, C])
            qb = sb("qkv_bias", [P, 6])
            vb = sb("v_bias", [P, C])
            band = sb("band", [P, 3, 2, BW])

            with ExitStack() as st:
                def sb(name, shape, dt=F32):
                    return st.enter_context(nc.sbuf_tensor(name, shape, dt))
                taps = sb("taps", [P, 18])
                diag = sb("diag", [P, 3, BW])
                w_raw = sb("w_raw", [P, 8, C])
                w_y = sb("w_y", [P, 8, C])
                p_q = sb("p_q", [P, KC, C], BF16)
                wmx, wmn, wsc, winv, wtop, wtmp = (sb(n, [P, 8]) for n in ("wmx", "wmn", "wsc", "winv", "wtop", "wtmp"))
                pT = st.enter_context(nc.psum_tensor("pT", [P, KC, C], BF16))
                s_w, s_zero, s_diag, s_dq, s_pq, s_pt, s_gst = (sem(n) for n in (
                    "setup_loaded", "setup_zeroed", "diag_ready", "wdq_ready", "pq_ready", "pt_ready", "gate_setup"))
                s_ib = sem("identb_ready")
                with nc.Block() as block:
                    @block.sync
                    def _(sp):
                        sp.dma_start(w_raw[:, 0:6, :], qkv_w.rearrange("(t p) c -> p t c", p=P)).then_inc(s_w, 16)
                        sp.dma_start(w_raw[:, 6:8, :], proj_w.rearrange("(t p) c -> p t c", p=P)).then_inc(s_w, 16)
                        sp.dma_start(taps[:, :], scharr.rearrange("f o a b -> o (f a b)").broadcast_to([P, 18])).then_inc(s_w, 16)
                        sp.dma_start(qb[:, :], qkv_b_col).then_inc(s_w, 16)
                        sp.dma_start(pb[:, :], proj_b_col).then_inc(s_w, 16)
                        sp.dma_start(vb[:, :], qkv_b.rearrange("(o n) -> o n", o=1)[:, 2 * C:3 * C].broadcast_to([P, C])).then_inc(s_w, 16)
                        sp.wait_ge(s_w, 96)

                    @block.gpsimd
                    def _(pool):
                        nc.gpsimd.memset(diag[:], 0.0).then_inc(s_zero, 1)
                        nc.gpsimd.memset(ident[:], 0.0).then_inc(s_zero, 1)
                        pool.wait_ge(s_zero, 2)
                        for dy in range(3):
                            nc.gpsimd.affine_select(out=diag[:, dy, :], in_=diag[:, dy, :], compare_op=ALU.not_equal,
                                                    fill=1.0, base=2 - dy, pattern=[[-1, BW]],
                                                    channel_multiplier=1).then_inc(s_diag, 1)
                        nc.gpsimd.affine_select(out=ident[:, :], in_=ident[:, :], compare_op=ALU.not_equal,
                                                fill=1.0, base=0, pattern=[[-1, P]],
                                                channel_multiplier=1).then_inc(s_diag, 1)

                    @block.vector
                    def _(dve):
                        link = linker(dve)
                        link(nc.vector.memset(magic[:], MAGIC))
                        dve.wait_ge(s_diag, 4)
                        nc.vector.tensor_copy(identb[:, :], ident[:, :]).then_inc(s_ib, 1)
                        dve.wait_ge(s_w, 96)
                        for dx in range(3):
                            for f in range(2):
                                o = band[:, dx, f, :]
                                k = 9 * f + dx
                                link(nc.vector.tensor_scalar(o, diag[:, 0, :], taps[:, k:k + 1], None, ALU.mult))
                                link(nc.vector.scalar_tensor_tensor(o, diag[:, 1, :], taps[:, k + 3:k + 4], o, ALU.mult, ALU.add))
                                link(nc.vector.scalar_tensor_tensor(o, diag[:, 2, :], taps[:, k + 6:k + 7], o, ALU.mult, ALU.add))
                        link(nc.vector.tensor_reduce(wmx[:, :], w_raw[:, :, :], AXX, ALU.max))
                        link(nc.vector.tensor_reduce(wmn[:, :], w_raw[:, :, :], AXX, ALU.min))
                        quant_scalars(dve, link, wmx[:, :], wmn[:, :], wsc[:, :], winv[:, :], wtop[:, :], wtmp[:, :])
                        for t in range(8):
                            link(nc.vector.tensor_scalar(w_y[:, t, :], w_raw[:, t, :], winv[:, t:t + 1], MAGIC, ALU.mult, ALU.add))
                            link(nc.vector.tensor_scalar(w_y[:, t, :], w_y[:, t, :], wtop[:, t:t + 1], MAGIC, ALU.min, ALU.subtract))
                            if t < 6:
                                link(nc.vector.tensor_scalar(wdq[:, t, :], w_y[:, t, :], wsc[:, t:t + 1], None, ALU.mult))
                        link(nc.vector.tensor_copy(pscale[:, :], wsc[:, 6:8]))
                        for t in range(KC):
                            for k in range(KC):
                                o = p_q[:, t, k * P:(k + 1) * P].rearrange("p (g j d) -> p j g d", g=2, j=J)
                                i_ = w_y[:, 6 + t, k * P:(k + 1) * P].rearrange("p (j g d) -> p j g d", g=2, j=J)
                                nc.vector.tensor_copy(o, i_).then_inc(s_pq, 1)
                        dve.wait_ge(s_pt, 1)
                        link(nc.vector.tensor_copy(pint[:, :, :], pT[:, :, :]))
                        linked(link)

                    @block.tensor
                    def _(pe):
                        pe.wait_ge(s_ib, 1)
                        pe.wait_ge(s_pq, 4)
                        for k in range(KC):
                            for t in range(KC):
                                last = nc.tensor.transpose(pT[:, k, t * P:(t + 1) * P], p_q[:, t, k * P:(k + 1) * P], identb[:, :])
                        last.then_inc(s_pt, 1)

            with ExitStack() as st:
                def sb(name, shape, dt=F32):
                    return st.enter_context(nc.sbuf_tensor(name, shape, dt))
                xin = [sb(f"xin{a}", [P, 3, 2, C]) for a in range(2)]
                gt = [sb(f"gt{a}", [P, 2, C]) for a in range(2)]
                gray = [sb(f"gray{a}", [P, 2, C + 2]) for a in range(2)]
                gx = [sb(f"gx{a}", [P, 2, N]) for a in range(4)]
                pc = [st.enter_context(nc.psum_tensor(f"pc{a}", [P, 2, N], F32)) for a in range(4)]
                s_x = [sem(f"x_loaded{a}") for a in range(2)]
                s_gt = [sem(f"gray_red_ready{a}") for a in range(2)]
                s_gray = [sem(f"gray_ready{a}") for a in range(2)]
                s_conv = [sem(f"conv_done{a}") for a in range(4)]
                s_gx = [sem(f"gx_ready{a}") for a in range(4)]
                s_h = [sem(f"edges_ready{a}") for a in range(4)]
                s_g1 = sem("gray_half")
                s_spill = sem("edges_spilled")
                s_cm = sem("cmax_part")
                HALF = B // 2

                with nc.Block() as block:
                    @block.sync
                    def _(sp):
                        def load(b, i, a):
                            sp.wait_ge(s_gray[a], i)
                            sp.dma_start(xin[a][:, :, :, :], x[b]).then_inc(s_x[a], 16)

                        def spill(i):
                            for k in range(4):
                                sp.wait_ge(s_h[k], i + 1)
                            sp.dma_start(hs[:, :, bass.ds(i * CH, CH)], hT[:, :, bass.ds(i * CH, CH)]).then_inc(s_spill, 16)
                        load(0, 0, 0)
                        load(1, 0, 1)
                        def turn(i):
                            load(i * 2 + 2, i + 1, 0)
                            load(i * 2 + 3, i + 1, 1)
                            spill(i)

                        turn(0)
                        with sp.Fori(1, HALF - 1) as i:
                            turn(i)
                        spill(HALF - 1)
                        sp.wait_ge(s_spill, 16 * HALF)

                    @block.scalar
                    def _(act):
                        def red(i, a):
                            act.wait_ge(s_x[a], i * 16 + 16)
                            act.wait_ge(s_gray[a], i)
                            nc.scalar.activation(gt[a][:, :, :], xin[a][:, 0, :, :], ACT.Copy, scale=GRAY[0]).then_inc(s_gt[a], 1)

                        def absx(i, a):
                            for k in range(KC):
                                m = 2 * a + k
                                act.wait_ge(s_conv[m], i + 1)
                                act.wait_ge(s_h[m], i)
                                nc.scalar.activation(gx[m][:, :, :], pc[m][:, :, :], ACT.Abs).then_inc(s_gx[m], 1)
                        red(0, 0)
                        def turn(i):
                            red(i, 1)
                            absx(i, 0)
                            red(i + 1, 0)
                            absx(i, 1)

                        turn(0)
                        with act.Fori(1, HALF - 1) as i:
                            turn(i)
                        red(HALF - 1, 1)
                        absx(HALF - 1, 0)
                        absx(HALF - 1, 1)

                    @block.vector
                    def _(dve):
                        link = linker(dve)
                        for a in range(2):
                            link(nc.vector.memset(gray[a][:], 0.0))

                        def grays(i, a):
                            dve.wait_ge(s_gt[a], i + 1)
                            dve.wait_ge(s_conv[2 * a + 1], i)
                            nc.vector.scalar_tensor_tensor(gray[a][:, :, 1:C + 1], xin[a][:, 1, :, :], GRAY[1], gt[a][:, :, :],
                                                           ALU.mult, ALU.add).then_inc(s_g1, 1)
                            dve.wait_ge(s_g1, i * 2 + a + 1)
                            nc.vector.scalar_tensor_tensor(gray[a][:, :, 1:C + 1], xin[a][:, 2, :, :], GRAY[2], gray[a][:, :, 1:C + 1],
                                                           ALU.mult, ALU.add).then_inc(s_gray[a], 1)

                        def edges(i, a):
                            for k in range(KC):
                                m = 2 * a + k
                                dve.wait_ge(s_gx[m], i + 1)
                                nc.vector.tensor_tensor(hT[:, k, bass.ds(i * CH + a * N, N)], gx[m][:, 0, :], gx[m][:, 1, :],
                                                        ALU.add).then_inc(s_h[m], 1)

                        def maxes(i):
                            for k in range(KC):
                                dve.wait_ge(s_h[k], i + 1)
                                dve.wait_ge(s_h[2 + k], i + 1)
                                nc.vector.reduce_max(cmax[:, k, bass.ds(i, 1)], hT[:, k, bass.ds(i * CH, CH)], AXX).then_inc(s_cm, 1)
                        grays(0, 0)
                        def turn(i):
                            grays(i, 1)
                            edges(i, 0)
                            grays(i + 1, 0)
                            edges(i, 1)
                            maxes(i)

                        turn(0)
                        with dve.Fori(1, HALF - 1) as i:
                            turn(i)
                        grays(HALF - 1, 1)
                        edges(HALF - 1, 0)
                        edges(HALF - 1, 1)
                        maxes(HALF - 1)
                        linked(link)

                    @block.tensor
                    def _(pe):
                        def conv(i, a):
                            pe.wait_ge(s_gray[a], i + 1)
                            for k in range(KC):
                                m = 2 * a + k
                                pe.wait_ge(s_h[m], i)
                                for t in range(2):
                                    for dx in range(3):
                                        last = nc.tensor.matmul(
                                            pc[m][:, :, 127 * t:127 * t + 129],
                                            gray[a][:, t, k * P + dx:k * P + dx + P],
                                            band[:, dx, :, 1 - t:130 - t],
                                            start=(t == 0 and dx == 0), stop=(t == 1 and dx == 2), skip_group_check=True)
                                last.then_inc(s_conv[m], 1)
                        def turn(i):
                            conv(i, 0)
                            conv(i, 1)

                        turn(0)
                        with pe.Fori(1, HALF) as i:
                            turn(i)

            with ExitStack() as st:
                def sb(name, shape, dt=F32):
                    return st.enter_context(nc.sbuf_tensor(name, shape, dt))
                cm, csc, cinv = (sb(n, [P, KC]) for n in ("cm", "cscale", "cinv"))
                wf = sb("wf", [P, KC, 6 * P])
                whi = sb("w_hi", [P, KC, 6 * P], F32R)
                wlo = sb("w_lo", [P, KC, 6 * P], F32R)
                xa = sb("xa", [P, KC, CH])
                xr = [sb(f"xr{a}", [P, KC, CH], F32R) for a in range(2)]
                qk = [sb(f"qk{a}", [P, 4, CH]) for a in range(2)]
                vt = [sb(f"vt{a}", [P, NT, C]) for a in range(2)]
                pq = [st.enter_context(nc.psum_tensor(f"pq{a}", [P, CH], F32)) for a in range(4)]
                pv = [st.enter_context(nc.psum_tensor(f"pv{a}", [P, 2, C], F32)) for a in range(4)]
                s_cs, s_wT, s_wf, s_wl = (sem(n) for n in ("cscale_ready", "wT_ready", "wf_ready", "w_split"))
                s_xa = sem("xa_ready")
                s_xr = sem("xr_ready")
                s_q = [sem(f"q_done{a}") for a in range(4)]
                s_v = [sem(f"v_done{a}") for a in range(4)]
                s_qk = sem("qk_ready")
                s_vt = sem("vt_ready")
                s_mm = sem("qkv_minmax")
                s_qst = [sem(f"qk_stored{a}") for a in range(2)]
                s_vst = [sem(f"v_stored{a}") for a in range(2)]

                with nc.Block() as block:
                    @block.tensor
                    def _(pe):
                        for m in range(6):
                            for k in range(KC):
                                n = m * KC + k
                                last = nc.tensor.transpose(pq[n // 4][:, (n % 4) * P:(n % 4 + 1) * P],
                                                           wdq[:, m, k * P:(k + 1) * P], ident[:, :])
                        last.then_inc(s_wT, 1)
                        pe.wait_ge(s_wl, 2)

                        def chunk(i, a):
                            n = i * 2 + a
                            pe.wait_ge(s_xr, n + 1)
                            for m in range(4):
                                pe.wait_ge(s_qk, n * 4 + m)
                                for k in range(KC):
                                    for w in (whi, wlo):
                                        last = nc.tensor.matmul(pq[m][:, :], w[:, k, m * P:(m + 1) * P], xr[a][:, k, :],
                                                                start=(k == 0 and w is whi), stop=(k == 1 and w is wlo))
                                last.then_inc(s_q[m], 1)
                            pe.wait_ge(s_vt, i * 4 + 2 * a)
                            for h in range(2):
                                for t in range(2):
                                    tt = 2 * h + t
                                    for k in range(KC):
                                        for w in (whi, wlo):
                                            last = nc.tensor.matmul(pv[2 * a + h][:, t, :], xr[a][:, k, tt * P:(tt + 1) * P],
                                                                    w[:, k, 4 * P:6 * P],
                                                                    start=(k == 0 and w is whi), stop=(k == 1 and w is wlo))
                                last.then_inc(s_v[2 * a + h], 1)
                        def turn(i):
                            chunk(i, 0)
                            chunk(i, 1)

                        turn(0)
                        with pe.Fori(1, NCH // 2) as i:
                            turn(i)

                    @block.scalar
                    def _(act):
                        act.wait_ge(s_wf, 12)
                        nc.scalar.copy(whi[:, :, :], wf[:, :, :]).then_inc(s_wl, 1)

                        def rounded(n):
                            act.wait_ge(s_xr, n)
                            for k in range(KC):
                                nc.scalar.activation(xa[:, k, :], hT[:, k, bass.ds(n * CH, CH)], ACT.Identity, bias=magic[:, 0:1],
                                                     scale=cinv[:, k:k + 1]).then_inc(s_xa, 1)

                        def chunk(i, a, more=True):
                            n = i * 2 + a
                            if more:
                                rounded(n + 1)
                            act.wait_ge(s_qst[a], i * 16)
                            act.wait_ge(s_mm, (i * 2 + a) * 6)
                            for m in range(4):
                                act.wait_ge(s_q[m], n + 1)
                                nc.scalar.activation(qk[a][:, m, :], pq[m][:, :], ACT.Identity, bias=qb[:, m:m + 1]).then_inc(s_qk, 1)
                        act.wait_ge(s_cs, 1)
                        rounded(0)
                        def turn(i):
                            chunk(i, 0)
                            chunk(i, 1)

                        turn(0)
                        with act.Fori(1, NCH // 2 - 1) as i:
                            turn(i)
                        chunk(NCH // 2 - 1, 0)
                        chunk(NCH // 2 - 1, 1, more=False)

                    @block.vector
                    def _(dve):
                        link = linker(dve)
                        link(nc.vector.reduce_max(cm[:, :], cmax[:, :, :], AXX))
                        link(nc.vector.tensor_scalar(csc[:, :], cm[:, :], 0.0, 1.0 / QMAX, ALU.max, ALU.mult))
                        link(nc.vector.tensor_scalar(csc[:, :], csc[:, :], 1e-8, None, ALU.max))
                        nc.vector.reciprocal(cinv[:, :], csc[:, :]).then_inc(s_cs, 1)
                        dve.wait_ge(s_wT, 1)
                        for m in range(6):
                            for k in range(KC):
                                n = m * KC + k
                                nc.vector.tensor_scalar(wf[:, k, m * P:(m + 1) * P], pq[n // 4][:, (n % 4) * P:(n % 4 + 1) * P],
                                                        csc[:, k:k + 1], None, ALU.mult).then_inc(s_wf, 1)
                        dve.wait_ge(s_wl, 1)
                        nc.vector.tensor_tensor(wlo[:, :, :], wf[:, :, :], whi[:, :, :].bitcast(F32), ALU.subtract).then_inc(s_wl, 1)

                        def quant(i, a):
                            n = i * 2 + a
                            dve.wait_ge(s_xa, n * 2 + 2)
                            dve.wait_ge(s_v[2 * a + 1], i)
                            nc.vector.tensor_scalar(xr[a][:, :, :], xa[:, :, :], MAGIC + QMAX, MAGIC, ALU.min, ALU.subtract).then_inc(s_xr, 1)

                        def chunk(i, a):
                            n = i * 2 + a
                            for q in range(2):
                                dve.wait_ge(s_qk, n * 4 + 2 * q + 2)
                                src = qk[a][:, 2 * q:2 * q + 2, :].rearrange("p a b -> p (a b)")
                                nc.vector.tensor_reduce(mx[:, q, bass.ds(n, 1)], src, AXX, ALU.max).then_inc(s_mm, 1)
                                nc.vector.tensor_reduce(mn[:, q, bass.ds(n, 1)], src, AXX, ALU.min).then_inc(s_mm, 1)
                            dve.wait_ge(s_vst[a], i * 16)
                            for h in range(2):
                                dve.wait_ge(s_v[2 * a + h], i + 1)
                                nc.vector.tensor_tensor(vt[a][:, 2 * h:2 * h + 2, :], pv[2 * a + h][:, :, :],
                                                        vb[:, :].unsqueeze(1).broadcast_to([P, 2, C]), ALU.add).then_inc(s_vt, 1)
                            dve.wait_ge(s_vt, n * 2 + 2)
                            src = vt[a][:, :, :].rearrange("p a b -> p (a b)")
                            nc.vector.tensor_reduce(mx[:, 2, bass.ds(n, 1)], src, AXX, ALU.max).then_inc(s_mm, 1)
                            nc.vector.tensor_reduce(mn[:, 2, bass.ds(n, 1)], src, AXX, ALU.min).then_inc(s_mm, 1)
                        quant(0, 0)
                        def turn(i):
                            quant(i, 1)
                            chunk(i, 0)
                            quant(i + 1, 0)
                            chunk(i, 1)

                        turn(0)
                        with dve.Fori(1, NCH // 2 - 1) as i:
                            turn(i)
                        quant(NCH // 2 - 1, 1)
                        chunk(NCH // 2 - 1, 0)
                        chunk(NCH // 2 - 1, 1)
                        linked(link)

                    @block.sync
                    def _(sp):
                        def store(i, a):
                            n = i * 2 + a
                            sp.wait_ge(s_qk, n * 4 + 4)
                            sp.dma_start(qk_s.rearrange("(m p) t -> p m t", p=P)[:, :, bass.ds(n * CH, CH)], qk[a][:, :, :]).then_inc(s_qst[a], 16)
                            sp.wait_ge(s_vt, n * 2 + 2)
                            sp.dma_start(v_s.rearrange("(t p) c -> p t c", p=P)[:, bass.ds(n * NT, NT), :], vt[a][:, :, :]).then_inc(s_vst[a], 16)
                        def turn(i):
                            store(i, 0)
                            store(i, 1)

                        turn(0)
                        with sp.Fori(1, NCH // 2) as i:
                            turn(i)
                        for a in range(2):
                            sp.wait_ge(s_qst[a], 16 * (NCH // 2))
                            sp.wait_ge(s_vst[a], 16 * (NCH // 2))

        with ExitStack() as at:
            def sb(name, shape, dt=F32):
                return at.enter_context(nc.sbuf_tensor(name, shape, dt))

            def ps(name, shape, dt=F32):
                return at.enter_context(nc.psum_tensor(name, shape, dt))
            ext = sb("qkv_ext", [P, 2, 3])
            exta = sb("qkv_ext_all", [P, 2, 3])
            qsc, qinv, qtop, qtmp = (sb(n, [P, 3]) for n in ("qkv_scale", "qkv_inv", "qkv_top", "qkv_tmp"))
            esc = sb("exp_scale", [P, 1])
            aug = sb("aug_rows", [P, 2, J])
            own = sb("own_rows", [P, 2, J])
            ownr = sb("own_any", [P, 2])
            qinvm = sb("q_inv_masked", [P, 2])
            raw = [sb(f"raw{r}", [P, 6, N]) for r in range(3)]
            ki = [sb(f"ki{r}", [P, 2, N], BF16) for r in range(3)]
            yq = sb("yq", [P, 2, 2, N])
            QK = [sb(f"QK{r}", [P, G, 1 + J, N], BF16) for r in range(3)]
            V = [sb(f"V{r}", [P, 2, H, 32]) for r in range(3)]
            qT = sb("qT", [P, G, N], BF16)
            nm = sb("neg_max", [P, 2, H])
            attn = [sb(f"attn{r}", [P, 2, C]) for r in range(3)]
            rem = sb("neg_max_rest", [P, 2, H])
            Tm = sb("neg_max_parts", [P, 2, G, P], BF16)
            pr_ = [sb(f"probs{a}", [P, J, 2, N]) for a in range(2)]
            ot = [sb(f"ot{a}", [P, 2, N]) for a in range(2)]
            rden = [sb(f"rden{a}", [P, 2 * 2 * J]) for a in range(2)]
            pS = [ps(f"pS{a}", [P, 2, N]) for a in range(2)]
            pST = [ps(f"pST{a}", [P, 2, 2, N]) for a in range(2)]
            pO = ps("pO", [P, 2, N])
            pM = ps("pM", [P, 512])
            zT = pM[:, :].bitcast(BF16).rearrange("p (g q) -> p g q", g=G)

            s_ext, s_all, s_qsc, s_init = (sem(n) for n in ("ext_ready", "ext_reduced", "qkv_scales", "attn_init"))
            s_ld = [sem(f"raw_loaded{r}") for r in range(3)]
            s_y, s_ki, s_qq, s_vq = (sem(n) for n in ("rounded", "k_int", "q_int", "v_int"))
            s_sc = [sem(f"QK_placed{r}") for r in range(3)]
            s_S, s_red, s_m, s_z, s_qT = (sem(n) for n in ("S_done", "S_reduced", "max_parts", "max_T", "qT_ready"))
            s_st, s_exp, s_pv, s_ot, s_r, s_norm, s_run = (sem(n) for n in (
                "ST_done", "exp_done", "PV_done", "ot_ready", "R_done", "norm_done", "run_done"))
            s_ast = [sem(f"attn_stored{r}") for r in range(3)]
            s_mc, s_nc = sem("max_chain"), sem("norm_chain")
            s_aug = sem("aug_chain")

            with nc.Block() as block:
                @block.sync
                def _(sp):
                    def load(n, r):
                        sp.dma_start(raw[r][:, 0:4, :], qk_s.rearrange("(m p) t -> p m t", p=P)[:, :, bass.ds(n * N, N)]).then_inc(s_ld[r], 16)
                        sp.dma_start(raw[r][:, 4:6, :], v_s.rearrange("(t p) c -> p t c", p=P)[:, bass.ds(n * 2, 2), :]).then_inc(s_ld[r], 16)

                    def place(n, r):
                        sp.wait_ge(s_ki, n + 1)
                        for j in range(J):
                            for gm in range(2):
                                p0 = 32 * j + D * gm
                                sp.dma_start(QK[r][p0:p0 + D, gm::2, 1 + j, :], ki[r][p0:p0 + D, :, :]).then_inc(s_sc[r], 16)
                    for n in range(3):
                        load(n, n)
                    sp.wait_ge(s_init, 1)
                    place(0, 0)
                    place(1, 1)

                    def step(n, r):
                        sp.wait_ge(s_vq, n + 1)
                        sp.wait_ge(s_ki, n + 1)
                        sp.wait_ge(s_qq, n * 2 + 2)
                        load(n + 3, r)
                        sp.wait_ge(s_st, n * 8)
                        place(n + 2, (r + 2) % 3)
                    step(0, 0)
                    step(1, 1)
                    def store(n, r):
                        sp.wait_ge(s_norm, n * 2 + 2)
                        sp.dma_start(at_s[:, bass.ds(n * 2, 2), :], attn[r][:, :, :]).then_inc(s_ast[r], 16)
                    with sp.Fori(0, 9) as i:
                        for k in range(3):
                            step(i * 3 + 2 + k, (2 + k) % 3)
                            store(i * 3 + k, k)
                    sp.wait_ge(s_st, 29 * 8)
                    place(31, 1)
                    for n in range(27, 32):
                        store(n, n % 3)
                    for r, uses in enumerate((11, 11, 10)):
                        sp.wait_ge(s_ast[r], uses * 16 + 16)

                @block.gpsimd
                def _(pool):
                    nc.gpsimd.memset(ext[:, :, :], 0.0).then_inc(s_aug, 1)
                    nc.gpsimd.memset(aug[:, :], 1.0).then_inc(s_aug, 1)
                    nc.gpsimd.memset(own[:, :, :], 1.0).then_inc(s_aug, 1)
                    pool.wait_ge(s_aug, 3)
                    for t, lo, hi, sign in ((aug, -D, D + 2, 1), (own, 0, D - 1, -1)):
                        nc.gpsimd.affine_select(out=t[:, :, :], in_=t[:, :, :], compare_op=ALU.is_ge, fill=0.0, base=lo,
                                                pattern=[[sign * D, 2], [-32, J]], channel_multiplier=1).then_inc(s_aug, 1)
                    pool.wait_ge(s_aug, 5)
                    for t, lo, hi, sign in ((aug, -D, D + 2, 1), (own, 0, D - 1, -1)):
                        nc.gpsimd.affine_select(out=t[:, :, :], in_=t[:, :, :], compare_op=ALU.is_ge, fill=0.0, base=hi,
                                                pattern=[[-sign * D, 2], [32, J]], channel_multiplier=-1).then_inc(s_aug, 1)
                    pool.wait_ge(s_ext, 1)
                    nc.gpsimd.partition_all_reduce(exta[:, :, :], ext[:, :, :], P, RMAX).then_inc(s_all, 1)
                    pool.wait_ge(s_qsc, 1)
                    pool.wait_ge(s_init, 1)

                    def quant(n, r, u, st_done):
                        wait_apart(pool, s_ld[r], u * 32 + 32, s_tick)
                        for t in (1, 2):
                            nc.gpsimd.tensor_scalar(raw[r][:, 2 * t:2 * t + 2, :], raw[r][:, 2 * t:2 * t + 2, :], qinv[:, t:t + 1], MAGIC,
                                                    ALU.mult, ALU.add).then_inc(s_y, 1)
                        wait_apart(pool, s_y, n * 4 + 1, s_tick)
                        nc.gpsimd.tensor_scalar(ki[r][:, :, :], raw[r][:, 2:4, :], qtop[:, 1:2], MAGIC,
                                                ALU.min, ALU.subtract).then_inc(s_ki, 1)
                        wait_apart(pool, s_qq, n * 2, s_tick)
                        for gm in range(2):
                            nc.gpsimd.tensor_scalar(yq[:, gm, :, :], raw[r][:, 0:2, :], qinvm[:, gm:gm + 1], MAGIC,
                                                    ALU.mult, ALU.add).then_inc(s_y, 1)
                        wait_apart(pool, s_st, st_done, s_tick)
                        for gm in range(2):
                            wait_apart(pool, s_y, n * 4 + 3 + gm, s_tick)
                            nc.gpsimd.tensor_scalar(QK[r][:, gm::2, 0, :], yq[:, gm, :, :], qtop[:, 0:1], MAGIC,
                                                    ALU.min, ALU.subtract).then_inc(s_qq, 1)
                        wait_apart(pool, s_y, n * 4 + 2, s_tick)
                        nc.gpsimd.tensor_scalar(V[r][:, :, :, 0:D], raw[r][:, 4:6, :].rearrange("p t (h d) -> p t h d", d=D), qtop[:, 2:3], MAGIC,
                                                ALU.min, ALU.subtract).then_inc(s_vq, 1)

                    def step(n, r, u):
                        pool.wait_ge(s_pv, n * 4)
                        pool.wait_ge(s_sc[(r + 2) % 3], (u + (r + 2) // 3) * 128)
                        quant(n + 2, (r + 2) % 3, u + (r + 2) // 3, n * 8)
                    quant(0, 0, 0, 0)
                    quant(1, 1, 0, 0)
                    step(0, 0, 0)
                    with pool.Fori(0, 9) as i:
                        for k in range(3):
                            step(i * 3 + 1 + k, (1 + k) % 3, i + (1 + k) // 3)
                    step(28, 1, 9)
                    step(29, 2, 9)

                @block.tensor
                def _(pe):
                    def S(n, r, u, c0, c1):
                        for c in range(c0, c1):
                            g, qt, h2 = c // 4, (c // 2) % 2, c % 2
                            if c == 0:
                                pe.wait_ge(s_sc[r], u * 128 + 128)
                                pe.wait_ge(s_qq, n * 2 + 2)
                            if not (isinstance(n, int) and n == 0 and c < 2):
                                pe.wait_ge(s_red, n * 16 + c - 1)
                            nc.tensor.matmul(pS[c % 2][:, :, :], QK[r][:, g, 0, qt * P:qt * P + P], QK[r][:, g, 1 + 2 * h2:3 + 2 * h2, :],
                                             start=True, stop=True).then_inc(s_S, 1)

                    def Z(n):
                        pe.wait_ge(s_m, n * 2 + 2)
                        if not (isinstance(n, int) and n == 0):
                            pe.wait_ge(s_norm, n * 2 - 1)
                        for g in range(G):
                            for qt in range(2):
                                last = nc.tensor.transpose(zT[:, g, qt * P:qt * P + P], Tm[:, qt, g, :], identb[:, :])
                        last.then_inc(s_z, 1)

                    def ST(n, r, g, h2):
                        if g == 0 and h2 == 0:
                            pe.wait_ge(s_qT, n + 1)
                        if not (isinstance(n, int) and n == 0 and g == 0):
                            pe.wait_ge(s_exp, n * 8 + 2 * g + h2 - 1)
                        for j in range(2):
                            for kt in range(2):
                                last = nc.tensor.matmul(pST[h2][:, j, kt, :], QK[r][:, g, 1 + 2 * h2 + j, kt * P:kt * P + P],
                                                        qT[:, g, :], start=True, stop=True)
                        last.then_inc(s_st, 1)

                    def PV(n, r, g):
                        if g == 0:
                            pe.wait_ge(s_vq, n + 1)
                        pe.wait_ge(s_exp, n * 8 + 2 * g + 2)
                        if g % 2 == 0:
                            pe.wait_ge(s_ot, n * 2 + g // 2)
                        for kt in range(2):
                            for j in range(J):
                                last = nc.tensor.matmul(pO[32 * j:32 * j + 32, g % 2, :], V[r][:, kt, 8 * (g // 2) + 2 * j + g % 2, :],
                                                        pr_[g % 2][:, j, kt, :], start=(kt == 0), stop=(kt == 1))
                        last.then_inc(s_pv, 1)

                    def R(n, h):
                        pe.wait_ge(s_ot, n * 2 + h + 1)
                        if h:
                            pe.wait_ge(s_qT, n + 2)
                        else:
                            pe.wait_ge(s_norm, n * 2)
                        for qt in range(2):
                            for g in range(2):
                                c = (qt * 2 + g) * P
                                last = nc.tensor.transpose(pM[:, c:c + P], ot[h][:, g, qt * P:qt * P + P], ident[:, :])
                        last.then_inc(s_r, 1)

                    def image(n, r, u, first=False, final=False):
                        nxt = (n + 1, (r + 1) % 3, u + (r + 1) // 3)
                        more = (lambda a, b: None) if final else (lambda a, b: S(*nxt, a, b))
                        ST(n, r, 0, 0)
                        more(0, 3)
                        ST(n, r, 0, 1)
                        more(3, 6)
                        if not first:
                            PV(n - 1, (r + 2) % 3, 3)
                        ST(n, r, 1, 0)
                        more(6, 9)
                        if not first:
                            R(n - 1, 1)
                        ST(n, r, 1, 1)
                        more(9, 11)
                        PV(n, r, 0)
                        ST(n, r, 2, 0)
                        more(11, 14)
                        ST(n, r, 2, 1)
                        more(14, 16)
                        PV(n, r, 1)
                        ST(n, r, 3, 0)
                        ST(n, r, 3, 1)
                        R(n, 0)
                        PV(n, r, 2)
                        if not final:
                            Z(n + 1)
                    S(0, 0, 0, 0, 16)
                    Z(0)
                    image(0, 0, 0, first=True)
                    with pe.Fori(0, 10) as i:
                        for k in range(3):
                            image(i * 3 + 1 + k, (1 + k) % 3, i + (1 + k) // 3)
                    image(31, 1, 10, final=True)
                    PV(31, 1, 3)
                    pe.wait_ge(s_ot, 64)
                    pe.wait_ge(s_norm, 63)
                    for qt in range(2):
                        for g in range(2):
                            c = (qt * 2 + g) * P
                            last = nc.tensor.transpose(pM[:, c:c + P], ot[1][:, g, qt * P:qt * P + P], ident[:, :])
                    last.then_inc(s_r, 1)

                @block.scalar
                def _(act):
                    def exps(n, g, first=False):
                        for h2 in range(2):
                            act.wait_ge(s_st, n * 8 + 2 * g + h2 + 1)
                            if not (first and g < 2):
                                act.wait_ge(s_pv, n * 4 + g - 1)
                            nc.scalar.activation(pr_[g % 2][:, 2 * h2:2 * h2 + 2, :, :], pST[h2][:, :, :, :], ACT.Exp,
                                                 scale=esc[:, 0:1]).then_inc(s_exp, 1)

                    def evac(n, h):
                        act.wait_ge(s_pv, n * 4 + 2 * h + 2)
                        if isinstance(n, int) and n == 0:
                            act.wait_ge(s_r, 1)
                        else:
                            act.wait_ge(s_r, n * 2 + h)
                        nc.scalar.copy(ot[h][:, :, :], pO[:, :, :]).then_inc(s_ot, 1)

                    def image(n, first=False):
                        exps(n, 0, first)
                        if not first:
                            evac(n - 1, 1)
                        exps(n, 1, first)
                        exps(n, 2)
                        evac(n, 0)
                        exps(n, 3)
                    act.wait_ge(s_qsc, 1)
                    image(0, first=True)
                    with act.Fori(0, 10) as i:
                        for k in range(3):
                            image(i * 3 + 1 + k)
                    image(31)
                    evac(31, 1)

                @block.vector
                def _(dve):
                    link = linker(dve)
                    dve.wait_ge(s_aug, 1)
                    link(nc.vector.tensor_reduce(ext[:, 0, :], mx[:, :, :], AXX, ALU.max))
                    nc.vector.tensor_reduce(ext[:, 1, :], mn[:, :, :], AXX, ALU.min, negate=True).then_inc(s_ext, 1)
                    dve.wait_ge(s_aug, 7)
                    for r in range(3):
                        link(nc.vector.memset(QK[r][:, :, 0, :], 0.0))
                        for j in range(J):
                            for gm in range(2):
                                link(nc.vector.tensor_copy(QK[r][:, gm::2, 1 + j, :],
                                                           aug[:, gm, j:j + 1].unsqueeze(2).broadcast_to([P, 2, N])))
                        link(nc.vector.memset(V[r][:], 0.0))
                        link(nc.vector.memset(V[r][:, :, :, D:D + 1], 1.0))
                    for r in range(3):
                        nc.vector.memset(attn[r][:], 0.0).then_inc(s_ast[r], 16)
                    link(nc.vector.memset(ot[0][:], 0.0))
                    nc.vector.memset(ot[1][:], 0.0).then_inc(s_r, 1)
                    link(nc.vector.memset(Tm[:], 0.0))
                    nc.vector.memset(rden[0][:], 0.0).then_inc(s_init, 1)
                    dve.wait_ge(s_all, 1)
                    link(nc.vector.tensor_scalar(exta[:, 1, :], exta[:, 1, :], -1.0, None, ALU.mult))
                    quant_scalars(dve, link, exta[:, 0, :], exta[:, 1, :], qsc[:, :], qinv[:, :], qtop[:, :], qtmp[:, :])
                    link(nc.vector.reduce_max(ownr[:, :], own[:, :, :], AXX))
                    link(nc.vector.tensor_scalar(qinvm[:, :], ownr[:, :], qinv[:, 0:1], None, ALU.mult))
                    nc.vector.scalar_tensor_tensor(esc[:, :], qsc[:, 0:1], D ** -0.5, qsc[:, 1:2], ALU.mult, ALU.mult).then_inc(s_qsc, 1)

                    def reduce(n, c0, c1):
                        for c in range(c0, c1):
                            g, qt, h2 = c // 4, (c // 2) % 2, c % 2
                            dve.wait_ge(s_S, n * 16 + c + 1)
                            nc.vector.tensor_reduce(nm[:, qt, 4 * g + 2 * h2:4 * g + 2 * h2 + 2], pS[c % 2][:, :, :], AXX, ALU.max,
                                                    negate=True).then_inc(s_red, 1)

                    def parts(n):
                        dve.wait_ge(s_red, n * 16 + 16)
                        if not (isinstance(n, int) and n == 0):
                            dve.wait_ge(s_z, n)
                        src = nm[:, :, :].rearrange("p q (m s j) -> p (q m) s j", s=2, j=J)
                        rst = rem[:, :, :].rearrange("p q (m s j) -> p (q m) s j", s=2, j=J)
                        to = [Tm[:, :, gm::2, :].rearrange("p q m (j e) -> p (q m) j e", e=32)[:, :, :, D * (1 - gm):D * (1 - gm) + 3]
                              for gm in range(2)]
                        for gm in range(2):
                            nc.vector.tensor_copy(to[gm][:, :, :, 0], src[:, :, gm, :]).then_inc(s_mc, 1)
                        for gm in range(2):
                            dve.wait_ge(s_mc, n * 6 + 1 + gm)
                            nc.vector.tensor_tensor(rst[:, :, gm, :], src[:, :, gm, :], to[gm][:, :, :, 0], ALU.subtract).then_inc(s_mc, 1)
                        for gm in range(2):
                            dve.wait_ge(s_mc, n * 6 + 3 + gm)
                            nc.vector.tensor_copy(to[gm][:, :, :, 1], rst[:, :, gm, :]).then_inc(s_mc, 1)
                        for gm in range(2):
                            dve.wait_ge(s_mc, n * 6 + 5 + gm)
                            nc.vector.tensor_tensor(to[gm][:, :, :, 2], rst[:, :, gm, :], to[gm][:, :, :, 1], ALU.subtract).then_inc(s_m, 1)

                    def addq(n, r):
                        dve.wait_ge(s_z, n + 1)
                        nc.vector.tensor_tensor(qT[:, :, :], zT[:, :, :], QK[r][:, :, 0, :], ALU.add).then_inc(s_qT, 1)

                    def norm(n, h, r, u):
                        dve.wait_ge(s_r, n * 2 + h + 2)
                        src = pM[:, :].rearrange("p (u e) -> p u e", e=32)
                        nc.vector.reciprocal(rden[h][:, :], src[:, :, D]).then_inc(s_nc, 1)
                        dve.wait_ge(s_nc, n * 4 + 2 * h + 1)
                        nc.vector.tensor_scalar(rden[h][:, :], rden[h][:, :], qsc[:, 2:3], None, ALU.mult).then_inc(s_nc, 1)
                        dve.wait_ge(s_nc, n * 4 + 2 * h + 2)
                        dve.wait_ge(s_ast[r], u * 16 + 16)
                        out_ = attn[r][:, :, P * h:P * h + P].rearrange("p t (u d) -> p t u d", d=D)
                        nc.vector.tensor_tensor(out_, src[:, :, 0:D].rearrange("p (t u) d -> p t u d", t=2),
                                                rden[h][:, :].rearrange("p (t u) -> p t u", t=2).unsqueeze(3).broadcast_to([P, 2, 8, D]),
                                                ALU.mult).then_inc(s_norm, 1)

                    def extremes(n, r):
                        dve.wait_ge(s_norm, n * 2 + 2)
                        o = attn[r][:, :, :].rearrange("p a b -> p (a b)")
                        nc.vector.tensor_reduce(omx[:, bass.ds(n, 1)], o, AXX, ALU.max)
                        nc.vector.tensor_reduce(omn[:, bass.ds(n, 1)], o, AXX, ALU.min)

                    def image(n, r, u, first=False, final=False):
                        more = (lambda a, b: None) if final else (lambda a, b: reduce(n + 1, a, b))
                        more(0, 9)
                        if not first:
                            norm(n - 1, 1, (r + 2) % 3, u + (r + 2) // 3 - 1)
                            extremes(n - 1, (r + 2) % 3)
                        more(9, 16)
                        if not final:
                            parts(n + 1)
                        norm(n, 0, r, u)
                        if not final:
                            addq(n + 1, (r + 1) % 3)
                    dve.wait_ge(s_init, 1)
                    reduce(0, 0, 16)
                    parts(0)
                    addq(0, 0)
                    image(0, 0, 0, first=True)
                    with dve.Fori(0, 10) as i:
                        for k in range(3):
                            image(i * 3 + 1 + k, (1 + k) % 3, i + (1 + k) // 3)
                    image(31, 1, 10, final=True)
                    norm(31, 1, 1, 10)
                    extremes(31, 1)
                    linked(link)

        with ExitStack() as ff:
            def sb(name, shape, dt=F32):
                return ff.enter_context(nc.sbuf_tensor(name, shape, dt))

            def ps(name, shape, dt=F32):
                return ff.enter_context(nc.psum_tensor(name, shape, dt))
            ghi, glo, uhi, ulo = (sb(n, [P, KC, NE, I], F32R) for n in ("gate_hi", "gate_lo", "up_hi", "up_lo"))
            dw = sb("down", [P, NE, C])
            rhi, rlo = (sb(n, [P, KC, E], F32R) for n in ("router_hi", "router_lo"))
            s_sl, s_hi2, s_lo2 = sem("ffn_staged"), sem("split_hi"), sem("split_lo")
            with ExitStack() as sg_:
                stage = [sg_.enter_context(nc.sbuf_tensor(f"stage{a}", [P, KC * NE * I], F32)) for a in range(2)]
                stager = sg_.enter_context(nc.sbuf_tensor("stage_router", [P, KC * E], F32))
                flat = lambda t: t[:, :, :, :].rearrange("p k e i -> p (k e i)")
                parts3 = ((stage[0][:, :], flat(ghi), flat(glo)), (stage[1][:, :], flat(uhi), flat(ulo)),
                          (stager[:, :], rhi[:, :, :].rearrange("p k e -> p (k e)"), rlo[:, :, :].rearrange("p k e -> p (k e)")))
                with nc.Block() as block:
                    @block.sync
                    def _(sp):
                        for t, w in zip(parts3, (gate_t, up_t, router_t)):
                            w = w.rearrange("p k e i -> p (k e i)") if w is not router_t else w.rearrange("p k e -> p (k e)")
                            sp.dma_start(t[0], w).then_inc(s_sl, 16)

                    @block.scalar
                    def _(act):
                        act.wait_ge(s_sl, 48)
                        for t, hi, lo in parts3:
                            nc.scalar.copy(hi, t).then_inc(s_hi2, 1)

                    @block.vector
                    def _(dve):
                        for n, (t, hi, lo) in enumerate(parts3):
                            dve.wait_ge(s_hi2, n + 1)
                            nc.vector.tensor_tensor(lo, t, hi.bitcast(F32), ALU.subtract).then_inc(s_lo2, 1)
            eb = sb("e_bias_all", [P, E])
            oext, oexta = sb("attn_ext", [P, 2]), sb("attn_ext_all", [P, 2])
            osc, oinv, otop, otmp = (sb(n, [P, 1]) for n in ("attn_scale", "attn_inv", "attn_top", "attn_tmp"))
            psc = sb("proj_scale_all", [P, KC])
            pick = sb("pick", [3 * E, E, P], BF16)
            lower4, lower16 = sb("lower4", [P, 4, 4]), sb("lower16", [P, E, E])
            rest15 = sb("rest15", [P, E])
            ac = [sb(f"attn_chunk{a}", [P, NT, C]) for a in range(2)]
            hc = [sb(f"edge_chunk{a}", [P, KC, CH]) for a in range(2)]
            oq = sb("attn_int", [P, NT, C], BF16)
            oqT = sb("attn_int_T", [P, KC, CH], BF16)
            x1T = sb("x1_T", [P, KC, CH])
            h1 = [sb(f"h1_{a}", [P, NT, C]) for a in range(2)]
            xh = [sb(f"h1T_hi{a}", [P, KC, CH], F32R) for a in range(2)]
            xl = [sb(f"h1T_lo{a}", [P, KC, CH], F32R) for a in range(2)]
            st6, mv, rs = sb("ln_stats", [P, NT, 6]), sb("ln_mv", [P, NT, 2]), sb("ln_rstd", [P, NT])
            st6b, mvb, rsb = sb("ln2_stats", [P, NT, 6]), sb("ln2_mv", [P, NT, 2]), sb("ln2_rstd", [P, NT])
            sg, scb, msk = (sb(n, [P, NT, E]) for n in ("scores", "scores_biased", "scores_masked"))
            pmx, pmn = sb("pair_max", [P, 16, 2]), sb("pair_min", [P, 16, 2])
            g1, g2, g3, gsum, grank, gsel = (sb(n, [P, NT * 4]) for n in ("g1", "g2", "g3", "gsum", "grank", "gsel"))
            cmp4, cmp4b = sb("cmp4", [P, NT, 4, 4]), sb("cmp4b", [P, NT, 4, 4])
            cmp16 = sb("cmp16", [P, NT, E, E])
            rrow, rcol, comb = (sb(n, [P, NT, E]) for n in ("rank_row", "rank_col", "combine"))
            wsum = sb("weight_sum", [P, NT])
            mhalf = sb("minus_half", [P, NT])
            cpart = sb("combine_parts", [P, NT, 3, E], BF16)
            crest = sb("combine_rest", [P, NT, E])
            cT = [sb(f"combine_T{a}", [3 * E, CH], BF16) for a in range(2)]
            sl = [sb(f"silu{a}", [P, CH]) for a in range(2)]
            sc_ = [sb(f"silu_combined{a}", [P, CH]) for a in range(2)]
            prod = [sb(f"prod{a}", [P, CH]) for a in range(2)]
            ys = sb("y", [P, NT, C])
            yo = sb("y_out", [P, NT, C])
            pG = [ps(f"pG{a}", [P, CH]) for a in range(2)]
            pU = [ps(f"pU{a}", [P, CH]) for a in range(2)]
            pC = ps("pC", [P, CH])
            pA = [ps(f"pA{a}", [P, 2, C]) for a in range(2)]
            pX = ps("pX", [P, CH])
            pXb = pX[:, :].bitcast(BF16)

            s_wl2, s_ext2, s_all2, s_osc, s_cst = (sem(n) for n in (
                "ffn_loaded", "attn_ext_ready", "attn_ext_reduced", "attn_scales", "ffn_consts"))
            s_cl = [sem(f"chunk_loaded{a}") for a in range(2)]
            (s_oy, s_oq, s_oT, s_oTs, s_pj, s_pja, s_x1, s_xn, s_mv, s_rs, s_h1, s_hT, s_spl) = (sem(n) for n in (
                "attn_rounded", "attn_int_ready", "attn_T_done", "attn_T_ready", "proj_done", "proj_scaled", "x1_ready",
                "x1_transposed", "ln_mv_ready", "ln_rstd_ready", "h1_ready", "h1_transposed", "h1T_split"))
            (s_rt, s_sig, s_cb, s_cT, s_cTs, s_route) = (sem(n) for n in (
                "router_done", "scores_ready", "combine_ready", "combine_T_done", "combine_T_ready", "route_chain"))
            (s_G, s_U, s_C, s_silu, s_t1, s_prod, s_dn, s_y2, s_mv2, s_rs2, s_yo, s_out, s_bn, s_bn2) = (sem(n) for n in (
                "gate_done", "up_done", "spread_done", "silu_ready", "silu_combined", "prod_ready", "down_done", "y_ready",
                "ln2_mv_ready", "ln2_rstd_ready", "out_ready", "out_stored", "ln_chain", "ln2_chain"))
            s_pw, s_pw2 = sem("power_chain"), sem("power2_chain")

            with nc.Block() as block:
                @block.sync
                def _(sp):
                    sp.dma_start(dw[:, :, :], down_t).then_inc(s_wl2, 16)
                    sp.dma_start(eb[:, :], e_bias.rearrange("(o n) -> o n", o=1).broadcast_to([P, E])).then_inc(s_wl2, 16)

                    def load(n, a):
                        sp.dma_start(ac[a][:, :, :], at_s[:, bass.ds(n * NT, NT), :]).then_inc(s_cl[a], 16)
                        sp.dma_start(hc[a][:, :, :], hs[:, :, bass.ds(n * CH, CH)]).then_inc(s_cl[a], 16)

                    load(0, 0)
                    load(1, 1)

                    def reload(n, a):
                        sp.wait_ge(s_x1, n * 2 - 2)
                        load(n, a)

                    def store(n):
                        sp.wait_ge(s_yo, n * NT + NT)
                        sp.dma_start(out.rearrange("b (t p) c -> p (b t) c", p=P)[:, bass.ds(n * NT, NT), :], yo[:, :, :]).then_inc(s_out, 16)
                    reload(2, 0)
                    reload(3, 1)
                    with sp.Fori(0, 6) as i:
                        for a in range(2):
                            store(i * 2 + a)
                            reload(i * 2 + 4 + a, a)
                    for n in range(12, NCH):
                        store(n)
                    sp.wait_ge(s_out, 16 * NCH + 16)

                @block.gpsimd
                def _(pool):
                    nc.gpsimd.memset(pick[:, :, :], 0.0).then_inc(s_cst, 1)
                    nc.gpsimd.memset(lower4[:, :, :], 1.0).then_inc(s_cst, 1)
                    nc.gpsimd.memset(lower16[:, :, :], 1.0).then_inc(s_cst, 1)
                    nc.gpsimd.iota(rest15[:, :], pattern=[[-1, E]], base=15, channel_multiplier=0,
                                   allow_small_or_imprecise_dtypes=True).then_inc(s_cst, 1)
                    nc.gpsimd.memset(mhalf[:, :], -0.5).then_inc(s_cst, 1)
                    pool.wait_ge(s_cst, 5)
                    for t, w in ((lower4, 4), (lower16, E)):
                        nc.gpsimd.affine_select(out=t[:, :, :], in_=t[:, :, :], compare_op=ALU.is_ge, fill=0.0, base=-1,
                                                pattern=[[1, w], [-1, w]], channel_multiplier=0).then_inc(s_cst, 1)
                    for k in range(3):
                        nc.gpsimd.affine_select(out=pick[:, :, :], in_=pick[:, :, :], compare_op=ALU.not_equal, fill=1.0, base=-E * k,
                                                pattern=[[-1, E], [0, P]], channel_multiplier=1).then_inc(s_cst, 1)
                        pool.wait_ge(s_cst, 8 + k)
                    pool.wait_ge(s_ext2, 2)
                    nc.gpsimd.partition_all_reduce(oexta[:, :], oext[:, :], P, RMAX).then_inc(s_all2, 1)
                    pool.wait_ge(s_osc, 1)

                    def quant(n, a, u):
                        wait_apart(pool, s_cl[a], u * 32 + 32, s_tick)
                        nc.gpsimd.tensor_scalar(ac[a][:, :, :], ac[a][:, :, :], oinv[:, 0:1], MAGIC, ALU.mult, ALU.add).then_inc(s_oy, 1)
                        wait_apart(pool, s_oy, n + 1, s_tick)
                        wait_apart(pool, s_oT, n, s_tick)
                        nc.gpsimd.tensor_scalar(oq[:, :, :], ac[a][:, :, :], otop[:, 0:1], MAGIC, ALU.min, ALU.subtract).then_inc(s_oq, 1)

                    def residual(n, a):
                        for k in range(KC):
                            pool.wait_ge(s_pja, n * 2 + k + 1)
                            nc.gpsimd.tensor_tensor(x1T[:, k, :], x1T[:, k, :], hc[a][:, k, :], ALU.add).then_inc(s_x1, 1)

                    def power(o, var, n, s_, chain):
                        nc.gpsimd.tensor_scalar(o, var, LN_EPS, None, ALU.add).then_inc(chain, 1)
                        pool.wait_ge(chain, n + 1)
                        nc.gpsimd.tensor_tensor(o, o, mhalf[:, 0:o.shape[1]], ALU.pow).then_inc(s_, 1)

                    def rstd(n):
                        for h in range(2):
                            wait_apart(pool, s_mv, n * NT + 2 * h + 2, s_tick)
                            power(rs[:, 2 * h:2 * h + 2], mv[:, 2 * h:2 * h + 2, 1], n * 2 + h, s_rs, s_pw)

                    def rstd2(n):
                        wait_apart(pool, s_mv2, n * NT + NT, s_tick)
                        power(rsb[:, :], mvb[:, :, 1], n, s_rs2, s_pw2)

                    quant(0, 0, 0)
                    residual(0, 0)
                    rstd(0)
                    quant(1, 1, 0)

                    def chunk(n, a, u, first=False, quants=True):
                        if not first:
                            rstd2(n - 1)
                        residual(n + 1, 1 - a)
                        rstd(n + 1)
                        if quants:
                            quant(n + 2, a, u + 1)
                    chunk(0, 0, 0, first=True)
                    with pool.Fori(0, 6) as i:
                        chunk(i * 2 + 1, 1, i)
                        chunk(i * 2 + 2, 0, i + 1)
                    chunk(13, 1, 6)
                    chunk(14, 0, 7, quants=False)
                    rstd2(14)
                    rstd2(15)

                @block.scalar
                def _(act):
                    def evacT(n):
                        act.wait_ge(s_oT, n + 1)
                        act.wait_ge(s_pj, n * 2)
                        nc.scalar.copy(oqT[:, :, :], pXb.rearrange("p (k t) -> p k t", k=KC)).then_inc(s_oTs, 1)

                    def scale(n, k):
                        act.wait_ge(s_pj, n * 2 + k + 1)
                        act.wait_ge(s_xn, n * 2)
                        nc.scalar.activation(x1T[:, k, :], pX[:, :], ACT.Identity, bias=pb[:, k:k + 1], scale=psc[:, k:k + 1]).then_inc(s_pja, 1)

                    def score(n):
                        act.wait_ge(s_rt, n + 1)
                        act.wait_ge(s_cb, n * 3)
                        nc.scalar.activation(sg[:, :, :], pX[:, 0:NT * E].rearrange("p (t e) -> p t e", e=E), ACT.Sigmoid).then_inc(s_sig, 1)

                    act.wait_ge(s_osc, 1)
                    evacT(0)
                    scale(0, 0)
                    scale(0, 1)
                    score(0)

                    def chunk(n, final=False):
                        for e in range(NE):
                            act.wait_ge(s_G, n * NE + e + 1)
                            if not (isinstance(n, int) and n == 0 and e < 2):
                                act.wait_ge(s_prod, n * NE + e - 1)
                            nc.scalar.activation(sl[e % 2][:, :], pG[e % 2][:, :], ACT.Silu).then_inc(s_silu, 1)
                            if not final:
                                if e == 2:
                                    evacT(n + 1)
                                if e == 4:
                                    scale(n + 1, 0)
                                if e == 5:
                                    scale(n + 1, 1)
                                if e == 13:
                                    score(n + 1)
                    chunk(0)
                    with act.Fori(0, NCH - 2) as i:
                        chunk(i + 1)
                    chunk(NCH - 1, final=True)

                @block.tensor
                def _(pe):
                    def oT(n):
                        pe.wait_ge(s_oq, n + 1)
                        pe.wait_ge(s_cTs, n)
                        for k in range(KC):
                            for t in range(NT):
                                last = nc.tensor.transpose(pXb[:, k * CH + t * P:k * CH + t * P + P], oq[:, t, k * P:k * P + P], identb[:, :])
                        last.then_inc(s_oT, 1)

                    def proj(n, m):
                        pe.wait_ge(s_oTs, n + 1)
                        pe.wait_ge(s_pja, n * 2 + m)
                        for k in range(KC):
                            last = nc.tensor.matmul(pX[:, :], pint[:, k, m * P:m * P + P], oqT[:, k, :], start=(k == 0), stop=(k == 1))
                        last.then_inc(s_pj, 1)

                    def xn(n, h):
                        pe.wait_ge(s_x1, n * 2 + 2)
                        pe.wait_ge(s_h1, n * NT + 2 * h)
                        for t in range(2):
                            for k in range(KC):
                                c = t * C + k * P
                                tt = (2 * h + t) * P
                                last = nc.tensor.transpose(pX[:, c:c + P], x1T[:, k, tt:tt + P], ident[:, :])
                        last.then_inc(s_xn, 1)

                    def hT_(n, a, k):
                        pe.wait_ge(s_h1, n * NT + NT)
                        pe.wait_ge(s_spl, n * 4 + 2 * k)
                        for t in range(NT):
                            last = nc.tensor.transpose(pX[:, t * P:t * P + P], h1[a][:, t, k * P:k * P + P], ident[:, :])
                        last.then_inc(s_hT, 1)

                    def route(n, a):
                        pe.wait_ge(s_spl, n * 4 + 4)
                        for t in range(NT):
                            m = 0
                            for k in range(KC):
                                for x_, w_ in ((xh, rhi), (xh, rlo), (xl, rhi)):
                                    last = nc.tensor.matmul(pX[:, t * E:t * E + E], x_[a][:, k, t * P:t * P + P], w_[:, k, :],
                                                            start=(m == 0), stop=(m == 5))
                                    m += 1
                        last.then_inc(s_rt, 1)

                    def combT(n):
                        wait_apart(pe, s_cb, n * 3 + 3, s_tick)
                        for t in range(NT):
                            last = nc.tensor.transpose(pXb[0:3 * E, t * P:t * P + P], cpart[:, t, :, :].rearrange("p a e -> p (a e)"), identb[:, :])
                        last.then_inc(s_cT, 1)

                    def down(n, e):
                        q = n * NE + e
                        pe.wait_ge(s_prod, q + 1)
                        if e == 0:
                            pe.wait_ge(s_y2, n * 2)
                        for t in range(NT):
                            last = nc.tensor.matmul(pA[t // 2][:, t % 2, :], prod[e % 2][:, t * P:t * P + P], dw[:, e, :],
                                                    start=(e == 0 and t % 2 == 0), stop=(e == NE - 1), skip_group_check=True)
                        last.then_inc(s_dn, 1)

                    def chunk(n, a, first=False, final=False):
                        for e in range(NE):
                            q = n * NE + e
                            if e == 0:
                                pe.wait_ge(s_cTs, n + 1)
                            if not (first and e < 2):
                                pe.wait_ge(s_silu, q - 1)
                                pe.wait_ge(s_prod, q - 1)
                            for w, po, s_ in (((ghi, glo), pG, s_G), ((uhi, ulo), pU, s_U)):
                                m = 0
                                for k in range(KC):
                                    for x_, w_ in ((xh, w[0]), (xl, w[0]), (xh, w[1])):
                                        last = nc.tensor.matmul(po[e % 2][:, :], w_[:, k, e, :], x_[a][:, k, :], start=(m == 0), stop=(m == 5))
                                        m += 1
                                last.then_inc(s_, 1)
                            if e < E:
                                pe.wait_ge(s_t1, n * E + e)
                                nc.tensor.matmul(pC[:, :], pick[:, e, :], cT[a][:, :], start=True, stop=True).then_inc(s_C, 1)
                            if e > 0:
                                down(n, e - 1)
                            elif not first:
                                down(n - 1, NE - 1)
                            if not final:
                                if e == 1:
                                    oT(n + 1)
                                if e == 3:
                                    proj(n + 1, 0)
                                if e == 4:
                                    proj(n + 1, 1)
                                if e == 6:
                                    xn(n + 1, 0)
                                if e == 8:
                                    xn(n + 1, 1)
                                if e == 10:
                                    hT_(n + 1, 1 - a, 0)
                                if e == 11:
                                    hT_(n + 1, 1 - a, 1)
                                if e == 12:
                                    route(n + 1, 1 - a)
                                if e == 17:
                                    combT(n + 1)
                    oT(0)
                    proj(0, 0)
                    proj(0, 1)
                    xn(0, 0)
                    xn(0, 1)
                    hT_(0, 0, 0)
                    hT_(0, 0, 1)
                    route(0, 0)
                    combT(0)
                    pe.wait_ge(s_cst, 10)
                    pe.wait_ge(s_wl2, 16 * 2)
                    chunk(0, 0, first=True)
                    with pe.Fori(0, NCH // 2 - 1) as i:
                        chunk(i * 2 + 1, 1)
                        chunk(i * 2 + 2, 0)
                    chunk(NCH - 1, 1, final=True)
                    down(NCH - 1, NE - 1)

                @block.vector
                def _(dve):
                    link = linker(dve)
                    link(nc.vector.reduce_max(oext[:, 0:1], omx[:, :], AXX))
                    nc.vector.tensor_reduce(oext[:, 1:2], omn[:, :], AXX, ALU.min, negate=True).then_inc(s_ext2, 2)
                    dve.wait_ge(s_all2, 1)
                    link(nc.vector.tensor_scalar(oexta[:, 1:2], oexta[:, 1:2], -1.0, None, ALU.mult))
                    quant_scalars(dve, link, oexta[:, 0:1], oexta[:, 1:2], osc[:, :], oinv[:, :], otop[:, :], otmp[:, :])
                    nc.vector.tensor_scalar(psc[:, :], pscale[:, :], osc[:, 0:1], None, ALU.mult).then_inc(s_osc, 1)

                    def ln(n, a, h):
                        dve.wait_ge(s_xn, n * 2 + h + 1)
                        for t in range(2):
                            nc.vector.bn_stats(st6[:, 2 * h + t, :], pX[:, t * C:t * C + C]).then_inc(s_bn, 1)
                        for t in range(2):
                            wait_apart(dve, s_bn, n * NT + 2 * h + t + 1, s_tick)
                            nc.vector.bn_aggr(mv[:, 2 * h + t, :], st6[:, 2 * h + t, :]).then_inc(s_mv, 1)
                        dve.wait_ge(s_rs, n * 2 + h + 1)
                        for t in range(2):
                            q = 2 * h + t
                            nc.vector.tensor_scalar(h1[a][:, q, :], pX[:, t * C:t * C + C], mv[:, q, 0:1], rs[:, q:q + 1],
                                                    ALU.subtract, ALU.mult).then_inc(s_h1, 1)

                    def split(n, a, k):
                        dve.wait_ge(s_hT, n * 2 + k + 1)
                        nc.vector.tensor_copy(xh[a][:, k, :], pX[:, :]).then_inc(s_spl, 1)
                        dve.wait_ge(s_spl, n * 4 + 2 * k + 1)
                        nc.vector.tensor_tensor(xl[a][:, k, :], pX[:, :], xh[a][:, k, :].bitcast(F32), ALU.subtract).then_inc(s_spl, 1)

                    def top_groups(n, c):
                        dve.wait_ge(s_sig, n + 1)
                        c(nc.vector.tensor_tensor(scb[:, :, :], sg[:, :, :], eb[:, :].unsqueeze(1).broadcast_to([P, NT, E]), ALU.add))
                        v = scb[:, :, :].rearrange("p t (g a b) -> p (t g) a b", a=2, b=2)
                        c(nc.vector.tensor_tensor(pmx[:, :, :], v[:, :, :, 0], v[:, :, :, 1], ALU.max))
                        c(nc.vector.tensor_tensor(pmn[:, :, :], v[:, :, :, 0], v[:, :, :, 1], ALU.min))
                        c(nc.vector.tensor_tensor(g1[:, :], pmx[:, :, 0], pmx[:, :, 1], ALU.max))
                        c(nc.vector.tensor_tensor(g2[:, :], pmx[:, :, 0], pmx[:, :, 1], ALU.min))
                        c(nc.vector.tensor_tensor(g3[:, :], pmn[:, :, 0], pmn[:, :, 1], ALU.max))
                        c(nc.vector.tensor_tensor(g2[:, :], g2[:, :], g3[:, :], ALU.max))
                        c(nc.vector.tensor_tensor(gsum[:, :], g1[:, :], g2[:, :], ALU.add))
                        gs = gsum[:, :].rearrange("p (t g) -> p t g", g=4)
                        mine, other = gs.unsqueeze(3).broadcast_to([P, NT, 4, 4]), gs.unsqueeze(2).broadcast_to([P, NT, 4, 4])
                        c(nc.vector.tensor_tensor(cmp4[:, :, :, :], other, mine, ALU.is_gt))
                        c(nc.vector.tensor_tensor(cmp4b[:, :, :, :], other, mine, ALU.is_equal))
                        c(nc.vector.tensor_tensor(cmp4b[:, :, :, :], cmp4b[:, :, :, :], lower4[:, :, :].unsqueeze(1).broadcast_to([P, NT, 4, 4]), ALU.mult))
                        c(nc.vector.tensor_tensor(cmp4[:, :, :, :], cmp4[:, :, :, :], cmp4b[:, :, :, :], ALU.add))
                        c(nc.vector.tensor_reduce(grank[:, :], cmp4[:, :, :, :].rearrange("p t g o -> p (t g) o"), AXX, ALU.add))
                        c(nc.vector.tensor_scalar(gsel[:, :], grank[:, :], 2.0, None, ALU.is_lt))
                        c(nc.vector.tensor_tensor(msk[:, :, :].rearrange("p t (g e) -> p (t g) e", e=4), scb[:, :, :].rearrange("p t (g e) -> p (t g) e", e=4),
                                                  gsel[:, :].unsqueeze(2).broadcast_to([P, 16, 4]), ALU.mult))

                    def top_experts(n, c):
                        mine, other = msk[:, :, :].unsqueeze(3).broadcast_to([P, NT, E, E]), msk[:, :, :].unsqueeze(2).broadcast_to([P, NT, E, E])
                        c(nc.vector.tensor_tensor(cmp16[:, :, :, :], other, mine, ALU.is_ge))
                        c(nc.vector.tensor_tensor(cmp16[:, :, :, :], cmp16[:, :, :, :], lower16[:, :, :].unsqueeze(1).broadcast_to([P, NT, E, E]), ALU.mult))
                        c(nc.vector.tensor_reduce(rrow[:, :, :], cmp16[:, :, :, :], AXX, ALU.add))
                        c(nc.vector.tensor_reduce(rcol[:, :, :], cmp16[:, :, :, :].rearrange("p t e o -> p t o e"), AXX, ALU.add))

                    def weights(n, c):
                        c(nc.vector.tensor_tensor(rrow[:, :, :], rrow[:, :, :], rcol[:, :, :], ALU.subtract))
                        c(nc.vector.tensor_tensor(rrow[:, :, :], rrow[:, :, :], rest15[:, :].unsqueeze(1).broadcast_to([P, NT, E]), ALU.add))
                        c(nc.vector.scalar_tensor_tensor(comb[:, :, :], rrow[:, :, :], 4.0, sg[:, :, :], ALU.is_lt, ALU.mult))
                        c(nc.vector.tensor_reduce(wsum[:, :], comb[:, :, :], AXX, ALU.add))
                        c(nc.vector.tensor_scalar(wsum[:, :], wsum[:, :], 1e-20, None, ALU.add))
                        c(nc.vector.reciprocal(wsum[:, :], wsum[:, :]))
                        c(nc.vector.tensor_scalar(wsum[:, :], wsum[:, :], 2.5, None, ALU.mult))
                        c(nc.vector.tensor_tensor(comb[:, :, :], comb[:, :, :], wsum[:, :].unsqueeze(2).broadcast_to([P, NT, E]), ALU.mult))
                        dve.wait_ge(s_cT, n)
                        nc.vector.tensor_copy(cpart[:, :, 0, :], comb[:, :, :]).then_inc(s_cb, 1)
                        dve.wait_ge(s_cb, n * 3 + 1)
                        c(nc.vector.tensor_tensor(crest[:, :, :], comb[:, :, :], cpart[:, :, 0, :], ALU.subtract))
                        nc.vector.tensor_copy(cpart[:, :, 1, :], crest[:, :, :]).then_inc(s_cb, 1)
                        dve.wait_ge(s_cb, n * 3 + 2)
                        nc.vector.tensor_tensor(cpart[:, :, 2, :], crest[:, :, :], cpart[:, :, 1, :], ALU.subtract).then_inc(s_cb, 1)

                    def combT(n, a):
                        dve.wait_ge(s_cT, n + 1)
                        nc.vector.tensor_copy(cT[a][:, :], pXb[0:3 * E, 0:CH]).then_inc(s_cTs, 1)

                    def chain(n):
                        return Chain(dve, s_route, n, 28)

                    def finish(n, a):
                        dve.wait_ge(s_dn, n * NE + NE)
                        for h in range(2):
                            nc.vector.tensor_tensor(ys[:, 2 * h:2 * h + 2, :], pA[h][:, :, :], h1[a][:, 2 * h:2 * h + 2, :], ALU.add).then_inc(s_y2, 1)

                    def finish_stats(n):
                        for t in range(NT):
                            dve.wait_ge(s_y2, n * 2 + t // 2 + 1)
                            nc.vector.bn_stats(st6b[:, t, :], ys[:, t, :]).then_inc(s_bn2, 1)
                        for t in range(NT):
                            wait_apart(dve, s_bn2, n * NT + t + 1, s_tick)
                            nc.vector.bn_aggr(mvb[:, t, :], st6b[:, t, :]).then_inc(s_mv2, 1)

                    def finish_out(n):
                        dve.wait_ge(s_rs2, n + 1)
                        dve.wait_ge(s_out, n * 16 + 16)
                        for t in range(NT):
                            nc.vector.tensor_scalar(yo[:, t, :], ys[:, t, :], mvb[:, t, 0:1], rsb[:, t:t + 1],
                                                    ALU.subtract, ALU.mult).then_inc(s_yo, 1)

                    nc.vector.memset(yo[:], 0.0).then_inc(s_out, 16)
                    ln(0, 0, 0)
                    ln(0, 0, 1)
                    split(0, 0, 0)
                    split(0, 0, 1)
                    dve.wait_ge(s_cst, 10)
                    dve.wait_ge(s_wl2, 16 * 2)
                    c = chain(0)
                    top_groups(0, c)
                    top_experts(0, c)
                    weights(0, c)
                    c.close()
                    combT(0, 0)

                    def chunk(n, a, first=False, final=False):
                        c = chain(n + 1)
                        for e in range(NE):
                            q = n * NE + e
                            dve.wait_ge(s_silu, q + 1)
                            src = sl[e % 2]
                            if e < E:
                                dve.wait_ge(s_C, n * E + e + 1)
                                nc.vector.tensor_tensor(sc_[e % 2][:, :], sl[e % 2][:, :], pC[:, :], ALU.mult).then_inc(s_t1, 1)
                                dve.wait_ge(s_t1, n * E + e + 1)
                                src = sc_[e % 2]
                            dve.wait_ge(s_U, q + 1)
                            if not (first and e < 2):
                                dve.wait_ge(s_dn, q - 1)
                            nc.vector.tensor_tensor(prod[e % 2][:, :], src[:, :], pU[e % 2][:, :], ALU.mult).then_inc(s_prod, 1)
                            if not first:
                                if e == 0:
                                    finish(n - 1, 1 - a)
                                if e == 1:
                                    finish_stats(n - 1)
                                if e == 2:
                                    finish_out(n - 1)
                            if not final:
                                if e == 6:
                                    ln(n + 1, 1 - a, 0)
                                if e == 8:
                                    ln(n + 1, 1 - a, 1)
                                if e == 10:
                                    split(n + 1, 1 - a, 0)
                                if e == 11:
                                    split(n + 1, 1 - a, 1)
                                if e == 13:
                                    top_groups(n + 1, c)
                                if e == 14:
                                    top_experts(n + 1, c)
                                if e == 15:
                                    weights(n + 1, c)
                                    c.close()
                                if e == 17:
                                    combT(n + 1, 1 - a)
                    chunk(0, 0, first=True)
                    with dve.Fori(0, NCH // 2 - 1) as i:
                        chunk(i * 2 + 1, 1)
                        chunk(i * 2 + 2, 0)
                    chunk(NCH - 1, 1, final=True)
                    finish(NCH - 1, 1)
                    finish_stats(NCH - 1)
                    finish_out(NCH - 1)
                    linked(link)


def kernel(**inputs):
    import numpy as np
    import concourse.bacc as bacc
    from concourse.bass_utils import run_bass_kernel_spmd

    a = {k: np.asarray(v) for k, v in inputs.items()}
    gate, up, down = a["L0_ffn_gate_w"], a["L0_ffn_up_w"], a["L0_ffn_down_w"]
    gate = np.concatenate([gate, a["L0_ffn_sh_gate_w"].reshape(2, I, C)])
    up = np.concatenate([up, a["L0_ffn_sh_up_w"].reshape(2, I, C)])
    down = np.concatenate([down, a["L0_ffn_sh_down_w"].reshape(C, 2, I).transpose(1, 0, 2)])
    by_c = lambda w: np.ascontiguousarray(w.reshape(NE, I, KC, P).transpose(3, 2, 0, 1))
    arrays = {
        "x": np.ascontiguousarray(a["x"].reshape(B, 3, 2, P, C).transpose(0, 3, 1, 2, 4)),
        "scharr": a["L0_tok_scharr"],
        "qkv_w": a["L0_attn_qkv_w"], "qkv_b": a["L0_attn_qkv_b"],
        "qkv_b_col": np.ascontiguousarray(a["L0_attn_qkv_b"].reshape(6, P).T),
        "proj_w": a["L0_attn_proj_w"],
        "proj_b_col": np.ascontiguousarray(a["L0_attn_proj_b"].reshape(KC, P).T),
        "router_t": np.ascontiguousarray(a["L0_ffn_router_weight"].reshape(E, KC, P).transpose(2, 1, 0)),
        "e_bias": a["L0_ffn_e_bias"],
        "gate_t": by_c(gate), "up_t": by_c(up),
        "down_t": np.ascontiguousarray(down.transpose(2, 0, 1)),
    }
    nc = bacc.Bacc("TRN2", target_bir_lowering=False, num_devices=1)
    args = [nc.dram_tensor(n, v.shape, mybir.dt.from_np(v.dtype), kind="ExternalInput").ap() for n, v in arrays.items()]
    args.append(nc.dram_tensor("out", (B, 256, 256), F32, kind="ExternalOutput").ap())
    build(nc, *args)
    r = run_bass_kernel_spmd(nc, [arrays], core_ids=[0])
    return r.results[0]["out"]
```

```python
import concourse.bass as bass
from concourse import mybir
from contextlib import ExitStack

F32 = mybir.dt.float32
F32R = mybir.dt.float32r
BF16 = mybir.dt.bfloat16
ALU = mybir.AluOpType
ACT = mybir.ActivationFunctionType
AXX = mybir.AxisListType.X
RMAX = bass.bass_isa.ReduceOp.max

P = 128
B = 32
N = 256
C = 256
KC = C // P
T = B * N
H, D = 16, 16
G, J = 4, 4
E, I = 16, 128
NE = E + 2
CH = 512
NCH = T // CH
NT = CH // P
QMAX = 255.0
MAGIC = 12582912.0
GRAY = (0.2989 * 0.5, 0.587 * 0.5, 0.114 * 0.5)
LN_EPS = 1e-5
BW = 131


class Chain:

    def __init__(self, eng, sem, i=0, per=0, base=0):
        self.eng, self.sem, self.start, self.n, self.per = eng, sem, i * per + base, 0, per

    def __call__(self, ins):
        self.n += 1
        ins.then_inc(self.sem, 1)
        self.eng.wait_ge(self.sem, self.start + self.n)

    def close(self):
        assert self.n == self.per, (self.n, self.per)


def wait_apart(eng, sem, value, tick):
    eng.wait_ge(sem, value)
    eng.sem_inc(tick, 1)


def quant_scalars(dve, link, mx, mn, scale, inv, top, tmp):
    nc = dve.bass
    link(nc.vector.tensor_scalar(mx, mx, 0.0, None, ALU.max))
    link(nc.vector.tensor_scalar(mn, mn, 0.0, None, ALU.min))
    link(nc.vector.tensor_tensor(tmp, mx, mn, ALU.subtract))
    link(nc.vector.tensor_scalar(scale, tmp, 1.0 / QMAX, 1e-8, ALU.mult, ALU.max))
    link(nc.vector.reciprocal(inv, scale))
    link(nc.vector.tensor_tensor(tmp, mn, inv, ALU.mult))
    link(nc.vector.tensor_scalar(tmp, tmp, MAGIC, None, ALU.add))
    link(nc.vector.tensor_scalar(top, tmp, QMAX, None, ALU.add))


def build(nc, x, scharr, qkv_w, qkv_b, qkv_b_col, proj_w, proj_b_col, router_t, e_bias, gate_t, up_t, down_t, out):
    hs = nc.dram_tensor("edges_scratch", (P, KC, T), F32).ap()
    qk_s = nc.dram_tensor("qk_scratch", (4 * P, T), F32).ap()
    at_s = nc.dram_tensor("attn_scratch", (P, T // P, C), F32).ap()
    v_s = nc.dram_tensor("v_scratch", (T, C), F32).ap()

    with ExitStack() as whole:
        def sem(name):
            return whole.enter_context(nc.semaphore(name))

        def keep(name, shape, dt=F32):
            return whole.enter_context(nc.sbuf_tensor(name, shape, dt))

        link_sem = sem("dve_link")
        ident = keep("ident", [P, P])
        identb = keep("identb", [P, P], BF16)
        magic = keep("magic", [P, 1])
        pint = keep("proj_int_T", [P, KC, C], BF16)
        pscale = keep("proj_scale", [P, KC])
        pb = keep("proj_bias", [P, KC])
        omx = keep("attn_max", [P, B])
        omn = keep("attn_min", [P, B])
        mx = keep("qkv_max", [P, 3, NCH])
        mn = keep("qkv_min", [P, 3, NCH])
        s_tick = sem("waits_apart")
        links = [0]

        def linker(dve):
            c = Chain(dve, link_sem, base=links[0])
            return c

        def linked(c):
            links[0] += c.n

        with ExitStack() as ab:
            def sb(name, shape, dt=F32):
                return ab.enter_context(nc.sbuf_tensor(name, shape, dt))
            hT = sb("edges_T", [P, KC, T])
            cmax = sb("cmax", [P, KC, NCH])
            wdq = sb("wdq", [P, 6, C])
            qb = sb("qkv_bias", [P, 6])
            vb = sb("v_bias", [P, C])
            band = sb("band", [P, 3, 2, BW])

            with ExitStack() as st:
                def sb(name, shape, dt=F32):
                    return st.enter_context(nc.sbuf_tensor(name, shape, dt))
                taps = sb("taps", [P, 18])
                diag = sb("diag", [P, 3, BW])
                w_raw = sb("w_raw", [P, 8, C])
                w_y = sb("w_y", [P, 8, C])
                p_q = sb("p_q", [P, KC, C], BF16)
                wmx, wmn, wsc, winv, wtop, wtmp = (sb(n, [P, 8]) for n in ("wmx", "wmn", "wsc", "winv", "wtop", "wtmp"))
                pT = st.enter_context(nc.psum_tensor("pT", [P, KC, C], BF16))
                s_w, s_zero, s_diag, s_dq, s_pq, s_pt, s_gst = (sem(n) for n in (
                    "setup_loaded", "setup_zeroed", "diag_ready", "wdq_ready", "pq_ready", "pt_ready", "gate_setup"))
                s_ib = sem("identb_ready")
                with nc.Block() as block:
                    @block.sync
                    def _(sp):
                        sp.dma_start(w_raw[:, 0:6, :], qkv_w.rearrange("(t p) c -> p t c", p=P)).then_inc(s_w, 16)
                        sp.dma_start(w_raw[:, 6:8, :], proj_w.rearrange("(t p) c -> p t c", p=P)).then_inc(s_w, 16)
                        sp.dma_start(taps[:, :], scharr.rearrange("f o a b -> o (f a b)").broadcast_to([P, 18])).then_inc(s_w, 16)
                        sp.dma_start(qb[:, :], qkv_b_col).then_inc(s_w, 16)
                        sp.dma_start(pb[:, :], proj_b_col).then_inc(s_w, 16)
                        sp.dma_start(vb[:, :], qkv_b.rearrange("(o n) -> o n", o=1)[:, 2 * C:3 * C].broadcast_to([P, C])).then_inc(s_w, 16)
                        sp.wait_ge(s_w, 96)

                    @block.gpsimd
                    def _(pool):
                        nc.gpsimd.memset(diag[:], 0.0).then_inc(s_zero, 1)
                        nc.gpsimd.memset(ident[:], 0.0).then_inc(s_zero, 1)
                        pool.wait_ge(s_zero, 2)
                        for dy in range(3):
                            nc.gpsimd.affine_select(out=diag[:, dy, :], in_=diag[:, dy, :], compare_op=ALU.not_equal,
                                                    fill=1.0, base=2 - dy, pattern=[[-1, BW]],
                                                    channel_multiplier=1).then_inc(s_diag, 1)
                        nc.gpsimd.affine_select(out=ident[:, :], in_=ident[:, :], compare_op=ALU.not_equal,
                                                fill=1.0, base=0, pattern=[[-1, P]],
                                                channel_multiplier=1).then_inc(s_diag, 1)

                    @block.vector
                    def _(dve):
                        link = linker(dve)
                        link(nc.vector.memset(magic[:], MAGIC))
                        dve.wait_ge(s_diag, 4)
                        nc.vector.tensor_copy(identb[:, :], ident[:, :]).then_inc(s_ib, 1)
                        dve.wait_ge(s_w, 96)
                        for dx in range(3):
                            for f in range(2):
                                o = band[:, dx, f, :]
                                k = 9 * f + dx
                                link(nc.vector.tensor_scalar(o, diag[:, 0, :], taps[:, k:k + 1], None, ALU.mult))
                                link(nc.vector.scalar_tensor_tensor(o, diag[:, 1, :], taps[:, k + 3:k + 4], o, ALU.mult, ALU.add))
                                link(nc.vector.scalar_tensor_tensor(o, diag[:, 2, :], taps[:, k + 6:k + 7], o, ALU.mult, ALU.add))
                        link(nc.vector.tensor_reduce(wmx[:, :], w_raw[:, :, :], AXX, ALU.max))
                        link(nc.vector.tensor_reduce(wmn[:, :], w_raw[:, :, :], AXX, ALU.min))
                        quant_scalars(dve, link, wmx[:, :], wmn[:, :], wsc[:, :], winv[:, :], wtop[:, :], wtmp[:, :])
                        for t in range(8):
                            link(nc.vector.tensor_scalar(w_y[:, t, :], w_raw[:, t, :], winv[:, t:t + 1], MAGIC, ALU.mult, ALU.add))
                            link(nc.vector.tensor_scalar(w_y[:, t, :], w_y[:, t, :], wtop[:, t:t + 1], MAGIC, ALU.min, ALU.subtract))
                            if t < 6:
                                link(nc.vector.tensor_scalar(wdq[:, t, :], w_y[:, t, :], wsc[:, t:t + 1], None, ALU.mult))
                        link(nc.vector.tensor_copy(pscale[:, :], wsc[:, 6:8]))
                        for t in range(KC):
                            for k in range(KC):
                                o = p_q[:, t, k * P:(k + 1) * P].rearrange("p (g j d) -> p j g d", g=2, j=J)
                                i_ = w_y[:, 6 + t, k * P:(k + 1) * P].rearrange("p (j g d) -> p j g d", g=2, j=J)
                                nc.vector.tensor_copy(o, i_).then_inc(s_pq, 1)
                        dve.wait_ge(s_pt, 1)
                        link(nc.vector.tensor_copy(pint[:, :, :], pT[:, :, :]))
                        linked(link)

                    @block.tensor
                    def _(pe):
                        pe.wait_ge(s_ib, 1)
                        pe.wait_ge(s_pq, 4)
                        for k in range(KC):
                            for t in range(KC):
                                last = nc.tensor.transpose(pT[:, k, t * P:(t + 1) * P], p_q[:, t, k * P:(k + 1) * P], identb[:, :])
                        last.then_inc(s_pt, 1)

            with ExitStack() as st:
                def sb(name, shape, dt=F32):
                    return st.enter_context(nc.sbuf_tensor(name, shape, dt))
                xin = [sb(f"xin{a}", [P, 3, 2, C]) for a in range(2)]
                gt = [sb(f"gt{a}", [P, 2, C]) for a in range(2)]
                gray = [sb(f"gray{a}", [P, 2, C + 2]) for a in range(2)]
                gx = [sb(f"gx{a}", [P, 2, N]) for a in range(4)]
                pc = [st.enter_context(nc.psum_tensor(f"pc{a}", [P, 2, N], F32)) for a in range(4)]
                s_x = [sem(f"x_loaded{a}") for a in range(2)]
                s_gt = [sem(f"gray_red_ready{a}") for a in range(2)]
                s_gray = [sem(f"gray_ready{a}") for a in range(2)]
                s_conv = [sem(f"conv_done{a}") for a in range(4)]
                s_gx = [sem(f"gx_ready{a}") for a in range(4)]
                s_h = [sem(f"edges_ready{a}") for a in range(4)]
                s_g1 = sem("gray_half")
                s_spill = sem("edges_spilled")
                s_cm = sem("cmax_part")
                HALF = B // 2

                with nc.Block() as block:
                    @block.sync
                    def _(sp):
                        def load(b, i, a):
                            sp.wait_ge(s_gray[a], i)
                            sp.dma_start(xin[a][:, :, :, :], x[b]).then_inc(s_x[a], 16)

                        def spill(i):
                            for k in range(4):
                                sp.wait_ge(s_h[k], i + 1)
                            sp.dma_start(hs[:, :, bass.ds(i * CH, CH)], hT[:, :, bass.ds(i * CH, CH)]).then_inc(s_spill, 16)
                        load(0, 0, 0)
                        load(1, 0, 1)
                        def turn(i):
                            load(i * 2 + 2, i + 1, 0)
                            load(i * 2 + 3, i + 1, 1)
                            spill(i)

                        turn(0)
                        with sp.Fori(1, HALF - 1) as i:
                            turn(i)
                        spill(HALF - 1)
                        sp.wait_ge(s_spill, 16 * HALF)

                    @block.scalar
                    def _(act):
                        def red(i, a):
                            act.wait_ge(s_x[a], i * 16 + 16)
                            act.wait_ge(s_gray[a], i)
                            nc.scalar.activation(gt[a][:, :, :], xin[a][:, 0, :, :], ACT.Copy, scale=GRAY[0]).then_inc(s_gt[a], 1)

                        def absx(i, a):
                            for k in range(KC):
                                m = 2 * a + k
                                act.wait_ge(s_conv[m], i + 1)
                                act.wait_ge(s_h[m], i)
                                nc.scalar.activation(gx[m][:, :, :], pc[m][:, :, :], ACT.Abs).then_inc(s_gx[m], 1)
                        red(0, 0)
                        def turn(i):
                            red(i, 1)
                            absx(i, 0)
                            red(i + 1, 0)
                            absx(i, 1)

                        turn(0)
                        with act.Fori(1, HALF - 1) as i:
                            turn(i)
                        red(HALF - 1, 1)
                        absx(HALF - 1, 0)
                        absx(HALF - 1, 1)

                    @block.vector
                    def _(dve):
                        link = linker(dve)
                        for a in range(2):
                            link(nc.vector.memset(gray[a][:], 0.0))

                        def grays(i, a):
                            dve.wait_ge(s_gt[a], i + 1)
                            dve.wait_ge(s_conv[2 * a + 1], i)
                            nc.vector.scalar_tensor_tensor(gray[a][:, :, 1:C + 1], xin[a][:, 1, :, :], GRAY[1], gt[a][:, :, :],
                                                           ALU.mult, ALU.add).then_inc(s_g1, 1)
                            dve.wait_ge(s_g1, i * 2 + a + 1)
                            nc.vector.scalar_tensor_tensor(gray[a][:, :, 1:C + 1], xin[a][:, 2, :, :], GRAY[2], gray[a][:, :, 1:C + 1],
                                                           ALU.mult, ALU.add).then_inc(s_gray[a], 1)

                        def edges(i, a):
                            for k in range(KC):
                                m = 2 * a + k
                                dve.wait_ge(s_gx[m], i + 1)
                                nc.vector.tensor_tensor(hT[:, k, bass.ds(i * CH + a * N, N)], gx[m][:, 0, :], gx[m][:, 1, :],
                                                        ALU.add).then_inc(s_h[m], 1)

                        def maxes(i):
                            for k in range(KC):
                                dve.wait_ge(s_h[k], i + 1)
                                dve.wait_ge(s_h[2 + k], i + 1)
                                nc.vector.reduce_max(cmax[:, k, bass.ds(i, 1)], hT[:, k, bass.ds(i * CH, CH)], AXX).then_inc(s_cm, 1)
                        grays(0, 0)
                        def turn(i):
                            grays(i, 1)
                            edges(i, 0)
                            grays(i + 1, 0)
                            edges(i, 1)
                            maxes(i)

                        turn(0)
                        with dve.Fori(1, HALF - 1) as i:
                            turn(i)
                        grays(HALF - 1, 1)
                        edges(HALF - 1, 0)
                        edges(HALF - 1, 1)
                        maxes(HALF - 1)
                        linked(link)

                    @block.tensor
                    def _(pe):
                        def conv(i, a):
                            pe.wait_ge(s_gray[a], i + 1)
                            for k in range(KC):
                                m = 2 * a + k
                                pe.wait_ge(s_h[m], i)
                                for t in range(2):
                                    for dx in range(3):
                                        last = nc.tensor.matmul(
                                            pc[m][:, :, 127 * t:127 * t + 129],
                                            gray[a][:, t, k * P + dx:k * P + dx + P],
                                            band[:, dx, :, 1 - t:130 - t],
                                            start=(t == 0 and dx == 0), stop=(t == 1 and dx == 2), skip_group_check=True)
                                last.then_inc(s_conv[m], 1)
                        def turn(i):
                            conv(i, 0)
                            conv(i, 1)

                        turn(0)
                        with pe.Fori(1, HALF) as i:
                            turn(i)

            with ExitStack() as st:
                def sb(name, shape, dt=F32):
                    return st.enter_context(nc.sbuf_tensor(name, shape, dt))
                cm, csc, cinv = (sb(n, [P, KC]) for n in ("cm", "cscale", "cinv"))
                wf = sb("wf", [P, KC, 6 * P])
                whi = sb("w_hi", [P, KC, 6 * P], F32R)
                wlo = sb("w_lo", [P, KC, 6 * P], F32R)
                xa = sb("xa", [P, KC, CH])
                xr = [sb(f"xr{a}", [P, KC, CH], F32R) for a in range(2)]
                qk = [sb(f"qk{a}", [P, 4, CH]) for a in range(2)]
                vt = [sb(f"vt{a}", [P, NT, C]) for a in range(2)]
                pq = [st.enter_context(nc.psum_tensor(f"pq{a}", [P, CH], F32)) for a in range(4)]
                pv = [st.enter_context(nc.psum_tensor(f"pv{a}", [P, 2, C], F32)) for a in range(4)]
                s_cs, s_wT, s_wf, s_wl = (sem(n) for n in ("cscale_ready", "wT_ready", "wf_ready", "w_split"))
                s_xa = sem("xa_ready")
                s_xr = sem("xr_ready")
                s_q = [sem(f"q_done{a}") for a in range(4)]
                s_v = [sem(f"v_done{a}") for a in range(4)]
                s_qk = sem("qk_ready")
                s_vt = sem("vt_ready")
                s_mm = sem("qkv_minmax")
                s_qst = [sem(f"qk_stored{a}") for a in range(2)]
                s_vst = [sem(f"v_stored{a}") for a in range(2)]

                with nc.Block() as block:
                    @block.tensor
                    def _(pe):
                        for m in range(6):
                            for k in range(KC):
                                n = m * KC + k
                                last = nc.tensor.transpose(pq[n // 4][:, (n % 4) * P:(n % 4 + 1) * P],
                                                           wdq[:, m, k * P:(k + 1) * P], ident[:, :])
                        last.then_inc(s_wT, 1)
                        pe.wait_ge(s_wl, 2)

                        def chunk(i, a):
                            n = i * 2 + a
                            pe.wait_ge(s_xr, n + 1)
                            for m in range(4):
                                pe.wait_ge(s_qk, n * 4 + m)
                                for k in range(KC):
                                    for w in (whi, wlo):
                                        last = nc.tensor.matmul(pq[m][:, :], w[:, k, m * P:(m + 1) * P], xr[a][:, k, :],
                                                                start=(k == 0 and w is whi), stop=(k == 1 and w is wlo))
                                last.then_inc(s_q[m], 1)
                            pe.wait_ge(s_vt, i * 4 + 2 * a)
                            for h in range(2):
                                for t in range(2):
                                    tt = 2 * h + t
                                    for k in range(KC):
                                        for w in (whi, wlo):
                                            last = nc.tensor.matmul(pv[2 * a + h][:, t, :], xr[a][:, k, tt * P:(tt + 1) * P],
                                                                    w[:, k, 4 * P:6 * P],
                                                                    start=(k == 0 and w is whi), stop=(k == 1 and w is wlo))
                                last.then_inc(s_v[2 * a + h], 1)
                        def turn(i):
                            chunk(i, 0)
                            chunk(i, 1)

                        turn(0)
                        with pe.Fori(1, NCH // 2) as i:
                            turn(i)

                    @block.scalar
                    def _(act):
                        act.wait_ge(s_wf, 12)
                        nc.scalar.copy(whi[:, :, :], wf[:, :, :]).then_inc(s_wl, 1)

                        def rounded(n):
                            act.wait_ge(s_xr, n)
                            for k in range(KC):
                                nc.scalar.activation(xa[:, k, :], hT[:, k, bass.ds(n * CH, CH)], ACT.Identity, bias=magic[:, 0:1],
                                                     scale=cinv[:, k:k + 1]).then_inc(s_xa, 1)

                        def chunk(i, a, more=True):
                            n = i * 2 + a
                            if more:
                                rounded(n + 1)
                            act.wait_ge(s_qst[a], i * 16)
                            if not (isinstance(i, int) and i == 0):
                                act.wait_ge(s_mm, n * 6 - 6)
                            for m in range(4):
                                act.wait_ge(s_q[m], n + 1)
                                nc.scalar.activation(qk[a][:, m, :], pq[m][:, :], ACT.Identity, bias=qb[:, m:m + 1]).then_inc(s_qk, 1)
                        act.wait_ge(s_cs, 1)
                        rounded(0)
                        def turn(i):
                            chunk(i, 0)
                            chunk(i, 1)

                        turn(0)
                        with act.Fori(1, NCH // 2 - 1) as i:
                            turn(i)
                        chunk(NCH // 2 - 1, 0)
                        chunk(NCH // 2 - 1, 1, more=False)

                    @block.vector
                    def _(dve):
                        link = linker(dve)
                        link(nc.vector.reduce_max(cm[:, :], cmax[:, :, :], AXX))
                        link(nc.vector.tensor_scalar(csc[:, :], cm[:, :], 0.0, 1.0 / QMAX, ALU.max, ALU.mult))
                        link(nc.vector.tensor_scalar(csc[:, :], csc[:, :], 1e-8, None, ALU.max))
                        nc.vector.reciprocal(cinv[:, :], csc[:, :]).then_inc(s_cs, 1)
                        dve.wait_ge(s_wT, 1)
                        for m in range(6):
                            for k in range(KC):
                                n = m * KC + k
                                nc.vector.tensor_scalar(wf[:, k, m * P:(m + 1) * P], pq[n // 4][:, (n % 4) * P:(n % 4 + 1) * P],
                                                        csc[:, k:k + 1], None, ALU.mult).then_inc(s_wf, 1)
                        dve.wait_ge(s_wl, 1)
                        nc.vector.tensor_tensor(wlo[:, :, :], wf[:, :, :], whi[:, :, :].bitcast(F32), ALU.subtract).then_inc(s_wl, 1)

                        def quant(i, a):
                            n = i * 2 + a
                            dve.wait_ge(s_xa, n * 2 + 2)
                            dve.wait_ge(s_v[2 * a + 1], i)
                            nc.vector.tensor_scalar(xr[a][:, :, :], xa[:, :, :], MAGIC + QMAX, MAGIC, ALU.min, ALU.subtract).then_inc(s_xr, 1)

                        def chunk(i, a):
                            n = i * 2 + a
                            for q in range(2):
                                dve.wait_ge(s_qk, n * 4 + 2 * q + 2)
                                src = qk[a][:, 2 * q:2 * q + 2, :].rearrange("p a b -> p (a b)")
                                nc.vector.tensor_reduce(mx[:, q, bass.ds(n, 1)], src, AXX, ALU.max).then_inc(s_mm, 1)
                                nc.vector.tensor_reduce(mn[:, q, bass.ds(n, 1)], src, AXX, ALU.min).then_inc(s_mm, 1)
                            dve.wait_ge(s_vst[a], i * 16)
                            for h in range(2):
                                dve.wait_ge(s_v[2 * a + h], i + 1)
                                nc.vector.tensor_tensor(vt[a][:, 2 * h:2 * h + 2, :], pv[2 * a + h][:, :, :],
                                                        vb[:, :].unsqueeze(1).broadcast_to([P, 2, C]), ALU.add).then_inc(s_vt, 1)
                            dve.wait_ge(s_vt, n * 2 + 2)
                            src = vt[a][:, :, :].rearrange("p a b -> p (a b)")
                            nc.vector.tensor_reduce(mx[:, 2, bass.ds(n, 1)], src, AXX, ALU.max).then_inc(s_mm, 1)
                            nc.vector.tensor_reduce(mn[:, 2, bass.ds(n, 1)], src, AXX, ALU.min).then_inc(s_mm, 1)
                        quant(0, 0)
                        def turn(i):
                            quant(i, 1)
                            chunk(i, 0)
                            quant(i + 1, 0)
                            chunk(i, 1)

                        turn(0)
                        with dve.Fori(1, NCH // 2 - 1) as i:
                            turn(i)
                        quant(NCH // 2 - 1, 1)
                        chunk(NCH // 2 - 1, 0)
                        chunk(NCH // 2 - 1, 1)
                        linked(link)

                    @block.sync
                    def _(sp):
                        def store(i, a):
                            n = i * 2 + a
                            sp.wait_ge(s_qk, n * 4 + 4)
                            sp.dma_start(qk_s.rearrange("(m p) t -> p m t", p=P)[:, :, bass.ds(n * CH, CH)], qk[a][:, :, :]).then_inc(s_qst[a], 16)
                            sp.wait_ge(s_vt, n * 2 + 2)
                            sp.dma_start(v_s.rearrange("(t p) c -> p t c", p=P)[:, bass.ds(n * NT, NT), :], vt[a][:, :, :]).then_inc(s_vst[a], 16)
                        def turn(i):
                            store(i, 0)
                            store(i, 1)

                        turn(0)
                        with sp.Fori(1, NCH // 2) as i:
                            turn(i)
                        for a in range(2):
                            sp.wait_ge(s_qst[a], 16 * (NCH // 2))
                            sp.wait_ge(s_vst[a], 16 * (NCH // 2))

        with ExitStack() as at:
            def sb(name, shape, dt=F32):
                return at.enter_context(nc.sbuf_tensor(name, shape, dt))

            def ps(name, shape, dt=F32):
                return at.enter_context(nc.psum_tensor(name, shape, dt))
            ext = sb("qkv_ext", [P, 2, 3])
            exta = sb("qkv_ext_all", [P, 2, 3])
            qsc, qinv, qtop, qtmp = (sb(n, [P, 3]) for n in ("qkv_scale", "qkv_inv", "qkv_top", "qkv_tmp"))
            esc = sb("exp_scale", [P, 1])
            aug = sb("aug_rows", [P, 2, J])
            own = sb("own_rows", [P, 2, J])
            ownr = sb("own_any", [P, 2])
            qinvm = sb("q_inv_masked", [P, 2])
            raw = [sb(f"raw{r}", [P, 6, N]) for r in range(3)]
            ki = [sb(f"ki{r}", [P, 2, N], BF16) for r in range(3)]
            yq = sb("yq", [P, 2, 2, N])
            QK = [sb(f"QK{r}", [P, G, 1 + J, N], BF16) for r in range(3)]
            V = [sb(f"V{r}", [P, 2, H, 32]) for r in range(3)]
            qT = [sb(f"qT{r}", [P, G, N], BF16) for r in range(3)]
            nm = sb("neg_max", [P, 2, H])
            attn = [sb(f"attn{r}", [P, 2, C]) for r in range(3)]
            rem = sb("neg_max_rest", [P, 2, H])
            Tm = sb("neg_max_parts", [P, 2, G, P], BF16)
            pr_ = [sb(f"probs{a}", [P, J, 2, N]) for a in range(2)]
            ot = [sb(f"ot{a}", [P, 2, N]) for a in range(2)]
            rden = [sb(f"rden{a}", [P, 2 * 2 * J]) for a in range(2)]
            pS = [ps(f"pS{a}", [P, 2, N]) for a in range(2)]
            pST = [ps(f"pST{a}", [P, 2, 2, N]) for a in range(2)]
            pO = ps("pO", [P, 2, N])
            pM = ps("pM", [P, 512])
            zT = pM[:, :].bitcast(BF16).rearrange("p (g q) -> p g q", g=G)

            s_ext, s_all, s_qsc, s_init = (sem(n) for n in ("ext_ready", "ext_reduced", "qkv_scales", "attn_init"))
            s_ld = [sem(f"raw_loaded{r}") for r in range(3)]
            s_y, s_kv, s_ki, s_qq, s_vq = (sem(n) for n in ("q_rounded", "kv_rounded", "k_int", "q_int", "v_int"))
            LEAD = 5
            INIT = 3 * 8 + 3 * 2 + 3 + 3
            s_sc = [sem(f"QK_placed{r}") for r in range(3)]
            s_S, s_red, s_m, s_z, s_qT = (sem(n) for n in ("S_done", "S_reduced", "max_parts", "max_T", "qT_ready"))
            s_st, s_exp, s_pv, s_ot, s_r, s_norm, s_run = (sem(n) for n in (
                "ST_done", "exp_done", "PV_done", "ot_ready", "R_done", "norm_done", "run_done"))
            s_ast = [sem(f"attn_stored{r}") for r in range(3)]
            s_mc, s_nc = sem("max_chain"), sem("norm_chain")
            s_aug, s_pad = sem("aug_chain"), sem("V_padded")

            with nc.Block() as block:
                @block.sync
                def _(sp):
                    def load(n, r):
                        sp.dma_start(raw[r][:, 0:4, :], qk_s.rearrange("(m p) t -> p m t", p=P)[:, :, bass.ds(n * N, N)]).then_inc(s_ld[r], 16)
                        sp.dma_start(raw[r][:, 4:6, :], v_s.rearrange("(t p) c -> p t c", p=P)[:, bass.ds(n * 2, 2), :]).then_inc(s_ld[r], 16)

                    def place(n, r):
                        sp.wait_ge(s_ki, n + 1)
                        for j in range(J):
                            for gm in range(2):
                                p0 = 32 * j + D * gm
                                sp.dma_start(QK[r][p0:p0 + D, gm::2, 1 + j, :], ki[r][p0:p0 + D, :, :]).then_inc(s_sc[r], 16)
                    for n in range(3):
                        load(n, n)
                    sp.wait_ge(s_init, INIT)
                    place(0, 0)
                    place(1, 1)

                    def step(n, r):
                        sp.wait_ge(s_vq, n + 1)
                        sp.wait_ge(s_ki, n + 1)
                        sp.wait_ge(s_qq, n * 2 + 2)
                        load(n + 3, r)
                        sp.wait_ge(s_st, n * 8)
                        place(n + 2, (r + 2) % 3)
                    step(0, 0)
                    step(1, 1)
                    def store(n, r):
                        sp.wait_ge(s_norm, n * 2 + 2)
                        sp.dma_start(at_s[:, bass.ds(n * 2, 2), :], attn[r][:, :, :]).then_inc(s_ast[r], 16)
                    with sp.Fori(0, 9) as i:
                        for k in range(3):
                            step(i * 3 + 2 + k, (2 + k) % 3)
                            store(i * 3 + k, k)
                    sp.wait_ge(s_st, 29 * 8)
                    place(31, 1)
                    for n in range(27, 32):
                        store(n, n % 3)
                    for r, uses in enumerate((11, 11, 10)):
                        sp.wait_ge(s_ast[r], uses * 16 + 16)

                @block.gpsimd
                def _(pool):
                    nc.gpsimd.memset(ext[:, :, :], 0.0).then_inc(s_aug, 1)
                    nc.gpsimd.memset(aug[:, :], 1.0).then_inc(s_aug, 1)
                    nc.gpsimd.memset(own[:, :, :], 1.0).then_inc(s_aug, 1)
                    pool.wait_ge(s_aug, 3)
                    for t, lo, hi, sign in ((aug, -D, D + 2, 1), (own, 0, D - 1, -1)):
                        nc.gpsimd.affine_select(out=t[:, :, :], in_=t[:, :, :], compare_op=ALU.is_ge, fill=0.0, base=lo,
                                                pattern=[[sign * D, 2], [-32, J]], channel_multiplier=1).then_inc(s_aug, 1)
                    pool.wait_ge(s_aug, 5)
                    for t, lo, hi, sign in ((aug, -D, D + 2, 1), (own, 0, D - 1, -1)):
                        nc.gpsimd.affine_select(out=t[:, :, :], in_=t[:, :, :], compare_op=ALU.is_ge, fill=0.0, base=hi,
                                                pattern=[[-sign * D, 2], [32, J]], channel_multiplier=-1).then_inc(s_aug, 1)
                    pool.wait_ge(s_ext, 1)
                    nc.gpsimd.partition_all_reduce(exta[:, :, :], ext[:, :, :], P, RMAX).then_inc(s_all, 1)
                    for r in range(3):
                        nc.gpsimd.memset(V[r][:, :, :, 0:D], 0.0).then_inc(s_init, 1)
                        nc.gpsimd.memset(V[r][:, :, :, D:D + 1], 1.0).then_inc(s_init, 1)
                        nc.gpsimd.memset(V[r][:, :, :, D + 1:32], 0.0).then_inc(s_pad, 1)
                    pool.wait_ge(s_pad, 3)
                    pool.wait_ge(s_qsc, 1)
                    pool.wait_ge(s_init, INIT)

                    def quant(n, r, after=None):
                        wait_apart(pool, s_kv, n * 2 + 1, s_tick)
                        nc.gpsimd.tensor_scalar(ki[r][:, :, :], raw[r][:, 2:4, :], qtop[:, 1:2], MAGIC,
                                                ALU.min, ALU.subtract).then_inc(s_ki, 1)
                        wait_apart(pool, s_qq, n * 2, s_tick)
                        for gm in range(2):
                            nc.gpsimd.tensor_scalar(yq[:, gm, :, :], raw[r][:, 0:2, :], qinvm[:, gm:gm + 1], MAGIC,
                                                    ALU.mult, ALU.add).then_inc(s_y, 1)
                        if after is not None:
                            wait_apart(pool, s_st, after * 8, s_tick)
                        for gm in range(2):
                            wait_apart(pool, s_y, n * 2 + 1 + gm, s_tick)
                            nc.gpsimd.tensor_scalar(QK[r][:, gm::2, 0, :], yq[:, gm, :, :], qtop[:, 0:1], MAGIC,
                                                    ALU.min, ALU.subtract).then_inc(s_qq, 1)
                        if after is not None:
                            wait_apart(pool, s_pv, after * 4, s_tick)
                        wait_apart(pool, s_kv, n * 2 + 2, s_tick)
                        nc.gpsimd.tensor_scalar(V[r][:, :, :, 0:D], raw[r][:, 4:6, :].rearrange("p t (h d) -> p t h d", d=D), qtop[:, 2:3], MAGIC,
                                                ALU.min, ALU.subtract).then_inc(s_vq, 1)

                    def step(n, r, u):
                        if not (isinstance(n, int) and n == 0):
                            pool.wait_ge(s_sc[(r + 2) % 3], (u + (r + 2) // 3) * 128)
                        quant(n + 2, (r + 2) % 3, n)
                    quant(0, 0)
                    quant(1, 1)
                    step(0, 0, 0)
                    with pool.Fori(0, 9) as i:
                        for k in range(3):
                            step(i * 3 + 1 + k, (1 + k) % 3, i + (1 + k) // 3)
                    step(28, 1, 9)
                    step(29, 2, 9)

                @block.tensor
                def _(pe):
                    def S(n, r, u, c0, c1):
                        for c in range(c0, c1):
                            g, qt, h2 = c // 4, (c // 2) % 2, c % 2
                            if c == 0:
                                pe.wait_ge(s_sc[r], u * 128 + 128)
                                pe.wait_ge(s_qq, n * 2 + 2)
                            if not (isinstance(n, int) and n == 0 and c < 2):
                                pe.wait_ge(s_red, n * 16 + c - 1)
                            nc.tensor.matmul(pS[c % 2][:, :, :], QK[r][:, g, 0, qt * P:qt * P + P], QK[r][:, g, 1 + 2 * h2:3 + 2 * h2, :],
                                             start=True, stop=True).then_inc(s_S, 1)

                    def Z(n):
                        pe.wait_ge(s_m, n * 2 + 2)
                        if not (isinstance(n, int) and n <= 1):
                            pe.wait_ge(s_norm, n * 2 - 2)
                        for g in range(G):
                            for qt in range(2):
                                last = nc.tensor.transpose(zT[:, g, qt * P:qt * P + P], Tm[:, qt, g, :], identb[:, :])
                        last.then_inc(s_z, 1)

                    def ST(n, r, g, h2):
                        if g == 0 and h2 == 0:
                            pe.wait_ge(s_qT, n + 1)
                        if not (isinstance(n, int) and n == 0 and g == 0):
                            pe.wait_ge(s_exp, n * 8 + 2 * g + h2 - 1)
                        for j in range(2):
                            for kt in range(2):
                                last = nc.tensor.matmul(pST[h2][:, j, kt, :], QK[r][:, g, 1 + 2 * h2 + j, kt * P:kt * P + P],
                                                        qT[r][:, g, :], start=True, stop=True)
                        last.then_inc(s_st, 1)

                    def PV(n, r, g, kt):
                        if kt == 0:
                            if g == 0:
                                pe.wait_ge(s_vq, n + 1)
                            pe.wait_ge(s_exp, n * 8 + 2 * g + 2)
                            if g % 2 == 0:
                                pe.wait_ge(s_ot, n * 2 + g // 2)
                        for j in range(J):
                            last = nc.tensor.matmul(pO[32 * j:32 * j + 32, g % 2, :], V[r][:, kt, 8 * (g // 2) + 2 * j + g % 2, :],
                                                    pr_[g % 2][:, j, kt, :], start=(kt == 0), stop=(kt == 1))
                        if kt == 1:
                            last.then_inc(s_pv, 1)

                    def R(n, h):
                        pe.wait_ge(s_ot, n * 2 + h + 1)
                        if h:
                            pe.wait_ge(s_norm, n * 2 + 1)
                        else:
                            pe.wait_ge(s_qT, min(n + 2, B) if isinstance(n, int) else n + 2)
                        for qt in range(2):
                            for g in range(2):
                                c = (qt * 2 + g) * P
                                last = nc.tensor.transpose(pM[:, c:c + P], ot[h][:, g, qt * P:qt * P + P], ident[:, :])
                        last.then_inc(s_r, 1)

                    def image(n, r, u, first=False, left=2):
                        for slot in range(16):
                            g, s = slot // 4, slot % 4
                            c = slot + LEAD
                            if c < 16 and left >= 1:
                                S(n + 1, (r + 1) % 3, u + (r + 1) // 3, c, c + 1)
                            if c >= 16 and left >= 2:
                                S(n + 2, (r + 2) % 3, u + (r + 2) // 3, c - 16, c - 15)
                            if s % 2 == 0:
                                ST(n, r, g, s // 2)
                            elif g > 0:
                                PV(n, r, g - 1, s // 2)
                            elif not first:
                                PV(n - 1, (r + 2) % 3, 3, s // 2)
                            if slot == 1 and not first:
                                R(n - 1, 0)
                            if slot == 6 and not first:
                                R(n - 1, 1)
                            if slot == 13 and left >= 1:
                                Z(n + 1)
                    S(0, 0, 0, 0, 16)
                    Z(0)
                    S(1, 1, 0, 0, LEAD)
                    image(0, 0, 0, first=True)
                    with pe.Fori(0, 9) as i:
                        for k in range(3):
                            image(i * 3 + 1 + k, (1 + k) % 3, i + (1 + k) // 3)
                    for n in range(28, B):
                        image(n, n % 3, n // 3, left=B - 1 - n)
                    PV(31, 1, 3, 0)
                    PV(31, 1, 3, 1)
                    pe.wait_ge(s_norm, 62)
                    R(31, 0)
                    R(31, 1)

                @block.scalar
                def _(act):
                    def exps(n, g, first=False):
                        for h2 in range(2):
                            act.wait_ge(s_st, n * 8 + 2 * g + h2 + 1)
                            if not (first and g < 2):
                                act.wait_ge(s_pv, n * 4 + g - 1)
                            nc.scalar.activation(pr_[g % 2][:, 2 * h2:2 * h2 + 2, :, :], pST[h2][:, :, :, :], ACT.Exp,
                                                 scale=esc[:, 0:1]).then_inc(s_exp, 1)

                    def evac(n, h):
                        act.wait_ge(s_pv, n * 4 + 2 * h + 2)
                        if isinstance(n, int) and n == 0:
                            act.wait_ge(s_r, 1)
                        else:
                            act.wait_ge(s_r, n * 2 + h)
                        nc.scalar.copy(ot[h][:, :, :], pO[:, :, :]).then_inc(s_ot, 1)

                    def round_kv(n, r, u):
                        act.wait_ge(s_ld[r], u * 32 + 32)
                        for t in (1, 2):
                            nc.scalar.activation(raw[r][:, 2 * t:2 * t + 2, :], raw[r][:, 2 * t:2 * t + 2, :], ACT.Identity,
                                                 bias=magic[:, 0:1], scale=qinv[:, t:t + 1]).then_inc(s_kv, 1)

                    def image(n, r, u, first=False, left=3):
                        exps(n, 0, first)
                        if not first:
                            evac(n - 1, 1)
                        exps(n, 1, first)
                        exps(n, 2)
                        evac(n, 0)
                        if left >= 3:
                            round_kv(n + 3, r, u + 1)
                        exps(n, 3)
                    act.wait_ge(s_aug, 7)
                    for j in range(J):
                        for gm in range(2):
                            nc.scalar.copy(QK[1][:, gm::2, 1 + j, :],
                                           aug[:, gm, j:j + 1].unsqueeze(2).broadcast_to([P, 2, N])).then_inc(s_init, 1)
                    act.wait_ge(s_qsc, 1)
                    for r in range(3):
                        round_kv(r, r, 0)
                    image(0, 0, 0, first=True)
                    with act.Fori(0, 9) as i:
                        for k in range(3):
                            image(i * 3 + 1 + k, (1 + k) % 3, i + (1 + k) // 3)
                    for n in range(28, B):
                        image(n, n % 3, n // 3, left=B - 1 - n)
                    evac(31, 1)

                @block.vector
                def _(dve):
                    link = linker(dve)
                    dve.wait_ge(s_aug, 1)
                    link(nc.vector.tensor_reduce(ext[:, 0, :], mx[:, :, :], AXX, ALU.max))
                    nc.vector.tensor_reduce(ext[:, 1, :], mn[:, :, :], AXX, ALU.min, negate=True).then_inc(s_ext, 1)
                    dve.wait_ge(s_aug, 7)
                    def k_rows(r):
                        for j in range(J):
                            for gm in range(2):
                                nc.vector.tensor_copy(QK[r][:, gm::2, 1 + j, :],
                                                      aug[:, gm, j:j + 1].unsqueeze(2).broadcast_to([P, 2, N])).then_inc(s_init, 1)
                    k_rows(0)
                    dve.wait_ge(s_all, 1)
                    link(nc.vector.tensor_scalar(exta[:, 1, :], exta[:, 1, :], -1.0, None, ALU.mult))
                    quant_scalars(dve, link, exta[:, 0, :], exta[:, 1, :], qsc[:, :], qinv[:, :], qtop[:, :], qtmp[:, :])
                    link(nc.vector.reduce_max(ownr[:, :], own[:, :, :], AXX))
                    link(nc.vector.tensor_scalar(qinvm[:, :], ownr[:, :], qinv[:, 0:1], None, ALU.mult))
                    nc.vector.scalar_tensor_tensor(esc[:, :], qsc[:, 0:1], D ** -0.5, qsc[:, 1:2], ALU.mult, ALU.mult).then_inc(s_qsc, 1)
                    k_rows(2)
                    for r in range(3):
                        nc.vector.memset(QK[r][:, :, 0, :], 0.0).then_inc(s_init, 1)
                        nc.vector.memset(attn[r][:], 0.0).then_inc(s_ast[r], 16)
                    nc.vector.memset(ot[0][:], 0.0).then_inc(s_init, 1)
                    nc.vector.memset(ot[1][:], 0.0).then_inc(s_r, 1)
                    nc.vector.memset(Tm[:], 0.0).then_inc(s_init, 1)
                    nc.vector.memset(rden[0][:], 0.0).then_inc(s_init, 1)

                    def reduce(n, c0, c1):
                        for c in range(c0, c1):
                            g, qt, h2 = c // 4, (c // 2) % 2, c % 2
                            dve.wait_ge(s_S, n * 16 + c + 1)
                            if c == 0 and not (isinstance(n, int) and n == 0):
                                dve.wait_ge(s_mc, (n - 1) * 6 + 4)
                            nc.vector.tensor_reduce(nm[:, qt, 4 * g + 2 * h2:4 * g + 2 * h2 + 2], pS[c % 2][:, :, :], AXX, ALU.max,
                                                    negate=True).then_inc(s_red, 1)

                    def parts(n, second):
                        if not second:
                            dve.wait_ge(s_red, n * 16 + 16)
                            if not (isinstance(n, int) and n == 0):
                                dve.wait_ge(s_z, n)
                        src = nm[:, :, :].rearrange("p q (m s j) -> p (q m) s j", s=2, j=J)
                        rst = rem[:, :, :].rearrange("p q (m s j) -> p (q m) s j", s=2, j=J)
                        to = [Tm[:, :, gm::2, :].rearrange("p q m (j e) -> p (q m) j e", e=32)[:, :, :, D * (1 - gm):D * (1 - gm) + 3]
                              for gm in range(2)]
                        if not second:
                            for gm in range(2):
                                nc.vector.tensor_copy(to[gm][:, :, :, 0], src[:, :, gm, :]).then_inc(s_mc, 1)
                            for gm in range(2):
                                dve.wait_ge(s_mc, n * 6 + 1 + gm)
                                nc.vector.tensor_tensor(rst[:, :, gm, :], src[:, :, gm, :], to[gm][:, :, :, 0], ALU.subtract).then_inc(s_mc, 1)
                            return
                        for gm in range(2):
                            dve.wait_ge(s_mc, n * 6 + 3 + gm)
                            nc.vector.tensor_copy(to[gm][:, :, :, 1], rst[:, :, gm, :]).then_inc(s_mc, 1)
                        for gm in range(2):
                            dve.wait_ge(s_mc, n * 6 + 5 + gm)
                            nc.vector.tensor_tensor(to[gm][:, :, :, 2], rst[:, :, gm, :], to[gm][:, :, :, 1], ALU.subtract).then_inc(s_m, 1)

                    def addq(n, r):
                        dve.wait_ge(s_z, n + 1)
                        nc.vector.tensor_tensor(qT[r][:, :, :], zT[:, :, :], QK[r][:, :, 0, :], ALU.add).then_inc(s_qT, 1)

                    src = pM[:, :].rearrange("p (u e) -> p u e", e=32)

                    def norm_scale(n, h):
                        dve.wait_ge(s_r, n * 2 + h + 2)
                        nc.vector.reciprocal(rden[h][:, :], src[:, :, D]).then_inc(s_nc, 1)
                        dve.wait_ge(s_nc, n * 4 + 2 * h + 1)
                        nc.vector.tensor_scalar(rden[h][:, :], rden[h][:, :], qsc[:, 2:3], None, ALU.mult).then_inc(s_nc, 1)

                    def norm(n, h, r, u):
                        dve.wait_ge(s_nc, n * 4 + 2 * h + 2)
                        dve.wait_ge(s_ast[r], u * 16 + 16)
                        out_ = attn[r][:, :, P * h:P * h + P].rearrange("p t (u d) -> p t u d", d=D)
                        nc.vector.tensor_tensor(out_, src[:, :, 0:D].rearrange("p (t u) d -> p t u d", t=2),
                                                rden[h][:, :].rearrange("p (t u) -> p t u", t=2).unsqueeze(3).broadcast_to([P, 2, 8, D]),
                                                ALU.mult).then_inc(s_norm, 1)

                    def extreme(n, r, to, op):
                        dve.wait_ge(s_norm, n * 2 + 2)
                        nc.vector.tensor_reduce(to[:, bass.ds(n, 1)], attn[r][:, :, :].rearrange("p a b -> p (a b)"), AXX, op)

                    def image(n, r, u, first=False, left=2):
                        m, mr, mu = n - 1, (r + 2) % 3, u + (r + 2) // 3 - 1
                        for slot in range(16):
                            c = slot + LEAD
                            if c < 16 and left >= 1:
                                reduce(n + 1, c, c + 1)
                            if c >= 16 and left >= 2:
                                reduce(n + 2, c - 16, c - 15)
                            if not first:
                                if slot == 2:
                                    norm_scale(m, 0)
                                if slot == 3:
                                    norm(m, 0, mr, mu)
                                if slot == 7:
                                    norm_scale(m, 1)
                                if slot == 8:
                                    norm(m, 1, mr, mu)
                                if slot == 9:
                                    extreme(m, mr, omx, ALU.max)
                                if slot == 12:
                                    extreme(m, mr, omn, ALU.min)
                            if left >= 1:
                                if slot == 15 - LEAD:
                                    parts(n + 1, False)
                                if slot == 16 - LEAD:
                                    parts(n + 1, True)
                                if slot == 13:
                                    addq(n + 1, (r + 1) % 3)
                    dve.wait_ge(s_init, INIT)
                    reduce(0, 0, 16)
                    parts(0, False)
                    parts(0, True)
                    addq(0, 0)
                    reduce(1, 0, LEAD)
                    image(0, 0, 0, first=True)
                    with dve.Fori(0, 9) as i:
                        for k in range(3):
                            image(i * 3 + 1 + k, (1 + k) % 3, i + (1 + k) // 3)
                    for n in range(28, B):
                        image(n, n % 3, n // 3, left=B - 1 - n)
                    for h in range(2):
                        norm_scale(31, h)
                        norm(31, h, 1, 10)
                    extreme(31, 1, omx, ALU.max)
                    extreme(31, 1, omn, ALU.min)
                    linked(link)

        with ExitStack() as ff:
            def sb(name, shape, dt=F32):
                return ff.enter_context(nc.sbuf_tensor(name, shape, dt))

            def ps(name, shape, dt=F32):
                return ff.enter_context(nc.psum_tensor(name, shape, dt))
            ghi, glo, uhi, ulo = (sb(n, [P, KC, NE, I], F32R) for n in ("gate_hi", "gate_lo", "up_hi", "up_lo"))
            dhi, dlo = (sb(n, [P, NE, C], F32R) for n in ("down_hi", "down_lo"))
            rhi, rlo = (sb(n, [P, KC, E], F32R) for n in ("router_hi", "router_lo"))
            s_sl, s_hi2, s_lo2 = sem("ffn_staged"), sem("split_hi"), sem("split_lo")
            with ExitStack() as sg_:
                stage = [sg_.enter_context(nc.sbuf_tensor(f"stage{a}", [P, KC * NE * I], F32)) for a in range(3)]
                stager = sg_.enter_context(nc.sbuf_tensor("stage_router", [P, KC * E], F32))
                flat = lambda t: t[:, :, :, :].rearrange("p k e i -> p (k e i)")
                parts3 = ((stage[0][:, :], flat(ghi), flat(glo)), (stage[1][:, :], flat(uhi), flat(ulo)),
                          (stage[2][:, :], dhi[:, :, :].rearrange("p e c -> p (e c)"), dlo[:, :, :].rearrange("p e c -> p (e c)")),
                          (stager[:, :], rhi[:, :, :].rearrange("p k e -> p (k e)"), rlo[:, :, :].rearrange("p k e -> p (k e)")))
                with nc.Block() as block:
                    @block.sync
                    def _(sp):
                        for t, w in zip(parts3, (gate_t, up_t, down_t, router_t)):
                            w = w.rearrange("p k e i -> p (k e i)") if len(w.shape) == 4 else w.rearrange("p a b -> p (a b)")
                            sp.dma_start(t[0], w).then_inc(s_sl, 16)

                    @block.scalar
                    def _(act):
                        act.wait_ge(s_sl, 64)
                        for t, hi, lo in parts3:
                            nc.scalar.copy(hi, t).then_inc(s_hi2, 1)

                    @block.vector
                    def _(dve):
                        for n, (t, hi, lo) in enumerate(parts3):
                            dve.wait_ge(s_hi2, n + 1)
                            nc.vector.tensor_tensor(lo, t, hi.bitcast(F32), ALU.subtract).then_inc(s_lo2, 1)
            eb = sb("e_bias_all", [P, E])
            oext, oexta = sb("attn_ext", [P, 2]), sb("attn_ext_all", [P, 2])
            osc, oinv, otop, otmp = (sb(n, [P, 1]) for n in ("attn_scale", "attn_inv", "attn_top", "attn_tmp"))
            psc = sb("proj_scale_all", [P, KC])
            pick = sb("pick", [3 * E, E, P], BF16)
            lower4, lower16 = sb("lower4", [P, 4, 4]), sb("lower16", [P, E, E])
            rest15 = sb("rest15", [P, E])
            ac = [sb(f"attn_chunk{a}", [P, NT, C]) for a in range(2)]
            hc = [sb(f"edge_chunk{a}", [P, KC, CH]) for a in range(2)]
            oq = sb("attn_int", [P, NT, C], BF16)
            oqT = sb("attn_int_T", [P, KC, CH], BF16)
            x1T = sb("x1_T", [P, KC, CH])
            h1 = [sb(f"h1_{a}", [P, NT, C]) for a in range(2)]
            xh = [sb(f"h1T_hi{a}", [P, KC, CH], F32R) for a in range(2)]
            xl = [sb(f"h1T_lo{a}", [P, KC, CH], F32R) for a in range(2)]
            st6, mv, rs = sb("ln_stats", [P, NT, 6]), sb("ln_mv", [P, NT, 2]), sb("ln_rstd", [P, NT])
            st6b, mvb, rsb = sb("ln2_stats", [P, NT, 6]), sb("ln2_mv", [P, NT, 2]), sb("ln2_rstd", [P, NT])
            sg, scb, msk = (sb(n, [P, NT, E]) for n in ("scores", "scores_biased", "scores_masked"))
            pmx, pmn = sb("pair_max", [P, 16, 2]), sb("pair_min", [P, 16, 2])
            g1, g2, g3, gsum, grank, gsel = (sb(n, [P, NT * 4]) for n in ("g1", "g2", "g3", "gsum", "grank", "gsel"))
            cmp4, cmp4b = sb("cmp4", [P, NT, 4, 4]), sb("cmp4b", [P, NT, 4, 4])
            cmp16 = sb("cmp16", [P, NT, E, E])
            rrow, rcol, comb = (sb(n, [P, NT, E]) for n in ("rank_row", "rank_col", "combine"))
            wsum = sb("weight_sum", [P, NT])
            mhalf = sb("minus_half", [P, NT])
            cpart = sb("combine_parts", [P, NT, 3, E], BF16)
            crest = sb("combine_rest", [P, NT, E])
            cT = [sb(f"combine_T{a}", [3 * E, CH], BF16) for a in range(2)]
            sl = [sb(f"silu{a}", [P, CH]) for a in range(2)]
            sc_ = [sb(f"silu_combined{a}", [P, CH]) for a in range(2)]
            prod = [sb(f"prod{a}", [P, CH]) for a in range(2)]
            ph = [sb(f"prod_hi{a}", [P, CH], F32R) for a in range(3)]
            pl = [sb(f"prod_lo{a}", [P, CH], F32R) for a in range(3)]
            ys = sb("y", [P, NT, C])
            yo = sb("y_out", [P, NT, C])
            pG = [ps(f"pG{a}", [P, CH]) for a in range(2)]
            pU = [ps(f"pU{a}", [P, CH]) for a in range(2)]
            pC = ps("pC", [P, CH])
            pA = [ps(f"pA{a}", [P, 2, C]) for a in range(2)]
            pX = ps("pX", [P, CH])
            pXb = pX[:, :].bitcast(BF16)

            s_wl2, s_ext2, s_all2, s_osc, s_cst = (sem(n) for n in (
                "ffn_loaded", "attn_ext_ready", "attn_ext_reduced", "attn_scales", "ffn_consts"))
            s_cl = [sem(f"chunk_loaded{a}") for a in range(2)]
            (s_oy, s_oq, s_oT, s_oTs, s_pj, s_pja, s_x1, s_xn, s_mv, s_rs, s_h1, s_hT, s_spl) = (sem(n) for n in (
                "attn_rounded", "attn_int_ready", "attn_T_done", "attn_T_ready", "proj_done", "proj_scaled", "x1_ready",
                "x1_transposed", "ln_mv_ready", "ln_rstd_ready", "h1_ready", "h1_transposed", "h1T_split"))
            (s_rt, s_sig, s_cb, s_cT, s_cTs, s_route) = (sem(n) for n in (
                "router_done", "scores_ready", "combine_ready", "combine_T_done", "combine_T_ready", "route_chain"))
            (s_G, s_U, s_C, s_silu, s_t1, s_prod, s_dn, s_y2, s_mv2, s_rs2, s_yo, s_out, s_bn, s_bn2) = (sem(n) for n in (
                "gate_done", "up_done", "spread_done", "silu_ready", "silu_combined", "prod_ready", "down_done", "y_ready",
                "ln2_mv_ready", "ln2_rstd_ready", "out_ready", "out_stored", "ln_chain", "ln2_chain"))
            s_ph, s_pl = sem("prod_hi_ready"), sem("prod_lo_ready")
            s_pw, s_pw2 = sem("power_chain"), sem("power2_chain")

            with nc.Block() as block:
                @block.sync
                def _(sp):
                    sp.dma_start(eb[:, :], e_bias.rearrange("(o n) -> o n", o=1).broadcast_to([P, E])).then_inc(s_wl2, 16)

                    def load(n, a):
                        sp.dma_start(ac[a][:, :, :], at_s[:, bass.ds(n * NT, NT), :]).then_inc(s_cl[a], 16)
                        sp.dma_start(hc[a][:, :, :], hs[:, :, bass.ds(n * CH, CH)]).then_inc(s_cl[a], 16)

                    load(0, 0)
                    load(1, 1)

                    def reload(n, a):
                        sp.wait_ge(s_x1, n * 2 - 2)
                        load(n, a)

                    def store(n):
                        sp.wait_ge(s_yo, n * NT + NT)
                        sp.dma_start(out.rearrange("b (t p) c -> p (b t) c", p=P)[:, bass.ds(n * NT, NT), :], yo[:, :, :]).then_inc(s_out, 16)
                    reload(2, 0)
                    reload(3, 1)
                    with sp.Fori(0, 6) as i:
                        for a in range(2):
                            store(i * 2 + a)
                            reload(i * 2 + 4 + a, a)
                    for n in range(12, NCH):
                        store(n)
                    sp.wait_ge(s_out, 16 * NCH + 16)

                @block.gpsimd
                def _(pool):
                    nc.gpsimd.memset(pick[:, :, :], 0.0).then_inc(s_cst, 1)
                    nc.gpsimd.memset(lower4[:, :, :], 1.0).then_inc(s_cst, 1)
                    nc.gpsimd.memset(lower16[:, :, :], 1.0).then_inc(s_cst, 1)
                    nc.gpsimd.iota(rest15[:, :], pattern=[[-1, E]], base=15, channel_multiplier=0,
                                   allow_small_or_imprecise_dtypes=True).then_inc(s_cst, 1)
                    nc.gpsimd.memset(mhalf[:, :], -0.5).then_inc(s_cst, 1)
                    pool.wait_ge(s_cst, 5)
                    for t, w in ((lower4, 4), (lower16, E)):
                        nc.gpsimd.affine_select(out=t[:, :, :], in_=t[:, :, :], compare_op=ALU.is_ge, fill=0.0, base=-1,
                                                pattern=[[1, w], [-1, w]], channel_multiplier=0).then_inc(s_cst, 1)
                    for k in range(3):
                        nc.gpsimd.affine_select(out=pick[:, :, :], in_=pick[:, :, :], compare_op=ALU.not_equal, fill=1.0, base=-E * k,
                                                pattern=[[-1, E], [0, P]], channel_multiplier=1).then_inc(s_cst, 1)
                        pool.wait_ge(s_cst, 8 + k)
                    pool.wait_ge(s_ext2, 2)
                    nc.gpsimd.partition_all_reduce(oexta[:, :], oext[:, :], P, RMAX).then_inc(s_all2, 1)
                    pool.wait_ge(s_osc, 1)

                    def quant(n, a, u):
                        wait_apart(pool, s_cl[a], u * 32 + 32, s_tick)
                        nc.gpsimd.tensor_scalar(ac[a][:, :, :], ac[a][:, :, :], oinv[:, 0:1], MAGIC, ALU.mult, ALU.add).then_inc(s_oy, 1)
                        wait_apart(pool, s_oy, n + 1, s_tick)
                        wait_apart(pool, s_oT, n, s_tick)
                        nc.gpsimd.tensor_scalar(oq[:, :, :], ac[a][:, :, :], otop[:, 0:1], MAGIC, ALU.min, ALU.subtract).then_inc(s_oq, 1)

                    def residual(n, a, k):
                        pool.wait_ge(s_pja, n * 2 + k + 1)
                        nc.gpsimd.tensor_tensor(x1T[:, k, :], x1T[:, k, :], hc[a][:, k, :], ALU.add).then_inc(s_x1, 1)

                    def low(n, e, start=False):
                        q = n * NE + e
                        if not (start and e < 3):
                            pool.wait_ge(s_dn, q - 2)
                        pool.wait_ge(s_ph, q + 1)
                        nc.gpsimd.tensor_tensor(pl[e % 3][:, :], prod[e % 2][:, :], ph[e % 3][:, :].bitcast(F32), ALU.subtract).then_inc(s_pl, 1)

                    def power(o, var, n, s_, chain):
                        nc.gpsimd.tensor_scalar(o, var, LN_EPS, None, ALU.add).then_inc(chain, 1)
                        pool.wait_ge(chain, n + 1)
                        nc.gpsimd.tensor_tensor(o, o, mhalf[:, 0:o.shape[1]], ALU.pow).then_inc(s_, 1)

                    def rstd(n, h):
                        wait_apart(pool, s_mv, n * NT + 2 * h + 2, s_tick)
                        power(rs[:, 2 * h:2 * h + 2], mv[:, 2 * h:2 * h + 2, 1], n * 2 + h, s_rs, s_pw)

                    def rstd2(n):
                        wait_apart(pool, s_mv2, n * NT + NT, s_tick)
                        power(rsb[:, :], mvb[:, :, 1], n, s_rs2, s_pw2)

                    quant(0, 0, 0)
                    residual(0, 0, 0)
                    residual(0, 0, 1)
                    rstd(0, 0)
                    rstd(0, 1)
                    quant(1, 1, 0)

                    def chunk(n, a, u, first=False, left=2):
                        for e in range(NE):
                            if e > 0:
                                low(n, e - 1, first)
                            elif not first:
                                low(n - 1, NE - 1)
                            if e == 3 and not first:
                                rstd2(n - 1)
                            if left >= 1:
                                if e in (3, 4):
                                    residual(n + 1, 1 - a, e - 3)
                                if e in (6, 8):
                                    rstd(n + 1, (e - 6) // 2)
                            if left >= 2 and e == 11:
                                quant(n + 2, a, u + 1)
                    chunk(0, 0, 0, first=True)
                    with pool.Fori(0, 6) as i:
                        chunk(i * 2 + 1, 1, i)
                        chunk(i * 2 + 2, 0, i + 1)
                    chunk(13, 1, 6)
                    chunk(14, 0, 7, left=1)
                    chunk(15, 1, 7, left=0)
                    low(15, NE - 1)
                    rstd2(15)

                @block.scalar
                def _(act):
                    def evacT(n):
                        act.wait_ge(s_oT, n + 1)
                        act.wait_ge(s_pj, n * 2)
                        nc.scalar.copy(oqT[:, :, :], pXb.rearrange("p (k t) -> p k t", k=KC)).then_inc(s_oTs, 1)

                    def scale(n, k):
                        act.wait_ge(s_pj, n * 2 + k + 1)
                        act.wait_ge(s_xn, n * 2)
                        nc.scalar.activation(x1T[:, k, :], pX[:, :], ACT.Identity, bias=pb[:, k:k + 1], scale=psc[:, k:k + 1]).then_inc(s_pja, 1)

                    def score(n):
                        act.wait_ge(s_rt, n + 1)
                        act.wait_ge(s_cb, n * 3)
                        nc.scalar.activation(sg[:, :, :], pX[:, 0:NT * E].rearrange("p (t e) -> p t e", e=E), ACT.Sigmoid).then_inc(s_sig, 1)

                    act.wait_ge(s_osc, 1)
                    evacT(0)
                    scale(0, 0)
                    scale(0, 1)
                    score(0)

                    def high(n, e, start=False):
                        q = n * NE + e
                        if not (start and e < 3):
                            act.wait_ge(s_dn, q - 2)
                        act.wait_ge(s_prod, q + 1)
                        nc.scalar.copy(ph[e % 3][:, :], prod[e % 2][:, :]).then_inc(s_ph, 1)

                    def chunk(n, first=False, final=False):
                        for e in range(NE):
                            if not final:
                                if e == 1:
                                    evacT(n + 1)
                                if e in (2, 3):
                                    scale(n + 1, e - 2)
                                if e == 12:
                                    score(n + 1)
                            act.wait_ge(s_G, n * NE + e + 1)
                            if not (first and e < 2):
                                act.wait_ge(s_prod, n * NE + e - 1)
                            nc.scalar.activation(sl[e % 2][:, :], pG[e % 2][:, :], ACT.Silu).then_inc(s_silu, 1)
                            if e > 0:
                                high(n, e - 1, first)
                            elif not first:
                                high(n - 1, NE - 1)
                    chunk(0, first=True)
                    with act.Fori(0, NCH - 2) as i:
                        chunk(i + 1)
                    chunk(NCH - 1, final=True)
                    high(NCH - 1, NE - 1)

                @block.tensor
                def _(pe):
                    def oT(n):
                        pe.wait_ge(s_oq, n + 1)
                        pe.wait_ge(s_cTs, n)
                        for k in range(KC):
                            for t in range(NT):
                                last = nc.tensor.transpose(pXb[:, k * CH + t * P:k * CH + t * P + P], oq[:, t, k * P:k * P + P], identb[:, :])
                        last.then_inc(s_oT, 1)

                    def proj(n, m):
                        pe.wait_ge(s_oTs, n + 1)
                        pe.wait_ge(s_pja, n * 2 + m)
                        for k in range(KC):
                            last = nc.tensor.matmul(pX[:, :], pint[:, k, m * P:m * P + P], oqT[:, k, :], start=(k == 0), stop=(k == 1))
                        last.then_inc(s_pj, 1)

                    def xn(n, h):
                        pe.wait_ge(s_x1, n * 2 + 2)
                        pe.wait_ge(s_h1, n * NT + 2 * h)
                        for t in range(2):
                            for k in range(KC):
                                c = t * C + k * P
                                tt = (2 * h + t) * P
                                last = nc.tensor.transpose(pX[:, c:c + P], x1T[:, k, tt:tt + P], ident[:, :])
                        last.then_inc(s_xn, 1)

                    def hT_(n, a, k):
                        pe.wait_ge(s_h1, n * NT + NT)
                        pe.wait_ge(s_spl, n * 4 + 2 * k)
                        for t in range(NT):
                            last = nc.tensor.transpose(pX[:, t * P:t * P + P], h1[a][:, t, k * P:k * P + P], ident[:, :])
                        last.then_inc(s_hT, 1)

                    def route(n, a):
                        pe.wait_ge(s_spl, n * 4 + 4)
                        for t in range(NT):
                            m = 0
                            for k in range(KC):
                                for x_, w_ in ((xh, rhi), (xh, rlo), (xl, rhi)):
                                    last = nc.tensor.matmul(pX[:, t * E:t * E + E], x_[a][:, k, t * P:t * P + P], w_[:, k, :],
                                                            start=(m == 0), stop=(m == 5))
                                    m += 1
                        last.then_inc(s_rt, 1)

                    def combT(n):
                        wait_apart(pe, s_cb, n * 3 + 3, s_tick)
                        for t in range(NT):
                            last = nc.tensor.transpose(pXb[0:3 * E, t * P:t * P + P], cpart[:, t, :, :].rearrange("p a e -> p (a e)"), identb[:, :])
                        last.then_inc(s_cT, 1)

                    def down(n, e):
                        q = n * NE + e
                        pe.wait_ge(s_pl, q + 1)
                        if e == 0:
                            pe.wait_ge(s_y2, n * 2)
                        for t in range(NT):
                            for m, (x_, w_) in enumerate(((ph, dhi), (ph, dlo), (pl, dhi))):
                                last = nc.tensor.matmul(pA[t // 2][:, t % 2, :], x_[e % 3][:, t * P:t * P + P], w_[:, e, :],
                                                        start=(e == 0 and t % 2 == 0 and m == 0), stop=(e == NE - 1 and m == 2),
                                                        skip_group_check=True)
                        last.then_inc(s_dn, 1)

                    def chunk(n, a, first=False, final=False):
                        for e in range(NE):
                            q = n * NE + e
                            if e == 0:
                                pe.wait_ge(s_cTs, n + 1)
                            if not (first and e < 2):
                                pe.wait_ge(s_silu, q - 1)
                                pe.wait_ge(s_prod, q - 1)
                            for w, po, s_ in (((ghi, glo), pG, s_G), ((uhi, ulo), pU, s_U)):
                                m = 0
                                for k in range(KC):
                                    for x_, w_ in ((xh, w[0]), (xl, w[0]), (xh, w[1])):
                                        last = nc.tensor.matmul(po[e % 2][:, :], w_[:, k, e, :], x_[a][:, k, :], start=(m == 0), stop=(m == 5))
                                        m += 1
                                last.then_inc(s_, 1)
                            if e < E:
                                pe.wait_ge(s_t1, n * E + e)
                                nc.tensor.matmul(pC[:, :], pick[:, e, :], cT[a][:, :], start=True, stop=True).then_inc(s_C, 1)
                            if e > 1:
                                down(n, e - 2)
                            elif not first:
                                down(n - 1, NE - 2 + e)
                            if not final:
                                if e == 0:
                                    oT(n + 1)
                                if e in (1, 2):
                                    proj(n + 1, e - 1)
                                if e in (5, 7):
                                    xn(n + 1, (e - 5) // 2)
                                if e in (9, 10):
                                    hT_(n + 1, 1 - a, e - 9)
                                if e == 11:
                                    route(n + 1, 1 - a)
                                if e == 16:
                                    combT(n + 1)
                    oT(0)
                    proj(0, 0)
                    proj(0, 1)
                    xn(0, 0)
                    xn(0, 1)
                    hT_(0, 0, 0)
                    hT_(0, 0, 1)
                    route(0, 0)
                    combT(0)
                    pe.wait_ge(s_cst, 10)
                    pe.wait_ge(s_wl2, 16)
                    chunk(0, 0, first=True)
                    with pe.Fori(0, NCH // 2 - 1) as i:
                        chunk(i * 2 + 1, 1)
                        chunk(i * 2 + 2, 0)
                    chunk(NCH - 1, 1, final=True)
                    down(NCH - 1, NE - 2)
                    down(NCH - 1, NE - 1)

                @block.vector
                def _(dve):
                    link = linker(dve)
                    link(nc.vector.reduce_max(oext[:, 0:1], omx[:, :], AXX))
                    nc.vector.tensor_reduce(oext[:, 1:2], omn[:, :], AXX, ALU.min, negate=True).then_inc(s_ext2, 2)
                    dve.wait_ge(s_all2, 1)
                    link(nc.vector.tensor_scalar(oexta[:, 1:2], oexta[:, 1:2], -1.0, None, ALU.mult))
                    quant_scalars(dve, link, oexta[:, 0:1], oexta[:, 1:2], osc[:, :], oinv[:, :], otop[:, :], otmp[:, :])
                    nc.vector.tensor_scalar(psc[:, :], pscale[:, :], osc[:, 0:1], None, ALU.mult).then_inc(s_osc, 1)

                    def ln_stats(n, h):
                        dve.wait_ge(s_xn, n * 2 + h + 1)
                        for t in range(2):
                            nc.vector.bn_stats(st6[:, 2 * h + t, :], pX[:, t * C:t * C + C]).then_inc(s_bn, 1)
                        for t in range(2):
                            wait_apart(dve, s_bn, n * NT + 2 * h + t + 1, s_tick)
                            nc.vector.bn_aggr(mv[:, 2 * h + t, :], st6[:, 2 * h + t, :]).then_inc(s_mv, 1)

                    def ln_apply(n, a, h):
                        dve.wait_ge(s_rs, n * 2 + h + 1)
                        for t in range(2):
                            q = 2 * h + t
                            nc.vector.tensor_scalar(h1[a][:, q, :], pX[:, t * C:t * C + C], mv[:, q, 0:1], rs[:, q:q + 1],
                                                    ALU.subtract, ALU.mult).then_inc(s_h1, 1)

                    def split(n, a, k):
                        dve.wait_ge(s_hT, n * 2 + k + 1)
                        nc.vector.tensor_copy(xh[a][:, k, :], pX[:, :]).then_inc(s_spl, 1)
                        dve.wait_ge(s_spl, n * 4 + 2 * k + 1)
                        nc.vector.tensor_tensor(xl[a][:, k, :], pX[:, :], xh[a][:, k, :].bitcast(F32), ALU.subtract).then_inc(s_spl, 1)

                    def top_groups(n, c):
                        dve.wait_ge(s_sig, n + 1)
                        c(nc.vector.tensor_tensor(scb[:, :, :], sg[:, :, :], eb[:, :].unsqueeze(1).broadcast_to([P, NT, E]), ALU.add))
                        v = scb[:, :, :].rearrange("p t (g a b) -> p (t g) a b", a=2, b=2)
                        c(nc.vector.tensor_tensor(pmx[:, :, :], v[:, :, :, 0], v[:, :, :, 1], ALU.max))
                        c(nc.vector.tensor_tensor(pmn[:, :, :], v[:, :, :, 0], v[:, :, :, 1], ALU.min))
                        c(nc.vector.tensor_tensor(g1[:, :], pmx[:, :, 0], pmx[:, :, 1], ALU.max))
                        c(nc.vector.tensor_tensor(g2[:, :], pmx[:, :, 0], pmx[:, :, 1], ALU.min))
                        c(nc.vector.tensor_tensor(g3[:, :], pmn[:, :, 0], pmn[:, :, 1], ALU.max))
                        c(nc.vector.tensor_tensor(g2[:, :], g2[:, :], g3[:, :], ALU.max))
                        c(nc.vector.tensor_tensor(gsum[:, :], g1[:, :], g2[:, :], ALU.add))
                        gs = gsum[:, :].rearrange("p (t g) -> p t g", g=4)
                        mine, other = gs.unsqueeze(3).broadcast_to([P, NT, 4, 4]), gs.unsqueeze(2).broadcast_to([P, NT, 4, 4])
                        c(nc.vector.tensor_tensor(cmp4[:, :, :, :], other, mine, ALU.is_gt))
                        c(nc.vector.tensor_tensor(cmp4b[:, :, :, :], other, mine, ALU.is_equal))
                        c(nc.vector.tensor_tensor(cmp4b[:, :, :, :], cmp4b[:, :, :, :], lower4[:, :, :].unsqueeze(1).broadcast_to([P, NT, 4, 4]), ALU.mult))
                        c(nc.vector.tensor_tensor(cmp4[:, :, :, :], cmp4[:, :, :, :], cmp4b[:, :, :, :], ALU.add))
                        c(nc.vector.tensor_reduce(grank[:, :], cmp4[:, :, :, :].rearrange("p t g o -> p (t g) o"), AXX, ALU.add))
                        c(nc.vector.tensor_scalar(gsel[:, :], grank[:, :], 2.0, None, ALU.is_lt))
                        c(nc.vector.tensor_tensor(msk[:, :, :].rearrange("p t (g e) -> p (t g) e", e=4), scb[:, :, :].rearrange("p t (g e) -> p (t g) e", e=4),
                                                  gsel[:, :].unsqueeze(2).broadcast_to([P, 16, 4]), ALU.mult))

                    def top_experts(n, c):
                        mine, other = msk[:, :, :].unsqueeze(3).broadcast_to([P, NT, E, E]), msk[:, :, :].unsqueeze(2).broadcast_to([P, NT, E, E])
                        c(nc.vector.tensor_tensor(cmp16[:, :, :, :], other, mine, ALU.is_ge))
                        c(nc.vector.tensor_tensor(cmp16[:, :, :, :], cmp16[:, :, :, :], lower16[:, :, :].unsqueeze(1).broadcast_to([P, NT, E, E]), ALU.mult))
                        c(nc.vector.tensor_reduce(rrow[:, :, :], cmp16[:, :, :, :], AXX, ALU.add))
                        c(nc.vector.tensor_reduce(rcol[:, :, :], cmp16[:, :, :, :].rearrange("p t e o -> p t o e"), AXX, ALU.add))

                    def weights(n, c):
                        c(nc.vector.tensor_tensor(rrow[:, :, :], rrow[:, :, :], rcol[:, :, :], ALU.subtract))
                        c(nc.vector.tensor_tensor(rrow[:, :, :], rrow[:, :, :], rest15[:, :].unsqueeze(1).broadcast_to([P, NT, E]), ALU.add))
                        c(nc.vector.scalar_tensor_tensor(comb[:, :, :], rrow[:, :, :], 4.0, sg[:, :, :], ALU.is_lt, ALU.mult))
                        c(nc.vector.tensor_reduce(wsum[:, :], comb[:, :, :], AXX, ALU.add))
                        c(nc.vector.tensor_scalar(wsum[:, :], wsum[:, :], 1e-20, None, ALU.add))
                        c(nc.vector.reciprocal(wsum[:, :], wsum[:, :]))
                        c(nc.vector.tensor_scalar(wsum[:, :], wsum[:, :], 2.5, None, ALU.mult))
                        c(nc.vector.tensor_tensor(comb[:, :, :], comb[:, :, :], wsum[:, :].unsqueeze(2).broadcast_to([P, NT, E]), ALU.mult))
                        dve.wait_ge(s_cT, n)
                        nc.vector.tensor_copy(cpart[:, :, 0, :], comb[:, :, :]).then_inc(s_cb, 1)
                        dve.wait_ge(s_cb, n * 3 + 1)
                        c(nc.vector.tensor_tensor(crest[:, :, :], comb[:, :, :], cpart[:, :, 0, :], ALU.subtract))
                        nc.vector.tensor_copy(cpart[:, :, 1, :], crest[:, :, :]).then_inc(s_cb, 1)
                        dve.wait_ge(s_cb, n * 3 + 2)
                        nc.vector.tensor_tensor(cpart[:, :, 2, :], crest[:, :, :], cpart[:, :, 1, :], ALU.subtract).then_inc(s_cb, 1)

                    def combT(n, a):
                        dve.wait_ge(s_cT, n + 1)
                        nc.vector.tensor_copy(cT[a][:, :], pXb[0:3 * E, 0:CH]).then_inc(s_cTs, 1)

                    def chain(n):
                        return Chain(dve, s_route, n, 28)

                    def finish(n, a):
                        dve.wait_ge(s_dn, n * NE + NE)
                        for h in range(2):
                            nc.vector.tensor_tensor(ys[:, 2 * h:2 * h + 2, :], pA[h][:, :, :], h1[a][:, 2 * h:2 * h + 2, :], ALU.add).then_inc(s_y2, 1)

                    def finish_stats(n):
                        for t in range(NT):
                            dve.wait_ge(s_y2, n * 2 + t // 2 + 1)
                            nc.vector.bn_stats(st6b[:, t, :], ys[:, t, :]).then_inc(s_bn2, 1)
                        for t in range(NT):
                            wait_apart(dve, s_bn2, n * NT + t + 1, s_tick)
                            nc.vector.bn_aggr(mvb[:, t, :], st6b[:, t, :]).then_inc(s_mv2, 1)

                    def finish_out(n):
                        dve.wait_ge(s_rs2, n + 1)
                        dve.wait_ge(s_out, n * 16 + 16)
                        for t in range(NT):
                            nc.vector.tensor_scalar(yo[:, t, :], ys[:, t, :], mvb[:, t, 0:1], rsb[:, t:t + 1],
                                                    ALU.subtract, ALU.mult).then_inc(s_yo, 1)

                    nc.vector.memset(yo[:], 0.0).then_inc(s_out, 16)
                    for h in range(2):
                        ln_stats(0, h)
                        ln_apply(0, 0, h)
                    split(0, 0, 0)
                    split(0, 0, 1)
                    dve.wait_ge(s_cst, 10)
                    dve.wait_ge(s_wl2, 16)
                    c = chain(0)
                    top_groups(0, c)
                    top_experts(0, c)
                    weights(0, c)
                    c.close()
                    combT(0, 0)

                    def chunk(n, a, first=False, final=False):
                        c = chain(n + 1)
                        for e in range(NE):
                            q = n * NE + e
                            dve.wait_ge(s_silu, q + 1)
                            src = sl[e % 2]
                            if e < E:
                                dve.wait_ge(s_C, n * E + e + 1)
                                nc.vector.tensor_tensor(sc_[e % 2][:, :], sl[e % 2][:, :], pC[:, :], ALU.mult).then_inc(s_t1, 1)
                                dve.wait_ge(s_t1, n * E + e + 1)
                                src = sc_[e % 2]
                            dve.wait_ge(s_U, q + 1)
                            if not (first and e < 2):
                                dve.wait_ge(s_pl, q - 1)
                            nc.vector.tensor_tensor(prod[e % 2][:, :], src[:, :], pU[e % 2][:, :], ALU.mult).then_inc(s_prod, 1)
                            if not first:
                                if e == 1:
                                    finish(n - 1, 1 - a)
                                if e == 2:
                                    finish_stats(n - 1)
                                if e == 4:
                                    finish_out(n - 1)
                            if not final:
                                if e in (5, 7):
                                    ln_stats(n + 1, (e - 5) // 2)
                                if e in (6, 8):
                                    ln_apply(n + 1, 1 - a, (e - 6) // 2)
                                if e in (9, 10):
                                    split(n + 1, 1 - a, e - 9)
                                if e == 12:
                                    top_groups(n + 1, c)
                                if e == 13:
                                    top_experts(n + 1, c)
                                if e == 14:
                                    weights(n + 1, c)
                                    c.close()
                                if e == 16:
                                    combT(n + 1, 1 - a)
                    chunk(0, 0, first=True)
                    with dve.Fori(0, NCH // 2 - 1) as i:
                        chunk(i * 2 + 1, 1)
                        chunk(i * 2 + 2, 0)
                    chunk(NCH - 1, 1, final=True)
                    finish(NCH - 1, 1)
                    finish_stats(NCH - 1)
                    finish_out(NCH - 1)
                    linked(link)


def kernel(**inputs):
    import numpy as np
    import concourse.bacc as bacc
    from concourse.bass_utils import run_bass_kernel_spmd

    a = {k: np.asarray(v) for k, v in inputs.items()}
    gate, up, down = a["L0_ffn_gate_w"], a["L0_ffn_up_w"], a["L0_ffn_down_w"]
    gate = np.concatenate([gate, a["L0_ffn_sh_gate_w"].reshape(2, I, C)])
    up = np.concatenate([up, a["L0_ffn_sh_up_w"].reshape(2, I, C)])
    down = np.concatenate([down, a["L0_ffn_sh_down_w"].reshape(C, 2, I).transpose(1, 0, 2)])
    by_c = lambda w: np.ascontiguousarray(w.reshape(NE, I, KC, P).transpose(3, 2, 0, 1))
    arrays = {
        "x": np.ascontiguousarray(a["x"].reshape(B, 3, 2, P, C).transpose(0, 3, 1, 2, 4)),
        "scharr": a["L0_tok_scharr"],
        "qkv_w": a["L0_attn_qkv_w"], "qkv_b": a["L0_attn_qkv_b"],
        "qkv_b_col": np.ascontiguousarray(a["L0_attn_qkv_b"].reshape(6, P).T),
        "proj_w": a["L0_attn_proj_w"],
        "proj_b_col": np.ascontiguousarray(a["L0_attn_proj_b"].reshape(KC, P).T),
        "router_t": np.ascontiguousarray(a["L0_ffn_router_weight"].reshape(E, KC, P).transpose(2, 1, 0)),
        "e_bias": a["L0_ffn_e_bias"],
        "gate_t": by_c(gate), "up_t": by_c(up),
        "down_t": np.ascontiguousarray(down.transpose(2, 0, 1)),
    }
    nc = bacc.Bacc("TRN2", target_bir_lowering=False, num_devices=1)
    args = [nc.dram_tensor(n, v.shape, mybir.dt.from_np(v.dtype), kind="ExternalInput").ap() for n, v in arrays.items()]
    args.append(nc.dram_tensor("out", (B, 256, 256), F32, kind="ExternalOutput").ap())
    build(nc, *args)
    r = run_bass_kernel_spmd(nc, [arrays], core_ids=[0])
    return r.results[0]["out"]
```

```python
import concourse.bass as bass
from concourse import mybir
from contextlib import ExitStack

F32 = mybir.dt.float32
F32R = mybir.dt.float32r
BF16 = mybir.dt.bfloat16
ALU = mybir.AluOpType
ACT = mybir.ActivationFunctionType
AXX = mybir.AxisListType.X
RMAX = bass.bass_isa.ReduceOp.max

P = 128
B = 32
N = 256
C = 256
KC = C // P
T = B * N
H, D = 16, 16
G, J = 4, 4
E, I = 16, 128
NE = E + 2
CH = 512
NCH = T // CH
NT = CH // P
QMAX = 255.0
MAGIC = 12582912.0
GRAY = (0.2989 * 0.5, 0.587 * 0.5, 0.114 * 0.5)
LN_EPS = 1e-5
BW = 132


class Chain:

    def __init__(self, eng, sem, i=0, per=0, base=0):
        self.eng, self.sem, self.start, self.n, self.per = eng, sem, i * per + base, 0, per

    def __call__(self, ins):
        self.n += 1
        ins.then_inc(self.sem, 1)
        self.eng.wait_ge(self.sem, self.start + self.n)

    def close(self):
        assert self.n == self.per, (self.n, self.per)


def wait_apart(eng, sem, value, tick):
    eng.wait_ge(sem, value)
    eng.sem_inc(tick, 1)


def quant_scalars(dve, link, mx, mn, scale, inv, top, tmp):
    nc = dve.bass
    link(nc.vector.tensor_scalar(mx, mx, 0.0, None, ALU.max))
    link(nc.vector.tensor_scalar(mn, mn, 0.0, None, ALU.min))
    link(nc.vector.tensor_tensor(tmp, mx, mn, ALU.subtract))
    link(nc.vector.tensor_scalar(scale, tmp, 1.0 / QMAX, 1e-8, ALU.mult, ALU.max))
    link(nc.vector.reciprocal(inv, scale))
    link(nc.vector.tensor_tensor(tmp, mn, inv, ALU.mult))
    link(nc.vector.tensor_scalar(tmp, tmp, MAGIC, None, ALU.add))
    link(nc.vector.tensor_scalar(top, tmp, QMAX, None, ALU.add))


def build(nc, x, scharr, qkv_w, qkv_b, qkv_b_col, proj_w, proj_b_col, router_t, e_bias, gate_t, up_t, down_t, out):
    hs = nc.dram_tensor("edges_scratch", (P, KC, T), F32).ap()
    qk_s = nc.dram_tensor("qk_scratch", (4 * P, T), F32).ap()
    at_s = nc.dram_tensor("attn_scratch", (P, T // P, C), F32).ap()
    v_s = nc.dram_tensor("v_scratch", (T, C), F32).ap()

    with ExitStack() as whole:
        def sem(name):
            return whole.enter_context(nc.semaphore(name))

        def keep(name, shape, dt=F32):
            return whole.enter_context(nc.sbuf_tensor(name, shape, dt))

        link_sem = sem("dve_link")
        ident = keep("ident", [P, P])
        identb = keep("identb", [P, P], BF16)
        magic = keep("magic", [P, 1])
        pint = keep("proj_int_T", [P, KC, C], BF16)
        pscale = keep("proj_scale", [P, KC])
        pb = keep("proj_bias", [P, KC])
        omx = keep("attn_max", [P, B])
        omn = keep("attn_min", [P, B])
        mx = keep("qkv_max", [P, 3, NCH])
        mn = keep("qkv_min", [P, 3, NCH])
        s_tick = sem("waits_apart")
        links = [0]

        def linker(dve):
            c = Chain(dve, link_sem, base=links[0])
            return c

        def linked(c):
            links[0] += c.n

        with ExitStack() as ab:
            def sb(name, shape, dt=F32):
                return ab.enter_context(nc.sbuf_tensor(name, shape, dt))
            hT = sb("edges_T", [P, KC, T])
            cmax = sb("cmax", [P, KC, NCH])
            wdq = sb("wdq", [P, 6, C])
            qb = sb("qkv_bias", [P, 6])
            vb = sb("v_bias", [P, C])
            band = sb("band", [P, 3, 2, BW])

            with ExitStack() as st:
                def sb(name, shape, dt=F32):
                    return st.enter_context(nc.sbuf_tensor(name, shape, dt))
                taps = sb("taps", [P, 18])
                diag = sb("diag", [P, 3, BW])
                w_raw = sb("w_raw", [P, 8, C])
                w_y = sb("w_y", [P, 8, C])
                p_q = sb("p_q", [P, KC, C], BF16)
                wmx, wmn, wsc, winv, wtop, wtmp = (sb(n, [P, 8]) for n in ("wmx", "wmn", "wsc", "winv", "wtop", "wtmp"))
                pT = st.enter_context(nc.psum_tensor("pT", [P, KC, C], BF16))
                s_tap, s_w, s_zero, s_diag, s_pq, s_pt = (sem(n) for n in (
                    "taps_loaded", "weights_loaded", "setup_zeroed", "diag_ready", "pq_ready", "pt_ready"))
                s_ib, s_wq, s_wi, s_band = (sem(n) for n in ("identb_ready", "weight_scales", "weight_ints", "band_ready"))
                s_wd = sem("wdq_ready")
                xin = [sb(f"xin{a}", [P, 3, 2, C]) for a in range(2)]
                gt = [sb(f"gt{a}", [P, 2, C]) for a in range(2)]
                gray = [sb(f"gray{a}", [P, 2, C + 2]) for a in range(2)]
                gh, gl = ([sb(f"gray_{n}{a}", [P, 2, C + 2], F32R) for a in range(2)] for n in ("hi", "lo"))
                bh, bl = (sb(f"band_{n}", [P, 3, 2, BW], F32R) for n in ("hi", "lo"))
                s_gh, s_gl = ([sem(f"gray_{n}_ready{a}") for a in range(2)] for n in ("hi", "lo"))
                gx = [sb(f"gx{a}", [P, 2, N]) for a in range(4)]
                pc = [st.enter_context(nc.psum_tensor(f"pc{a}", [P, 2, N], F32)) for a in range(4)]
                s_x = [sem(f"x_loaded{a}") for a in range(2)]
                s_gt = [sem(f"gray_red_ready{a}") for a in range(2)]
                s_gray = [sem(f"gray_ready{a}") for a in range(2)]
                s_conv = [sem(f"conv_done{a}") for a in range(4)]
                s_gx = [sem(f"gx_ready{a}") for a in range(4)]
                s_h = [sem(f"edges_ready{a}") for a in range(4)]
                s_g1 = sem("gray_half")
                s_spill = sem("edges_spilled")
                s_cm = sem("cmax_part")
                HALF = B // 2

                with nc.Block() as block:
                    @block.sync
                    def _(sp):
                        def load(b, i, a):
                            sp.wait_ge(s_gray[a], i)
                            sp.dma_start(xin[a][:, :, :, :], x[b]).then_inc(s_x[a], 16)

                        def spill(i):
                            for k in range(4):
                                sp.wait_ge(s_h[k], i + 1)
                            sp.dma_start(hs[:, :, bass.ds(i * CH, CH)], hT[:, :, bass.ds(i * CH, CH)]).then_inc(s_spill, 16)
                        sp.dma_start(taps[:, :], scharr.rearrange("f o a b -> o (f a b)").broadcast_to([P, 18])).then_inc(s_tap, 16)
                        load(0, 0, 0)
                        load(1, 0, 1)
                        sp.dma_start(w_raw[:, 0:6, :], qkv_w.rearrange("(t p) c -> p t c", p=P)).then_inc(s_w, 16)
                        sp.dma_start(w_raw[:, 6:8, :], proj_w.rearrange("(t p) c -> p t c", p=P)).then_inc(s_w, 16)
                        sp.dma_start(qb[:, :], qkv_b_col).then_inc(s_w, 16)
                        sp.dma_start(pb[:, :], proj_b_col).then_inc(s_w, 16)
                        sp.dma_start(vb[:, :], qkv_b.rearrange("(o n) -> o n", o=1)[:, 2 * C:3 * C].broadcast_to([P, C])).then_inc(s_w, 16)

                        def turn(i):
                            load(i * 2 + 4, i + 2, 0)
                            load(i * 2 + 5, i + 2, 1)
                            spill(i)
                        load(2, 1, 0)
                        load(3, 1, 1)
                        turn(0)
                        with sp.Fori(1, HALF - 2) as i:
                            turn(i)
                        spill(HALF - 2)
                        spill(HALF - 1)
                        sp.wait_ge(s_spill, 16 * HALF)
                        sp.wait_ge(s_w, 80)

                    @block.gpsimd
                    def _(pool):
                        nc.gpsimd.memset(diag[:], 0.0).then_inc(s_zero, 1)
                        nc.gpsimd.memset(ident[:], 0.0).then_inc(s_zero, 1)
                        pool.wait_ge(s_zero, 2)
                        for dy in range(3):
                            nc.gpsimd.affine_select(out=diag[:, dy, :], in_=diag[:, dy, :], compare_op=ALU.not_equal,
                                                    fill=1.0, base=3 - dy, pattern=[[-1, BW]],
                                                    channel_multiplier=1).then_inc(s_diag, 1)
                        nc.gpsimd.affine_select(out=ident[:, :], in_=ident[:, :], compare_op=ALU.not_equal,
                                                fill=1.0, base=0, pattern=[[-1, P]],
                                                channel_multiplier=1).then_inc(s_diag, 1)

                        def low(i, a):
                            pool.wait_ge(s_gh[a], i + 1)
                            nc.gpsimd.tensor_tensor(gl[a][:, :, :], gray[a][:, :, :], gh[a][:, :, :].bitcast(F32), ALU.subtract).then_inc(s_gl[a], 1)

                        def weight(t):
                            pool.wait_ge(s_wq, 1)
                            nc.gpsimd.tensor_scalar(w_y[:, t, :], w_raw[:, t, :], winv[:, t:t + 1], MAGIC, ALU.mult, ALU.add).then_inc(s_wi, 1)
                            pool.wait_ge(s_wi, 2 * t + 1)
                            nc.gpsimd.tensor_scalar(w_y[:, t, :], w_y[:, t, :], wtop[:, t:t + 1], MAGIC, ALU.min, ALU.subtract).then_inc(s_wi, 1)
                            if t < 6:
                                pool.wait_ge(s_wi, 2 * t + 2)
                                nc.gpsimd.tensor_scalar(wdq[:, t, :], w_y[:, t, :], wsc[:, t:t + 1], 0.0, ALU.mult, ALU.add).then_inc(s_wd, 1)
                        for i in range(6):
                            for a in range(2):
                                low(i, a)
                                if i > 1:
                                    weight((i - 2) * 2 + a)
                        with pool.Fori(6, HALF) as i:
                            for a in range(2):
                                low(i, a)

                    @block.scalar
                    def _(act):
                        def red(i, a):
                            act.wait_ge(s_x[a], i * 16 + 16)
                            act.wait_ge(s_gray[a], i)
                            nc.scalar.activation(gt[a][:, :, :], xin[a][:, 0, :, :], ACT.Copy, scale=GRAY[0]).then_inc(s_gt[a], 1)

                        def absx(i, a):
                            for k in range(KC):
                                m = 2 * a + k
                                act.wait_ge(s_conv[m], i + 1)
                                act.wait_ge(s_h[m], i)
                                nc.scalar.activation(gx[m][:, :, :], pc[m][:, :, :], ACT.Abs).then_inc(s_gx[m], 1)
                        def high(i, a):
                            act.wait_ge(s_gray[a], i + 1)
                            act.wait_ge(s_conv[2 * a + 1], i)
                            nc.scalar.copy(gh[a][:, :, :], gray[a][:, :, :]).then_inc(s_gh[a], 1)
                        for a in range(2):
                            red(0, a)
                            high(0, a)

                        def turn(i):
                            for a in range(2):
                                red(i + 1, a)
                                high(i + 1, a)
                                absx(i, a)

                        turn(0)
                        with act.Fori(1, HALF - 1) as i:
                            turn(i)
                        absx(HALF - 1, 0)
                        absx(HALF - 1, 1)

                    @block.vector
                    def _(dve):
                        link = linker(dve)
                        for a in range(2):
                            link(nc.vector.memset(gray[a][:], 0.0))

                        def bands():
                            dve.wait_ge(s_diag, 4)
                            dve.wait_ge(s_tap, 16)
                            for m, op1 in ((0, None), (1, ALU.add), (2, ALU.add)):
                                for dx in range(3):
                                    for f in range(2):
                                        o = band[:, dx, f, :]
                                        k = 9 * f + dx + 3 * m
                                        if m:
                                            dve.wait_ge(s_band, 6 * m - 5 + dx * 2 + f)
                                            nc.vector.scalar_tensor_tensor(o, diag[:, m, :], taps[:, k:k + 1], o, ALU.mult, ALU.add).then_inc(s_band, 1)
                                        else:
                                            nc.vector.tensor_scalar(o, diag[:, m, :], taps[:, k:k + 1], None, ALU.mult).then_inc(s_band, 1)
                            dve.wait_ge(s_band, 18)
                            link(nc.vector.tensor_copy(bh[:, :, :, :], band[:, :, :, :]))
                            nc.vector.tensor_tensor(bl[:, :, :, :], band[:, :, :, :], bh[:, :, :, :].bitcast(F32), ALU.subtract).then_inc(s_band, 1)

                        def weights():
                            link(nc.vector.memset(magic[:], MAGIC))
                            nc.vector.tensor_copy(identb[:, :], ident[:, :]).then_inc(s_ib, 1)
                            dve.wait_ge(s_w, 80)
                            link(nc.vector.tensor_reduce(wmx[:, :], w_raw[:, :, :], AXX, ALU.max))
                            link(nc.vector.tensor_reduce(wmn[:, :], w_raw[:, :, :], AXX, ALU.min))
                            quant_scalars(dve, link, wmx[:, :], wmn[:, :], wsc[:, :], winv[:, :], wtop[:, :], wtmp[:, :])
                            nc.vector.tensor_copy(pscale[:, :], wsc[:, 6:8]).then_inc(s_wq, 1)

                        def grays(i, a):
                            dve.wait_ge(s_gt[a], i + 1)
                            dve.wait_ge(s_gl[a], i)
                            nc.vector.scalar_tensor_tensor(gray[a][:, :, 1:C + 1], xin[a][:, 1, :, :], GRAY[1], gt[a][:, :, :],
                                                           ALU.mult, ALU.add).then_inc(s_g1, 1)
                            dve.wait_ge(s_g1, i * 2 + a + 1)
                            nc.vector.scalar_tensor_tensor(gray[a][:, :, 1:C + 1], xin[a][:, 2, :, :], GRAY[2], gray[a][:, :, 1:C + 1],
                                                           ALU.mult, ALU.add).then_inc(s_gray[a], 1)

                        def edges(i, a):
                            for k in range(KC):
                                m = 2 * a + k
                                dve.wait_ge(s_gx[m], i + 1)
                                nc.vector.tensor_tensor(hT[:, k, bass.ds(i * CH + a * N, N)], gx[m][:, 0, :], gx[m][:, 1, :],
                                                        ALU.add).then_inc(s_h[m], 1)

                        def maxes(i):
                            for k in range(KC):
                                dve.wait_ge(s_h[k], i + 1)
                                dve.wait_ge(s_h[2 + k], i + 1)
                                nc.vector.reduce_max(cmax[:, k, bass.ds(i, 1)], hT[:, k, bass.ds(i * CH, CH)], AXX).then_inc(s_cm, 1)
                        bands()
                        for a in range(2):
                            grays(0, a)

                        def turn(i):
                            for a in range(2):
                                grays(i + 1, a)
                                edges(i, a)
                            maxes(i)

                        turn(0)
                        weights()
                        with dve.Fori(1, HALF - 1) as i:
                            turn(i)
                        dve.wait_ge(s_wi, 16)
                        for t in range(KC):
                            for k in range(KC):
                                o = p_q[:, t, k * P:(k + 1) * P].rearrange("p (g j d) -> p j g d", g=2, j=J)
                                i_ = w_y[:, 6 + t, k * P:(k + 1) * P].rearrange("p (j g d) -> p j g d", g=2, j=J)
                                nc.vector.tensor_copy(o, i_).then_inc(s_pq, 1)
                        edges(HALF - 1, 0)
                        edges(HALF - 1, 1)
                        maxes(HALF - 1)
                        dve.wait_ge(s_pt, 1)
                        link(nc.vector.tensor_copy(pint[:, :, :], pT[:, :, :]))
                        linked(link)

                    @block.tensor
                    def _(pe):
                        def conv(i, a):
                            pe.wait_ge(s_gl[a], i + 1)
                            for k in range(KC):
                                m = 2 * a + k
                                pe.wait_ge(s_h[m], i)
                                for t in range(2):
                                    for dx in range(3):
                                        for q, (x_, w_) in enumerate(((gh, bh), (gl, bh), (gh, bl))):
                                            last = nc.tensor.matmul(
                                                pc[m][:, :, 126 * t:126 * t + 130],
                                                x_[a][:, t, k * P + dx:k * P + dx + P],
                                                w_[:, dx, :, 2 - 2 * t:132 - 2 * t],
                                                start=(t == 0 and dx == 0 and q == 0), stop=(t == 1 and dx == 2 and q == 2),
                                                skip_group_check=True)
                                last.then_inc(s_conv[m], 1)
                        def turn(i):
                            conv(i, 0)
                            conv(i, 1)

                        pe.wait_ge(s_band, 19)
                        turn(0)
                        with pe.Fori(1, HALF) as i:
                            turn(i)
                        pe.wait_ge(s_ib, 1)
                        pe.wait_ge(s_pq, 4)
                        for k in range(KC):
                            for t in range(KC):
                                last = nc.tensor.transpose(pT[:, k, t * P:(t + 1) * P], p_q[:, t, k * P:(k + 1) * P], identb[:, :])
                        last.then_inc(s_pt, 1)

            with ExitStack() as st:
                def sb(name, shape, dt=F32):
                    return st.enter_context(nc.sbuf_tensor(name, shape, dt))
                cm, csc, cinv = (sb(n, [P, KC]) for n in ("cm", "cscale", "cinv"))
                wf = sb("wf", [P, KC, 6 * P])
                whi = sb("w_hi", [P, KC, 6 * P], F32R)
                wlo = sb("w_lo", [P, KC, 6 * P], F32R)
                xa = sb("xa", [P, KC, CH])
                xr = [sb(f"xr{a}", [P, KC, CH], F32R) for a in range(2)]
                qk = [sb(f"qk{a}", [P, 4, CH]) for a in range(2)]
                vt = [sb(f"vt{a}", [P, NT, C]) for a in range(2)]
                pq = [st.enter_context(nc.psum_tensor(f"pq{a}", [P, CH], F32)) for a in range(4)]
                pv = [st.enter_context(nc.psum_tensor(f"pv{a}", [P, 2, C], F32)) for a in range(4)]
                s_cs, s_wT, s_wf, s_wl = (sem(n) for n in ("cscale_ready", "wT_ready", "wf_ready", "w_split"))
                s_xa = sem("xa_ready")
                s_xr = sem("xr_ready")
                s_q = [sem(f"q_done{a}") for a in range(4)]
                s_v = [sem(f"v_done{a}") for a in range(4)]
                s_qk = sem("qk_ready")
                s_vt = sem("vt_ready")
                s_mm, s_mmv, s_vc = sem("qk_minmax"), sem("v_minmax"), sem("v_copied")
                s_qst = [sem(f"qk_stored{a}") for a in range(2)]
                s_vst = [sem(f"v_stored{a}") for a in range(2)]

                with nc.Block() as block:
                    @block.tensor
                    def _(pe):
                        for m in range(6):
                            for k in range(KC):
                                n = m * KC + k
                                last = nc.tensor.transpose(pq[n // 4][:, (n % 4) * P:(n % 4 + 1) * P],
                                                           wdq[:, m, k * P:(k + 1) * P], ident[:, :])
                        last.then_inc(s_wT, 1)
                        pe.wait_ge(s_wl, 2)

                        def chunk(i, a):
                            n = i * 2 + a
                            pe.wait_ge(s_xr, n + 1)
                            for m in range(4):
                                if not (isinstance(n, int) and n == 0):
                                    pe.wait_ge(s_qk, n * 4 + m - 3)
                                for k in range(KC):
                                    for w in (whi, wlo):
                                        last = nc.tensor.matmul(pq[m][:, :], w[:, k, m * P:(m + 1) * P], xr[a][:, k, :],
                                                                start=(k == 0 and w is whi), stop=(k == 1 and w is wlo))
                                last.then_inc(s_q[m], 1)
                            if not (isinstance(i, int) and i == 0):
                                pe.wait_ge(s_vc, i * 4 + 2 * a - 2)
                            for h in range(2):
                                for t in range(2):
                                    tt = 2 * h + t
                                    for k in range(KC):
                                        for w in (whi, wlo):
                                            last = nc.tensor.matmul(pv[2 * a + h][:, t, :], xr[a][:, k, tt * P:(tt + 1) * P],
                                                                    w[:, k, 4 * P:6 * P],
                                                                    start=(k == 0 and w is whi), stop=(k == 1 and w is wlo))
                                last.then_inc(s_v[2 * a + h], 1)
                        def turn(i):
                            chunk(i, 0)
                            chunk(i, 1)

                        turn(0)
                        with pe.Fori(1, NCH // 2) as i:
                            turn(i)

                    @block.scalar
                    def _(act):
                        act.wait_ge(s_wf, 12)
                        nc.scalar.copy(whi[:, :, :], wf[:, :, :]).then_inc(s_wl, 1)

                        def rounded(n):
                            act.wait_ge(s_xr, n)
                            for k in range(KC):
                                nc.scalar.activation(xa[:, k, :], hT[:, k, bass.ds(n * CH, CH)], ACT.Identity, bias=magic[:, 0:1],
                                                     scale=cinv[:, k:k + 1]).then_inc(s_xa, 1)

                        def chunk(i, a, more=True):
                            n = i * 2 + a
                            if more:
                                rounded(n + 1)
                            act.wait_ge(s_qst[a], i * 16)
                            if not (isinstance(i, int) and i == 0):
                                act.wait_ge(s_mm, n * 4 - 4)
                            for m in range(4):
                                act.wait_ge(s_q[m], n + 1)
                                nc.scalar.activation(qk[a][:, m, :], pq[m][:, :], ACT.Identity, bias=qb[:, m:m + 1]).then_inc(s_qk, 1)
                            act.wait_ge(s_vst[a], i * 16)
                            if not (isinstance(i, int) and i == 0):
                                act.wait_ge(s_mmv, n * 2 - 2)
                            for h in range(2):
                                act.wait_ge(s_v[2 * a + h], i + 1)
                                nc.scalar.copy(vt[a][:, 2 * h:2 * h + 2, :], pv[2 * a + h][:, :, :]).then_inc(s_vc, 1)
                        act.wait_ge(s_cs, 1)
                        rounded(0)
                        def turn(i):
                            chunk(i, 0)
                            chunk(i, 1)

                        turn(0)
                        with act.Fori(1, NCH // 2 - 1) as i:
                            turn(i)
                        chunk(NCH // 2 - 1, 0)
                        chunk(NCH // 2 - 1, 1, more=False)

                    @block.vector
                    def _(dve):
                        link = linker(dve)
                        link(nc.vector.reduce_max(cm[:, :], cmax[:, :, :], AXX))
                        link(nc.vector.tensor_scalar(csc[:, :], cm[:, :], 0.0, 1.0 / QMAX, ALU.max, ALU.mult))
                        link(nc.vector.tensor_scalar(csc[:, :], csc[:, :], 1e-8, None, ALU.max))
                        nc.vector.reciprocal(cinv[:, :], csc[:, :]).then_inc(s_cs, 1)
                        dve.wait_ge(s_wT, 1)
                        for m in range(6):
                            for k in range(KC):
                                n = m * KC + k
                                nc.vector.tensor_scalar(wf[:, k, m * P:(m + 1) * P], pq[n // 4][:, (n % 4) * P:(n % 4 + 1) * P],
                                                        csc[:, k:k + 1], None, ALU.mult).then_inc(s_wf, 1)
                        dve.wait_ge(s_wl, 1)
                        nc.vector.tensor_tensor(wlo[:, :, :], wf[:, :, :], whi[:, :, :].bitcast(F32), ALU.subtract).then_inc(s_wl, 1)

                        def extremes(to_mx, to_mn, src, sem_):
                            src = src.rearrange("p a b -> p (a b)")
                            nc.vector.tensor_reduce(to_mx, src, AXX, ALU.max).then_inc(sem_, 1)
                            nc.vector.tensor_reduce(to_mn, src, AXX, ALU.min).then_inc(sem_, 1)

                        def of_qk(i, a):
                            n = i * 2 + a
                            for q in range(2):
                                dve.wait_ge(s_qk, n * 4 + 2 * q + 2)
                                extremes(mx[:, q, bass.ds(n, 1)], mn[:, q, bass.ds(n, 1)], qk[a][:, 2 * q:2 * q + 2, :], s_mm)

                        def of_v(i, a):
                            n = i * 2 + a
                            dve.wait_ge(s_vt, n * 2 + 2)
                            extremes(mx[:, 2, bass.ds(n, 1)], mn[:, 2, bass.ds(n, 1)], vt[a][:, :, :], s_mmv)
                        of_qk(0, 0)

                        def turn(i):
                            of_qk(i, 1)
                            of_v(i, 0)
                            of_qk(i + 1, 0)
                            of_v(i, 1)

                        with dve.Fori(0, NCH // 2 - 1) as i:
                            turn(i)
                        of_qk(NCH // 2 - 1, 1)
                        of_v(NCH // 2 - 1, 0)
                        of_v(NCH // 2 - 1, 1)
                        linked(link)

                    @block.gpsimd
                    def _(pool):
                        def quant(i, a):
                            n = i * 2 + a
                            wait_apart(pool, s_xa, n * 2 + 2, s_tick)
                            wait_apart(pool, s_v[2 * a + 1], i, s_tick)
                            nc.gpsimd.tensor_scalar(xr[a][:, :, :], xa[:, :, :], MAGIC + QMAX, MAGIC, ALU.min, ALU.subtract).then_inc(s_xr, 1)

                        def bias(i, a):
                            for h in range(2):
                                pool.wait_ge(s_vc, i * 4 + 2 * a + h + 1)
                                nc.gpsimd.tensor_tensor(vt[a][:, 2 * h:2 * h + 2, :], vt[a][:, 2 * h:2 * h + 2, :],
                                                        vb[:, :].unsqueeze(1).broadcast_to([P, 2, C]), ALU.add).then_inc(s_vt, 1)
                        quant(0, 0)

                        def turn(i):
                            quant(i, 1)
                            bias(i, 0)
                            quant(i + 1, 0)
                            bias(i, 1)

                        turn(0)
                        with pool.Fori(1, NCH // 2 - 1) as i:
                            turn(i)
                        quant(NCH // 2 - 1, 1)
                        bias(NCH // 2 - 1, 0)
                        bias(NCH // 2 - 1, 1)

                    @block.sync
                    def _(sp):
                        def store(i, a):
                            n = i * 2 + a
                            sp.wait_ge(s_qk, n * 4 + 4)
                            sp.dma_start(qk_s.rearrange("(m p) t -> p m t", p=P)[:, :, bass.ds(n * CH, CH)], qk[a][:, :, :]).then_inc(s_qst[a], 16)
                            sp.wait_ge(s_vt, n * 2 + 2)
                            sp.dma_start(v_s.rearrange("(t p) c -> p t c", p=P)[:, bass.ds(n * NT, NT), :], vt[a][:, :, :]).then_inc(s_vst[a], 16)
                        def turn(i):
                            store(i, 0)
                            store(i, 1)

                        turn(0)
                        with sp.Fori(1, NCH // 2) as i:
                            turn(i)
                        for a in range(2):
                            sp.wait_ge(s_qst[a], 16 * (NCH // 2))
                            sp.wait_ge(s_vst[a], 16 * (NCH // 2))

        lows = (("gate", [P, KC, NE, I]), ("up", [P, KC, NE, I]), ("down", [P, NE, C]), ("router", [P, KC, E]))
        with ExitStack() as place:
            graw, uraw, draw, rraw = (place.enter_context(nc.sbuf_tensor(f"{n}_raw", shape, F32)) for n, shape in lows)
        glo, ulo, dlo, rlo = (keep(f"{n}_lo", shape, F32R) for n, shape in lows)
        ghi, uhi = (keep(n, [P, KC, NE, I], F32R) for n in ("gate_hi", "up_hi"))
        rhi = keep("router_hi", [P, KC, E], F32R)
        flat_ = lambda t: t.rearrange("p a e i -> p (a e i)") if len(t.shape) == 4 else t.rearrange("p a b -> p (a b)")
        whole_ = lambda t: t[:, :, :, :] if len(t.shape) == 4 else t[:, :, :]
        flat = lambda t: flat_(whole_(t))
        s_sl, s_hi2, s_lo2 = sem("ffn_staged"), sem("split_hi"), sem("split_lo")
        WF = KC * NE * I
        LP, HP = WF // 9, WF // 4
        with ExitStack() as at:
            def sb(name, shape, dt=F32):
                return at.enter_context(nc.sbuf_tensor(name, shape, dt))

            def ps(name, shape, dt=F32):
                return at.enter_context(nc.psum_tensor(name, shape, dt))
            ext = sb("qkv_ext", [P, 2, 3])
            exta = sb("qkv_ext_all", [P, 2, 3])
            qsc, qinv, qtop, qtmp = (sb(n, [P, 3]) for n in ("qkv_scale", "qkv_inv", "qkv_top", "qkv_tmp"))
            esc = sb("exp_scale", [P, 1])
            aug = sb("aug_rows", [P, 2, J])
            own = sb("own_rows", [P, 2, J])
            ownr = sb("own_any", [P, 2])
            qinvm = sb("q_inv_masked", [P, 2])
            raw = [sb(f"raw{r}", [P, 6, N]) for r in range(3)]
            ki = [sb(f"ki{r}", [P, 2, N], BF16) for r in range(3)]
            yq = sb("yq", [P, 2, 2, N])
            QK = [sb(f"QK{r}", [P, G, 1 + J, N], BF16) for r in range(3)]
            V = [sb(f"V{r}", [P, 2, H, 32]) for r in range(3)]
            qT = [sb(f"qT{r}", [P, G, N], BF16) for r in range(3)]
            nm = sb("neg_max", [P, 2, H])
            attn = [sb(f"attn{r}", [P, 2, C]) for r in range(3)]
            rem = sb("neg_max_rest", [P, 2, H])
            Tm = sb("neg_max_parts", [P, 2, G, P], BF16)
            pr_ = [sb(f"probs{a}", [P, J, 2, N]) for a in range(2)]
            ot = [sb(f"ot{a}", [P, 2, N]) for a in range(2)]
            rden = [sb(f"rden{a}", [P, 2 * 2 * J]) for a in range(2)]
            pS = [ps(f"pS{a}", [P, 2, N]) for a in range(2)]
            pST = [ps(f"pST{a}", [P, 2, 2, N]) for a in range(2)]
            pO = ps("pO", [P, 2, N])
            pM = ps("pM", [P, 512])
            zT = pM[:, :].bitcast(BF16).rearrange("p (g q) -> p g q", g=G)

            s_ext, s_all, s_qsc = (sem(n) for n in ("ext_ready", "ext_reduced", "qkv_scales"))
            s_ld = [sem(f"raw_loaded{r}") for r in range(3)]
            s_y, s_kv, s_ki, s_qq, s_vq = (sem(n) for n in ("q_rounded", "kv_rounded", "k_int", "q_int", "v_int"))
            LEAD = 5
            s_rows = [sem(f"k_rows_laid{r}") for r in range(3)]
            s_sc = [sem(f"QK_placed{r}") for r in range(3)]
            s_S, s_red, s_m, s_z, s_qT = (sem(n) for n in ("S_done", "S_reduced", "max_parts", "max_T", "qT_ready"))
            s_st, s_exp, s_pv, s_ot, s_r, s_norm, s_run = (sem(n) for n in (
                "ST_done", "exp_done", "PV_done", "ot_ready", "R_done", "norm_done", "run_done"))
            s_ast = [sem(f"attn_stored{r}") for r in range(3)]
            s_mc, s_nc = sem("max_chain"), sem("norm_chain")
            s_aug, s_pad = sem("aug_chain"), sem("V_padded")

            with nc.Block() as block:
                @block.sync
                def _(sp):
                    def load(n, r):
                        sp.dma_start(raw[r][:, 0:4, :], qk_s.rearrange("(m p) t -> p m t", p=P)[:, :, bass.ds(n * N, N)]).then_inc(s_ld[r], 16)
                        sp.dma_start(raw[r][:, 4:6, :], v_s.rearrange("(t p) c -> p t c", p=P)[:, bass.ds(n * 2, 2), :]).then_inc(s_ld[r], 16)

                    def place(n, r):
                        sp.wait_ge(s_ki, n + 1)
                        for j in range(J):
                            for gm in range(2):
                                p0 = 32 * j + D * gm
                                sp.dma_start(QK[r][p0:p0 + D, gm::2, 1 + j, :], ki[r][p0:p0 + D, :, :]).then_inc(s_sc[r], 16)
                    for n in range(3):
                        load(n, n)
                    for r in range(2):
                        sp.wait_ge(s_rows[r], 8)
                        place(r, r)
                    sp.wait_ge(s_rows[2], 8)

                    def step(n, r):
                        sp.wait_ge(s_vq, n + 1)
                        sp.wait_ge(s_ki, n + 1)
                        sp.wait_ge(s_qq, n * 2 + 2)
                        load(n + 3, r)
                        sp.wait_ge(s_st, n * 8)
                        place(n + 2, (r + 2) % 3)
                    step(0, 0)
                    step(1, 1)
                    def store(n, r):
                        sp.wait_ge(s_norm, n * 2 + 2)
                        sp.dma_start(at_s[:, bass.ds(n * 2, 2), :], attn[r][:, :, :]).then_inc(s_ast[r], 16)
                    sp.dma_start(flat(rraw), flat(router_t)).then_inc(s_sl, 16)
                    with sp.Fori(0, 9) as i:
                        for k, (raw_, w) in enumerate(((graw, gate_t), (uraw, up_t), (draw, down_t))):
                            step(i * 3 + 2 + k, (2 + k) % 3)
                            store(i * 3 + k, k)
                            sp.dma_start(flat(raw_)[:, bass.ds(i * LP, LP)], flat(w)[:, bass.ds(i * LP, LP)]).then_inc(s_sl, 16)
                    sp.wait_ge(s_st, 29 * 8)
                    place(31, 1)
                    for n in range(27, 32):
                        store(n, n % 3)
                    for r, uses in enumerate((11, 11, 10)):
                        sp.wait_ge(s_ast[r], uses * 16 + 16)

                @block.gpsimd
                def _(pool):
                    nc.gpsimd.memset(ext[:, :, :], 0.0).then_inc(s_aug, 1)
                    nc.gpsimd.memset(aug[:, :], 1.0).then_inc(s_aug, 1)
                    nc.gpsimd.memset(own[:, :, :], 1.0).then_inc(s_aug, 1)
                    pool.wait_ge(s_aug, 3)
                    for t, lo, hi, sign in ((aug, -D, D + 2, 1), (own, 0, D - 1, -1)):
                        nc.gpsimd.affine_select(out=t[:, :, :], in_=t[:, :, :], compare_op=ALU.is_ge, fill=0.0, base=lo,
                                                pattern=[[sign * D, 2], [-32, J]], channel_multiplier=1).then_inc(s_aug, 1)
                    pool.wait_ge(s_aug, 5)
                    for t, lo, hi, sign in ((aug, -D, D + 2, 1), (own, 0, D - 1, -1)):
                        nc.gpsimd.affine_select(out=t[:, :, :], in_=t[:, :, :], compare_op=ALU.is_ge, fill=0.0, base=hi,
                                                pattern=[[-sign * D, 2], [32, J]], channel_multiplier=-1).then_inc(s_aug, 1)
                    pool.wait_ge(s_ext, 1)
                    nc.gpsimd.partition_all_reduce(exta[:, :, :], ext[:, :, :], P, RMAX).then_inc(s_all, 1)
                    for r in range(3):
                        nc.gpsimd.memset(V[r][:, :, :, D:D + 1], 1.0).then_inc(s_pad, 1)
                        nc.gpsimd.memset(V[r][:, :, :, D + 1:32], 0.0).then_inc(s_pad, 1)
                    pool.wait_ge(s_pad, 6)
                    pool.wait_ge(s_qsc, 1)

                    def quant(n, r, after=None):
                        wait_apart(pool, s_kv, n * 2 + 1, s_tick)
                        nc.gpsimd.tensor_scalar(ki[r][:, :, :], raw[r][:, 2:4, :], qtop[:, 1:2], MAGIC,
                                                ALU.min, ALU.subtract).then_inc(s_ki, 1)
                        if after is not None:
                            wait_apart(pool, s_st, after * 8, s_tick)
                        for gm in range(2):
                            wait_apart(pool, s_y, n * 2 + 1 + gm, s_tick)
                            nc.gpsimd.tensor_scalar(QK[r][:, gm::2, 0, :], yq[:, gm, :, :], qtop[:, 0:1], MAGIC,
                                                    ALU.min, ALU.subtract).then_inc(s_qq, 1)
                        if after is not None:
                            wait_apart(pool, s_pv, after * 4, s_tick)
                        wait_apart(pool, s_kv, n * 2 + 2, s_tick)
                        nc.gpsimd.tensor_scalar(V[r][:, :, :, 0:D], raw[r][:, 4:6, :].rearrange("p t (h d) -> p t h d", d=D), qtop[:, 2:3], MAGIC,
                                                ALU.min, ALU.subtract).then_inc(s_vq, 1)

                    def step(n, r, u):
                        if not (isinstance(n, int) and n == 0):
                            pool.wait_ge(s_sc[(r + 2) % 3], (u + (r + 2) // 3) * 128)
                        quant(n + 2, (r + 2) % 3, n)
                    quant(0, 0)
                    quant(1, 1)
                    step(0, 0, 0)
                    with pool.Fori(0, 9) as i:
                        for k in range(3):
                            step(i * 3 + 1 + k, (1 + k) % 3, i + (1 + k) // 3)
                    step(28, 1, 9)
                    step(29, 2, 9)
                    pool.wait_ge(s_hi2, 1)
                    nc.gpsimd.tensor_tensor(flat(rlo), flat(rraw), flat(rhi).bitcast(F32), ALU.subtract).then_inc(s_lo2, 1)
                    for q in range(8):
                        w, lo, hi = ((graw, glo, ghi), (uraw, ulo, uhi))[q % 2]
                        c = q // 2 * HP
                        pool.wait_ge(s_hi2, q + 2)
                        nc.gpsimd.tensor_tensor(flat(lo)[:, c:c + HP], flat(w)[:, c:c + HP],
                                                flat(hi).bitcast(F32)[:, c:c + HP], ALU.subtract).then_inc(s_lo2, 1)

                @block.tensor
                def _(pe):
                    def S(n, r, u, c0, c1):
                        for c in range(c0, c1):
                            g, qt, h2 = c // 4, (c // 2) % 2, c % 2
                            if c == 0:
                                pe.wait_ge(s_sc[r], u * 128 + 128)
                                pe.wait_ge(s_qq, n * 2 + 2)
                            if not (isinstance(n, int) and n == 0 and c < 2):
                                pe.wait_ge(s_red, n * 16 + c - 1)
                            nc.tensor.matmul(pS[c % 2][:, :, :], QK[r][:, g, 0, qt * P:qt * P + P], QK[r][:, g, 1 + 2 * h2:3 + 2 * h2, :],
                                             start=True, stop=True).then_inc(s_S, 1)

                    def Z(n):
                        pe.wait_ge(s_m, n * 2 + 2)
                        if not (isinstance(n, int) and n <= 1):
                            pe.wait_ge(s_norm, n * 2 - 2)
                        for g in range(G):
                            for qt in range(2):
                                last = nc.tensor.transpose(zT[:, g, qt * P:qt * P + P], Tm[:, qt, g, :], identb[:, :])
                        last.then_inc(s_z, 1)

                    def ST(n, r, g, h2):
                        if g == 0 and h2 == 0:
                            pe.wait_ge(s_qT, n + 1)
                        if not (isinstance(n, int) and n == 0 and g == 0):
                            pe.wait_ge(s_exp, n * 8 + 2 * g + h2 - 1)
                        for j in range(2):
                            for kt in range(2):
                                last = nc.tensor.matmul(pST[h2][:, j, kt, :], QK[r][:, g, 1 + 2 * h2 + j, kt * P:kt * P + P],
                                                        qT[r][:, g, :], start=True, stop=True)
                        last.then_inc(s_st, 1)

                    def PV(n, r, g, kt):
                        if kt == 0:
                            if g == 0:
                                pe.wait_ge(s_vq, n + 1)
                            pe.wait_ge(s_exp, n * 8 + 2 * g + 2)
                            if g % 2 == 0:
                                pe.wait_ge(s_ot, n * 2 + g // 2)
                        for j in range(J):
                            last = nc.tensor.matmul(pO[32 * j:32 * j + 32, g % 2, :], V[r][:, kt, 8 * (g // 2) + 2 * j + g % 2, :],
                                                    pr_[g % 2][:, j, kt, :], start=(kt == 0), stop=(kt == 1))
                        if kt == 1:
                            last.then_inc(s_pv, 1)

                    def R(n, h):
                        pe.wait_ge(s_ot, n * 2 + h + 1)
                        if h:
                            pe.wait_ge(s_norm, n * 2 + 1)
                        else:
                            pe.wait_ge(s_qT, min(n + 2, B) if isinstance(n, int) else n + 2)
                        for qt in range(2):
                            for g in range(2):
                                c = (qt * 2 + g) * P
                                last = nc.tensor.transpose(pM[:, c:c + P], ot[h][:, g, qt * P:qt * P + P], ident[:, :])
                        last.then_inc(s_r, 1)

                    def image(n, r, u, first=False, left=2):
                        for slot in range(16):
                            g, s = slot // 4, slot % 4
                            c = slot + LEAD
                            if c < 16 and left >= 1:
                                S(n + 1, (r + 1) % 3, u + (r + 1) // 3, c, c + 1)
                            if c >= 16 and left >= 2:
                                S(n + 2, (r + 2) % 3, u + (r + 2) // 3, c - 16, c - 15)
                            if s % 2 == 0:
                                ST(n, r, g, s // 2)
                            elif g > 0:
                                PV(n, r, g - 1, s // 2)
                            elif not first:
                                PV(n - 1, (r + 2) % 3, 3, s // 2)
                            if slot == 1 and not first:
                                R(n - 1, 0)
                            if slot == 6 and not first:
                                R(n - 1, 1)
                            if slot == 13 and left >= 1:
                                Z(n + 1)
                    S(0, 0, 0, 0, 16)
                    Z(0)
                    S(1, 1, 0, 0, LEAD)
                    image(0, 0, 0, first=True)
                    with pe.Fori(0, 9) as i:
                        for k in range(3):
                            image(i * 3 + 1 + k, (1 + k) % 3, i + (1 + k) // 3)
                    for n in range(28, B):
                        image(n, n % 3, n // 3, left=B - 1 - n)
                    PV(31, 1, 3, 0)
                    PV(31, 1, 3, 1)
                    pe.wait_ge(s_norm, 62)
                    R(31, 0)
                    R(31, 1)

                @block.scalar
                def _(act):
                    def exps(n, g, first=False):
                        for h2 in range(2):
                            act.wait_ge(s_st, n * 8 + 2 * g + h2 + 1)
                            if not (first and g < 2):
                                act.wait_ge(s_pv, n * 4 + g - 1)
                            nc.scalar.activation(pr_[g % 2][:, 2 * h2:2 * h2 + 2, :, :], pST[h2][:, :, :, :], ACT.Exp,
                                                 scale=esc[:, 0:1]).then_inc(s_exp, 1)

                    def evac(n, h):
                        act.wait_ge(s_pv, n * 4 + 2 * h + 2)
                        if isinstance(n, int) and n == 0:
                            act.wait_ge(s_r, 1)
                        else:
                            act.wait_ge(s_r, n * 2 + h)
                        nc.scalar.copy(ot[h][:, :, :], pO[:, :, :]).then_inc(s_ot, 1)

                    def round_kv(n, r, u):
                        act.wait_ge(s_ld[r], u * 32 + 32)
                        for t in (1, 2):
                            nc.scalar.activation(raw[r][:, 2 * t:2 * t + 2, :], raw[r][:, 2 * t:2 * t + 2, :], ACT.Identity,
                                                 bias=magic[:, 0:1], scale=qinv[:, t:t + 1]).then_inc(s_kv, 1)

                    def round_q(n, r):
                        act.wait_ge(s_qq, n * 2)
                        for gm in range(2):
                            nc.scalar.activation(yq[:, gm, :, :], raw[r][:, 0:2, :], ACT.Identity,
                                                 bias=magic[:, 0:1], scale=qinvm[:, gm:gm + 1]).then_inc(s_y, 1)

                    def image(n, r, u, first=False, left=3):
                        exps(n, 0, first)
                        if not first:
                            evac(n - 1, 1)
                        exps(n, 1, first)
                        exps(n, 2)
                        evac(n, 0)
                        if left >= 3:
                            round_kv(n + 3, r, u + 1)
                            round_q(n + 3, r)
                        exps(n, 3)
                    act.wait_ge(s_aug, 7)
                    for j in range(J):
                        for gm in range(2):
                            nc.scalar.copy(QK[1][:, gm::2, 1 + j, :],
                                           aug[:, gm, j:j + 1].unsqueeze(2).broadcast_to([P, 2, N])).then_inc(s_rows[1], 1)
                    act.wait_ge(s_qsc, 1)
                    for r in range(3):
                        round_kv(r, r, 0)
                        round_q(r, r)
                    image(0, 0, 0, first=True)
                    with act.Fori(0, 9) as i:
                        for k in range(3):
                            image(i * 3 + 1 + k, (1 + k) % 3, i + (1 + k) // 3)
                    act.wait_ge(s_sl, 16 * 28)
                    nc.scalar.copy(flat(rhi), flat(rraw)).then_inc(s_hi2, 1)
                    for n in range(28, B):
                        image(n, n % 3, n // 3, left=B - 1 - n)
                        for w, hi in ((graw, ghi), (uraw, uhi)):
                            c = (n - 28) * HP
                            nc.scalar.copy(flat(hi)[:, c:c + HP], flat(w)[:, c:c + HP]).then_inc(s_hi2, 1)
                    evac(31, 1)

                @block.vector
                def _(dve):
                    link = linker(dve)
                    dve.wait_ge(s_aug, 1)
                    link(nc.vector.tensor_reduce(ext[:, 0, :], mx[:, :, :], AXX, ALU.max))
                    nc.vector.tensor_reduce(ext[:, 1, :], mn[:, :, :], AXX, ALU.min, negate=True).then_inc(s_ext, 1)
                    dve.wait_ge(s_aug, 7)
                    def k_rows(r):
                        for j in range(J):
                            for gm in range(2):
                                nc.vector.tensor_copy(QK[r][:, gm::2, 1 + j, :],
                                                      aug[:, gm, j:j + 1].unsqueeze(2).broadcast_to([P, 2, N])).then_inc(s_rows[r], 1)
                    k_rows(0)
                    dve.wait_ge(s_all, 1)
                    link(nc.vector.tensor_scalar(exta[:, 1, :], exta[:, 1, :], -1.0, None, ALU.mult))
                    quant_scalars(dve, link, exta[:, 0, :], exta[:, 1, :], qsc[:, :], qinv[:, :], qtop[:, :], qtmp[:, :])
                    link(nc.vector.reduce_max(ownr[:, :], own[:, :, :], AXX))
                    link(nc.vector.tensor_scalar(qinvm[:, :], ownr[:, :], qinv[:, 0:1], None, ALU.mult))
                    nc.vector.scalar_tensor_tensor(esc[:, :], qsc[:, 0:1], D ** -0.5, qsc[:, 1:2], ALU.mult, ALU.mult).then_inc(s_qsc, 1)
                    k_rows(2)
                    for r in range(3):
                        nc.vector.memset(attn[r][:, 0, 0:1], 0.0).then_inc(s_ast[r], 16)
                    nc.vector.memset(ot[1][:, 0, 0:1], 0.0).then_inc(s_r, 1)
                    link(nc.vector.memset(Tm[:], 0.0))

                    def reduce(n, c0, c1):
                        for c in range(c0, c1):
                            g, qt, h2 = c // 4, (c // 2) % 2, c % 2
                            dve.wait_ge(s_S, n * 16 + c + 1)
                            if c == 0 and not (isinstance(n, int) and n == 0):
                                dve.wait_ge(s_mc, (n - 1) * 6 + 4)
                            nc.vector.tensor_reduce(nm[:, qt, 4 * g + 2 * h2:4 * g + 2 * h2 + 2], pS[c % 2][:, :, :], AXX, ALU.max,
                                                    negate=True).then_inc(s_red, 1)

                    def parts(n, second):
                        if not second:
                            dve.wait_ge(s_red, n * 16 + 16)
                            if not (isinstance(n, int) and n == 0):
                                dve.wait_ge(s_z, n)
                        src = nm[:, :, :].rearrange("p q (m s j) -> p (q m) s j", s=2, j=J)
                        rst = rem[:, :, :].rearrange("p q (m s j) -> p (q m) s j", s=2, j=J)
                        to = [Tm[:, :, gm::2, :].rearrange("p q m (j e) -> p (q m) j e", e=32)[:, :, :, D * (1 - gm):D * (1 - gm) + 3]
                              for gm in range(2)]
                        if not second:
                            for gm in range(2):
                                nc.vector.tensor_copy(to[gm][:, :, :, 0], src[:, :, gm, :]).then_inc(s_mc, 1)
                            for gm in range(2):
                                dve.wait_ge(s_mc, n * 6 + 1 + gm)
                                nc.vector.tensor_tensor(rst[:, :, gm, :], src[:, :, gm, :], to[gm][:, :, :, 0], ALU.subtract).then_inc(s_mc, 1)
                            return
                        for gm in range(2):
                            dve.wait_ge(s_mc, n * 6 + 3 + gm)
                            nc.vector.tensor_copy(to[gm][:, :, :, 1], rst[:, :, gm, :]).then_inc(s_mc, 1)
                        for gm in range(2):
                            dve.wait_ge(s_mc, n * 6 + 5 + gm)
                            nc.vector.tensor_tensor(to[gm][:, :, :, 2], rst[:, :, gm, :], to[gm][:, :, :, 1], ALU.subtract).then_inc(s_m, 1)

                    def addq(n, r):
                        dve.wait_ge(s_z, n + 1)
                        nc.vector.tensor_tensor(qT[r][:, :, :], zT[:, :, :], QK[r][:, :, 0, :], ALU.add).then_inc(s_qT, 1)

                    src = pM[:, :].rearrange("p (u e) -> p u e", e=32)

                    def norm_scale(n, h):
                        dve.wait_ge(s_r, n * 2 + h + 2)
                        nc.vector.reciprocal(rden[h][:, :], src[:, :, D]).then_inc(s_nc, 1)
                        dve.wait_ge(s_nc, n * 4 + 2 * h + 1)
                        nc.vector.tensor_scalar(rden[h][:, :], rden[h][:, :], qsc[:, 2:3], None, ALU.mult).then_inc(s_nc, 1)

                    def norm(n, h, r, u):
                        dve.wait_ge(s_nc, n * 4 + 2 * h + 2)
                        dve.wait_ge(s_ast[r], u * 16 + 16)
                        out_ = attn[r][:, :, P * h:P * h + P].rearrange("p t (u d) -> p t u d", d=D)
                        nc.vector.tensor_tensor(out_, src[:, :, 0:D].rearrange("p (t u) d -> p t u d", t=2),
                                                rden[h][:, :].rearrange("p (t u) -> p t u", t=2).unsqueeze(3).broadcast_to([P, 2, 8, D]),
                                                ALU.mult).then_inc(s_norm, 1)

                    def extreme(n, r, to, op):
                        dve.wait_ge(s_norm, n * 2 + 2)
                        nc.vector.tensor_reduce(to[:, bass.ds(n, 1)], attn[r][:, :, :].rearrange("p a b -> p (a b)"), AXX, op)

                    def image(n, r, u, first=False, left=2):
                        m, mr, mu = n - 1, (r + 2) % 3, u + (r + 2) // 3 - 1
                        for slot in range(16):
                            c = slot + LEAD
                            if c < 16 and left >= 1:
                                reduce(n + 1, c, c + 1)
                            if c >= 16 and left >= 2:
                                reduce(n + 2, c - 16, c - 15)
                            if not first:
                                if slot == 2:
                                    norm_scale(m, 0)
                                if slot == 3:
                                    norm(m, 0, mr, mu)
                                if slot == 7:
                                    norm_scale(m, 1)
                                if slot == 8:
                                    norm(m, 1, mr, mu)
                                if slot == 9:
                                    extreme(m, mr, omx, ALU.max)
                                if slot == 12:
                                    extreme(m, mr, omn, ALU.min)
                            if left >= 1:
                                if slot == 15 - LEAD:
                                    parts(n + 1, False)
                                if slot == 16 - LEAD:
                                    parts(n + 1, True)
                                if slot == 13:
                                    addq(n + 1, (r + 1) % 3)
                    reduce(0, 0, 16)
                    parts(0, False)
                    parts(0, True)
                    addq(0, 0)
                    reduce(1, 0, LEAD)
                    image(0, 0, 0, first=True)
                    with dve.Fori(0, 9) as i:
                        for k in range(3):
                            image(i * 3 + 1 + k, (1 + k) % 3, i + (1 + k) // 3)
                    for n in range(28, B):
                        image(n, n % 3, n // 3, left=B - 1 - n)
                    for h in range(2):
                        norm_scale(31, h)
                        norm(31, h, 1, 10)
                    extreme(31, 1, omx, ALU.max)
                    extreme(31, 1, omn, ALU.min)
                    linked(link)

        with ExitStack() as ff:
            def sb(name, shape, dt=F32):
                return ff.enter_context(nc.sbuf_tensor(name, shape, dt))

            def ps(name, shape, dt=F32):
                return ff.enter_context(nc.psum_tensor(name, shape, dt))
            dhi = sb("down_hi", [P, NE, C], F32R)
            s_dhi, s_dlo = sem("down_hi_ready"), sem("down_lo_ready")
            eb = sb("e_bias_all", [P, E])
            oext, oexta = sb("attn_ext", [P, 2]), sb("attn_ext_all", [P, 2])
            osc, oinv, otop, otmp = (sb(n, [P, 1]) for n in ("attn_scale", "attn_inv", "attn_top", "attn_tmp"))
            psc = sb("proj_scale_all", [P, KC])
            pick = sb("pick", [3 * E, E, P], BF16)
            lower4, lower16 = sb("lower4", [P, 4, 4]), sb("lower16", [P, E, E])
            rest15 = sb("rest15", [P, E])
            ac = [sb(f"attn_chunk{a}", [P, NT, C]) for a in range(2)]
            hc = [sb(f"edge_chunk{a}", [P, KC, CH]) for a in range(2)]
            oq = sb("attn_int", [P, NT, C], BF16)
            oqT = sb("attn_int_T", [P, KC, CH], BF16)
            x1T = sb("x1_T", [P, KC, CH])
            h1 = [sb(f"h1_{a}", [P, NT, C]) for a in range(2)]
            xh = [sb(f"h1T_hi{a}", [P, KC, CH], F32R) for a in range(2)]
            xl = [sb(f"h1T_lo{a}", [P, KC, CH], F32R) for a in range(2)]
            st6, mv, rs = sb("ln_stats", [P, NT, 6]), sb("ln_mv", [P, NT, 2]), sb("ln_rstd", [P, NT])
            st6b, mvb, rsb = sb("ln2_stats", [P, NT, 6]), sb("ln2_mv", [P, NT, 2]), sb("ln2_rstd", [P, NT])
            sg, scb, msk = (sb(n, [P, NT, E]) for n in ("scores", "scores_biased", "scores_masked"))
            pmx, pmn = sb("pair_max", [P, 16, 2]), sb("pair_min", [P, 16, 2])
            g1, g2, g3, gsum, grank, gsel = (sb(n, [P, NT * 4]) for n in ("g1", "g2", "g3", "gsum", "grank", "gsel"))
            cmp4, cmp4b = sb("cmp4", [P, NT, 4, 4]), sb("cmp4b", [P, NT, 4, 4])
            cmp16 = sb("cmp16", [P, NT, E, E])
            rrow, rcol, comb = (sb(n, [P, NT, E]) for n in ("rank_row", "rank_col", "combine"))
            wsum = sb("weight_sum", [P, NT])
            mhalf = sb("minus_half", [P, NT])
            cpart = sb("combine_parts", [P, NT, 3, E], BF16)
            crest = sb("combine_rest", [P, NT, E])
            cT = [sb(f"combine_T{a}", [3 * E, CH], BF16) for a in range(2)]
            sl = [sb(f"silu{a}", [P, CH]) for a in range(2)]
            sc_ = [sb(f"silu_combined{a}", [P, CH]) for a in range(2)]
            prod = [sb(f"prod{a}", [P, CH]) for a in range(2)]
            ph = [sb(f"prod_hi{a}", [P, CH], F32R) for a in range(3)]
            pl = [sb(f"prod_lo{a}", [P, CH], F32R) for a in range(3)]
            ys = sb("y", [P, NT, C])
            yo = sb("y_out", [P, NT, C])
            pG = [ps(f"pG{a}", [P, CH]) for a in range(2)]
            pU = [ps(f"pU{a}", [P, CH]) for a in range(2)]
            pC = ps("pC", [P, CH])
            pA = [ps(f"pA{a}", [P, 2, C]) for a in range(2)]
            pX = ps("pX", [P, CH])
            pXb = pX[:, :].bitcast(BF16)

            s_wl2, s_ext2, s_all2, s_osc, s_cst = (sem(n) for n in (
                "ffn_loaded", "attn_ext_ready", "attn_ext_reduced", "attn_scales", "ffn_consts"))
            s_cl = [sem(f"chunk_loaded{a}") for a in range(2)]
            (s_oy, s_oq, s_oT, s_oTs, s_pj, s_pja, s_x1, s_xn, s_mv, s_rs, s_h1, s_hT, s_spl) = (sem(n) for n in (
                "attn_rounded", "attn_int_ready", "attn_T_done", "attn_T_ready", "proj_done", "proj_scaled", "x1_ready",
                "x1_transposed", "ln_mv_ready", "ln_rstd_ready", "h1_ready", "h1_transposed", "h1T_split"))
            (s_rt, s_sig, s_cb, s_cT, s_cTs, s_route) = (sem(n) for n in (
                "router_done", "scores_ready", "combine_ready", "combine_T_done", "combine_T_ready", "route_chain"))
            (s_G, s_U, s_C, s_silu, s_t1, s_prod, s_dn, s_y2, s_mv2, s_rs2, s_yo, s_out, s_bn, s_bn2) = (sem(n) for n in (
                "gate_done", "up_done", "spread_done", "silu_ready", "silu_combined", "prod_ready", "down_done", "y_ready",
                "ln2_mv_ready", "ln2_rstd_ready", "out_ready", "out_stored", "ln_chain", "ln2_chain"))
            s_ph, s_pl = sem("prod_hi_ready"), sem("prod_lo_ready")
            s_pw, s_pw2 = sem("power_chain"), sem("power2_chain")

            with nc.Block() as block:
                @block.sync
                def _(sp):
                    sp.dma_start(eb[:, :], e_bias.rearrange("(o n) -> o n", o=1).broadcast_to([P, E])).then_inc(s_wl2, 16)

                    def load(n, a):
                        sp.dma_start(ac[a][:, :, :], at_s[:, bass.ds(n * NT, NT), :]).then_inc(s_cl[a], 16)
                        sp.dma_start(hc[a][:, :, :], hs[:, :, bass.ds(n * CH, CH)]).then_inc(s_cl[a], 16)

                    load(0, 0)
                    load(1, 1)

                    def reload(n, a):
                        sp.wait_ge(s_x1, n * 2 - 2)
                        load(n, a)

                    def store(n):
                        sp.wait_ge(s_yo, n * NT + NT)
                        sp.dma_start(out.rearrange("b (t p) c -> p (b t) c", p=P)[:, bass.ds(n * NT, NT), :], yo[:, :, :]).then_inc(s_out, 16)
                    reload(2, 0)
                    reload(3, 1)
                    with sp.Fori(0, 6) as i:
                        for a in range(2):
                            store(i * 2 + a)
                            reload(i * 2 + 4 + a, a)
                    for n in range(12, NCH):
                        store(n)
                    sp.wait_ge(s_out, 16 * NCH + 16)

                @block.gpsimd
                def _(pool):
                    pool.wait_ge(s_ext2, 2)
                    nc.gpsimd.partition_all_reduce(oexta[:, :], oext[:, :], P, RMAX).then_inc(s_all2, 1)
                    nc.gpsimd.memset(lower4[:, :, :], 1.0).then_inc(s_cst, 1)
                    nc.gpsimd.memset(lower16[:, :, :], 1.0).then_inc(s_cst, 1)
                    nc.gpsimd.iota(rest15[:, :], pattern=[[-1, E]], base=15, channel_multiplier=0,
                                   allow_small_or_imprecise_dtypes=True).then_inc(s_cst, 1)
                    nc.gpsimd.memset(mhalf[:, :], -0.5).then_inc(s_cst, 1)
                    pool.wait_ge(s_cst, 4)
                    for t, w in ((lower4, 4), (lower16, E)):
                        nc.gpsimd.affine_select(out=t[:, :, :], in_=t[:, :, :], compare_op=ALU.is_ge, fill=0.0, base=-1,
                                                pattern=[[1, w], [-1, w]], channel_multiplier=0).then_inc(s_cst, 1)

                    def pick_part(k):
                        pool.wait_ge(s_cst, 7 + k)
                        nc.gpsimd.affine_select(out=pick[:, :, :], in_=pick[:, :, :], compare_op=ALU.not_equal, fill=1.0, base=-E * k,
                                                pattern=[[-1, E], [0, P]], channel_multiplier=1).then_inc(s_cst, 1)
                    pool.wait_ge(s_osc, 1)

                    def quant(n, a, u):
                        wait_apart(pool, s_cl[a], u * 32 + 32, s_tick)
                        nc.gpsimd.tensor_scalar(ac[a][:, :, :], ac[a][:, :, :], oinv[:, 0:1], MAGIC, ALU.mult, ALU.add).then_inc(s_oy, 1)
                        wait_apart(pool, s_oy, n + 1, s_tick)
                        wait_apart(pool, s_oT, n, s_tick)
                        nc.gpsimd.tensor_scalar(oq[:, :, :], ac[a][:, :, :], otop[:, 0:1], MAGIC, ALU.min, ALU.subtract).then_inc(s_oq, 1)

                    def residual(n, a, k):
                        pool.wait_ge(s_pja, n * 2 + k + 1)
                        nc.gpsimd.tensor_tensor(x1T[:, k, :], x1T[:, k, :], hc[a][:, k, :], ALU.add).then_inc(s_x1, 1)

                    def low(n, e, start=False):
                        q = n * NE + e
                        if not (start and e < 3):
                            pool.wait_ge(s_dn, q - 2)
                        pool.wait_ge(s_ph, q + 1)
                        nc.gpsimd.tensor_tensor(pl[e % 3][:, :], prod[e % 2][:, :], ph[e % 3][:, :].bitcast(F32), ALU.subtract).then_inc(s_pl, 1)

                    def power(o, var, n, s_, chain):
                        nc.gpsimd.tensor_scalar(o, var, LN_EPS, None, ALU.add).then_inc(chain, 1)
                        pool.wait_ge(chain, n + 1)
                        nc.gpsimd.tensor_tensor(o, o, mhalf[:, 0:o.shape[1]], ALU.pow).then_inc(s_, 1)

                    def rstd(n, h):
                        wait_apart(pool, s_mv, n * NT + 2 * h + 2, s_tick)
                        power(rs[:, 2 * h:2 * h + 2], mv[:, 2 * h:2 * h + 2, 1], n * 2 + h, s_rs, s_pw)

                    def rstd2(n):
                        wait_apart(pool, s_mv2, n * NT + NT, s_tick)
                        power(rsb[:, :], mvb[:, :, 1], n, s_rs2, s_pw2)

                    quant(0, 0, 0)
                    nc.gpsimd.memset(pick[:, :, :], 0.0).then_inc(s_cst, 1)
                    residual(0, 0, 0)
                    residual(0, 0, 1)
                    rstd(0, 0)
                    rstd(0, 1)
                    for k in range(3):
                        pick_part(k)
                    quant(1, 1, 0)

                    def chunk(n, a, u, first=False, left=2):
                        for e in range(NE):
                            if e > 0:
                                low(n, e - 1, first)
                            elif not first:
                                low(n - 1, NE - 1)
                            if e == 3 and not first:
                                rstd2(n - 1)
                            if left >= 1:
                                if e in (3, 4):
                                    residual(n + 1, 1 - a, e - 3)
                                if e in (6, 8):
                                    rstd(n + 1, (e - 6) // 2)
                            if left >= 2 and e == 11:
                                quant(n + 2, a, u + 1)
                    chunk(0, 0, 0, first=True)
                    with pool.Fori(0, 6) as i:
                        chunk(i * 2 + 1, 1, i)
                        chunk(i * 2 + 2, 0, i + 1)
                    chunk(13, 1, 6)
                    chunk(14, 0, 7, left=1)
                    chunk(15, 1, 7, left=0)
                    low(15, NE - 1)
                    rstd2(15)

                @block.scalar
                def _(act):
                    def evacT(n):
                        act.wait_ge(s_oT, n + 1)
                        act.wait_ge(s_pj, n * 2)
                        nc.scalar.copy(oqT[:, :, :], pXb.rearrange("p (k t) -> p k t", k=KC)).then_inc(s_oTs, 1)

                    def scale(n, k):
                        act.wait_ge(s_pj, n * 2 + k + 1)
                        act.wait_ge(s_xn, n * 2)
                        nc.scalar.activation(x1T[:, k, :], pX[:, :], ACT.Identity, bias=pb[:, k:k + 1], scale=psc[:, k:k + 1]).then_inc(s_pja, 1)

                    def score(n):
                        act.wait_ge(s_rt, n + 1)
                        act.wait_ge(s_cb, n * 3)
                        nc.scalar.activation(sg[:, :, :], pX[:, 0:NT * E].rearrange("p (t e) -> p t e", e=E), ACT.Sigmoid).then_inc(s_sig, 1)

                    nc.scalar.copy(flat(dhi), flat(draw)).then_inc(s_dhi, 1)
                    act.wait_ge(s_osc, 1)
                    evacT(0)
                    scale(0, 0)
                    scale(0, 1)
                    score(0)

                    def high(n, e, start=False):
                        q = n * NE + e
                        if not (start and e < 3):
                            act.wait_ge(s_dn, q - 2)
                        act.wait_ge(s_prod, q + 1)
                        nc.scalar.copy(ph[e % 3][:, :], prod[e % 2][:, :]).then_inc(s_ph, 1)

                    def chunk(n, first=False, final=False):
                        for e in range(NE):
                            if not final:
                                if e == 1:
                                    evacT(n + 1)
                                if e in (2, 3):
                                    scale(n + 1, e - 2)
                                if e == 12:
                                    score(n + 1)
                            act.wait_ge(s_G, n * NE + e + 1)
                            if not (first and e < 2):
                                act.wait_ge(s_prod, n * NE + e - 1)
                            nc.scalar.activation(sl[e % 2][:, :], pG[e % 2][:, :], ACT.Silu).then_inc(s_silu, 1)
                            if e > 0:
                                high(n, e - 1, first)
                            elif not first:
                                high(n - 1, NE - 1)
                    chunk(0, first=True)
                    with act.Fori(0, NCH - 2) as i:
                        chunk(i + 1)
                    chunk(NCH - 1, final=True)
                    high(NCH - 1, NE - 1)

                @block.tensor
                def _(pe):
                    def oT(n):
                        pe.wait_ge(s_oq, n + 1)
                        pe.wait_ge(s_cTs, n)
                        for k in range(KC):
                            for t in range(NT):
                                last = nc.tensor.transpose(pXb[:, k * CH + t * P:k * CH + t * P + P], oq[:, t, k * P:k * P + P], identb[:, :])
                        last.then_inc(s_oT, 1)

                    def proj(n, m):
                        pe.wait_ge(s_oTs, n + 1)
                        pe.wait_ge(s_pja, n * 2 + m)
                        for k in range(KC):
                            last = nc.tensor.matmul(pX[:, :], pint[:, k, m * P:m * P + P], oqT[:, k, :], start=(k == 0), stop=(k == 1))
                        last.then_inc(s_pj, 1)

                    def xn(n, h):
                        pe.wait_ge(s_x1, n * 2 + 2)
                        pe.wait_ge(s_h1, n * NT + 2 * h)
                        for t in range(2):
                            for k in range(KC):
                                c = t * C + k * P
                                tt = (2 * h + t) * P
                                last = nc.tensor.transpose(pX[:, c:c + P], x1T[:, k, tt:tt + P], ident[:, :])
                        last.then_inc(s_xn, 1)

                    def hT_(n, a, k):
                        pe.wait_ge(s_h1, n * NT + NT)
                        pe.wait_ge(s_spl, n * 4 + 2 * k)
                        for t in range(NT):
                            last = nc.tensor.transpose(pX[:, t * P:t * P + P], h1[a][:, t, k * P:k * P + P], ident[:, :])
                        last.then_inc(s_hT, 1)

                    def route(n, a):
                        pe.wait_ge(s_spl, n * 4 + 4)
                        for t in range(NT):
                            m = 0
                            for k in range(KC):
                                for x_, w_ in ((xh, rhi), (xh, rlo), (xl, rhi)):
                                    last = nc.tensor.matmul(pX[:, t * E:t * E + E], x_[a][:, k, t * P:t * P + P], w_[:, k, :],
                                                            start=(m == 0), stop=(m == 5))
                                    m += 1
                        last.then_inc(s_rt, 1)

                    def combT(n):
                        wait_apart(pe, s_cb, n * 3 + 3, s_tick)
                        for t in range(NT):
                            last = nc.tensor.transpose(pXb[0:3 * E, t * P:t * P + P], cpart[:, t, :, :].rearrange("p a e -> p (a e)"), identb[:, :])
                        last.then_inc(s_cT, 1)

                    def down(n, e):
                        q = n * NE + e
                        if isinstance(n, int) and n == 0 and e == 0:
                            pe.wait_ge(s_dlo, 1)
                        pe.wait_ge(s_pl, q + 1)
                        if e == 0:
                            pe.wait_ge(s_y2, n * 2)
                        for t in range(NT):
                            for m, (x_, w_) in enumerate(((ph, dhi), (ph, dlo), (pl, dhi))):
                                last = nc.tensor.matmul(pA[t // 2][:, t % 2, :], x_[e % 3][:, t * P:t * P + P], w_[:, e, :],
                                                        start=(e == 0 and t % 2 == 0 and m == 0), stop=(e == NE - 1 and m == 2),
                                                        skip_group_check=True)
                        last.then_inc(s_dn, 1)

                    def chunk(n, a, first=False, final=False):
                        for e in range(NE):
                            q = n * NE + e
                            if not (first and e < 2):
                                pe.wait_ge(s_silu, q - 1)
                                pe.wait_ge(s_prod, q - 1)
                            for w, po, s_ in (((ghi, glo), pG, s_G), ((uhi, ulo), pU, s_U)):
                                m = 0
                                for k in range(KC):
                                    for x_, w_ in ((xh, w[0]), (xl, w[0]), (xh, w[1])):
                                        last = nc.tensor.matmul(po[e % 2][:, :], w_[:, k, e, :], x_[a][:, k, :], start=(m == 0), stop=(m == 5))
                                        m += 1
                                last.then_inc(s_, 1)
                            if first and e == 0:
                                combT(0)
                            if e == 0:
                                pe.wait_ge(s_cTs, n + 1)
                            if e < E:
                                pe.wait_ge(s_t1, n * E + e)
                                nc.tensor.matmul(pC[:, :], pick[:, e, :], cT[a][:, :], start=True, stop=True).then_inc(s_C, 1)
                            if e > 1:
                                down(n, e - 2)
                            elif not first:
                                down(n - 1, NE - 2 + e)
                            if not final:
                                if e == 0:
                                    oT(n + 1)
                                if e in (1, 2):
                                    proj(n + 1, e - 1)
                                if e in (5, 7):
                                    xn(n + 1, (e - 5) // 2)
                                if e in (9, 10):
                                    hT_(n + 1, 1 - a, e - 9)
                                if e == 11:
                                    route(n + 1, 1 - a)
                                if e == 16:
                                    combT(n + 1)
                    oT(0)
                    proj(0, 0)
                    proj(0, 1)
                    xn(0, 0)
                    xn(0, 1)
                    hT_(0, 0, 0)
                    hT_(0, 0, 1)
                    route(0, 0)
                    pe.wait_ge(s_cst, 10)
                    pe.wait_ge(s_wl2, 16)
                    chunk(0, 0, first=True)
                    with pe.Fori(0, NCH // 2 - 1) as i:
                        chunk(i * 2 + 1, 1)
                        chunk(i * 2 + 2, 0)
                    chunk(NCH - 1, 1, final=True)
                    down(NCH - 1, NE - 2)
                    down(NCH - 1, NE - 1)

                @block.vector
                def _(dve):
                    link = linker(dve)
                    link(nc.vector.reduce_max(oext[:, 0:1], omx[:, :], AXX))
                    nc.vector.tensor_reduce(oext[:, 1:2], omn[:, :], AXX, ALU.min, negate=True).then_inc(s_ext2, 2)
                    dve.wait_ge(s_all2, 1)
                    link(nc.vector.tensor_scalar(oexta[:, 1:2], oexta[:, 1:2], -1.0, None, ALU.mult))
                    quant_scalars(dve, link, oexta[:, 0:1], oexta[:, 1:2], osc[:, :], oinv[:, :], otop[:, :], otmp[:, :])
                    nc.vector.tensor_scalar(psc[:, :], pscale[:, :], osc[:, 0:1], None, ALU.mult).then_inc(s_osc, 1)
                    dve.wait_ge(s_dhi, 1)
                    nc.vector.tensor_tensor(flat(dlo), flat(draw), flat(dhi).bitcast(F32), ALU.subtract).then_inc(s_dlo, 1)

                    def ln_stats(n, h):
                        dve.wait_ge(s_xn, n * 2 + h + 1)
                        for t in range(2):
                            nc.vector.bn_stats(st6[:, 2 * h + t, :], pX[:, t * C:t * C + C]).then_inc(s_bn, 1)
                        for t in range(2):
                            wait_apart(dve, s_bn, n * NT + 2 * h + t + 1, s_tick)
                            nc.vector.bn_aggr(mv[:, 2 * h + t, :], st6[:, 2 * h + t, :]).then_inc(s_mv, 1)

                    def ln_apply(n, a, h):
                        dve.wait_ge(s_rs, n * 2 + h + 1)
                        for t in range(2):
                            q = 2 * h + t
                            nc.vector.tensor_scalar(h1[a][:, q, :], pX[:, t * C:t * C + C], mv[:, q, 0:1], rs[:, q:q + 1],
                                                    ALU.subtract, ALU.mult).then_inc(s_h1, 1)

                    def split(n, a, k):
                        dve.wait_ge(s_hT, n * 2 + k + 1)
                        nc.vector.tensor_copy(xh[a][:, k, :], pX[:, :]).then_inc(s_spl, 1)
                        dve.wait_ge(s_spl, n * 4 + 2 * k + 1)
                        nc.vector.tensor_tensor(xl[a][:, k, :], pX[:, :], xh[a][:, k, :].bitcast(F32), ALU.subtract).then_inc(s_spl, 1)

                    def top_groups(n, c):
                        dve.wait_ge(s_sig, n + 1)
                        c(nc.vector.tensor_tensor(scb[:, :, :], sg[:, :, :], eb[:, :].unsqueeze(1).broadcast_to([P, NT, E]), ALU.add))
                        v = scb[:, :, :].rearrange("p t (g a b) -> p (t g) a b", a=2, b=2)
                        c(nc.vector.tensor_tensor(pmx[:, :, :], v[:, :, :, 0], v[:, :, :, 1], ALU.max))
                        c(nc.vector.tensor_tensor(pmn[:, :, :], v[:, :, :, 0], v[:, :, :, 1], ALU.min))
                        c(nc.vector.tensor_tensor(g1[:, :], pmx[:, :, 0], pmx[:, :, 1], ALU.max))
                        c(nc.vector.tensor_tensor(g2[:, :], pmx[:, :, 0], pmx[:, :, 1], ALU.min))
                        c(nc.vector.tensor_tensor(g3[:, :], pmn[:, :, 0], pmn[:, :, 1], ALU.max))
                        c(nc.vector.tensor_tensor(g2[:, :], g2[:, :], g3[:, :], ALU.max))
                        c(nc.vector.tensor_tensor(gsum[:, :], g1[:, :], g2[:, :], ALU.add))
                        gs = gsum[:, :].rearrange("p (t g) -> p t g", g=4)
                        mine, other = gs.unsqueeze(3).broadcast_to([P, NT, 4, 4]), gs.unsqueeze(2).broadcast_to([P, NT, 4, 4])
                        c(nc.vector.tensor_tensor(cmp4[:, :, :, :], other, mine, ALU.is_gt))
                        c(nc.vector.tensor_tensor(cmp4b[:, :, :, :], other, mine, ALU.is_equal))
                        c(nc.vector.tensor_tensor(cmp4b[:, :, :, :], cmp4b[:, :, :, :], lower4[:, :, :].unsqueeze(1).broadcast_to([P, NT, 4, 4]), ALU.mult))
                        c(nc.vector.tensor_tensor(cmp4[:, :, :, :], cmp4[:, :, :, :], cmp4b[:, :, :, :], ALU.add))
                        c(nc.vector.tensor_reduce(grank[:, :], cmp4[:, :, :, :].rearrange("p t g o -> p (t g) o"), AXX, ALU.add))
                        c(nc.vector.tensor_scalar(gsel[:, :], grank[:, :], 2.0, None, ALU.is_lt))
                        c(nc.vector.tensor_tensor(msk[:, :, :].rearrange("p t (g e) -> p (t g) e", e=4), scb[:, :, :].rearrange("p t (g e) -> p (t g) e", e=4),
                                                  gsel[:, :].unsqueeze(2).broadcast_to([P, 16, 4]), ALU.mult))

                    def top_experts(n, c):
                        mine, other = msk[:, :, :].unsqueeze(3).broadcast_to([P, NT, E, E]), msk[:, :, :].unsqueeze(2).broadcast_to([P, NT, E, E])
                        c(nc.vector.tensor_tensor(cmp16[:, :, :, :], other, mine, ALU.is_ge))
                        c(nc.vector.tensor_tensor(cmp16[:, :, :, :], cmp16[:, :, :, :], lower16[:, :, :].unsqueeze(1).broadcast_to([P, NT, E, E]), ALU.mult))
                        c(nc.vector.tensor_reduce(rrow[:, :, :], cmp16[:, :, :, :], AXX, ALU.add))
                        c(nc.vector.tensor_reduce(rcol[:, :, :], cmp16[:, :, :, :].rearrange("p t e o -> p t o e"), AXX, ALU.add))

                    def weights(n, c):
                        c(nc.vector.tensor_tensor(rrow[:, :, :], rrow[:, :, :], rcol[:, :, :], ALU.subtract))
                        c(nc.vector.tensor_tensor(rrow[:, :, :], rrow[:, :, :], rest15[:, :].unsqueeze(1).broadcast_to([P, NT, E]), ALU.add))
                        c(nc.vector.scalar_tensor_tensor(comb[:, :, :], rrow[:, :, :], 4.0, sg[:, :, :], ALU.is_lt, ALU.mult))
                        c(nc.vector.tensor_reduce(wsum[:, :], comb[:, :, :], AXX, ALU.add))
                        c(nc.vector.tensor_scalar(wsum[:, :], wsum[:, :], 1e-20, None, ALU.add))
                        c(nc.vector.reciprocal(wsum[:, :], wsum[:, :]))
                        c(nc.vector.tensor_scalar(wsum[:, :], wsum[:, :], 2.5, None, ALU.mult))
                        c(nc.vector.tensor_tensor(comb[:, :, :], comb[:, :, :], wsum[:, :].unsqueeze(2).broadcast_to([P, NT, E]), ALU.mult))
                        dve.wait_ge(s_cT, n)
                        nc.vector.tensor_copy(cpart[:, :, 0, :], comb[:, :, :]).then_inc(s_cb, 1)
                        dve.wait_ge(s_cb, n * 3 + 1)
                        c(nc.vector.tensor_tensor(crest[:, :, :], comb[:, :, :], cpart[:, :, 0, :], ALU.subtract))
                        nc.vector.tensor_copy(cpart[:, :, 1, :], crest[:, :, :]).then_inc(s_cb, 1)
                        dve.wait_ge(s_cb, n * 3 + 2)
                        nc.vector.tensor_tensor(cpart[:, :, 2, :], crest[:, :, :], cpart[:, :, 1, :], ALU.subtract).then_inc(s_cb, 1)

                    def combT(n, a):
                        dve.wait_ge(s_cT, n + 1)
                        nc.vector.tensor_copy(cT[a][:, :], pXb[0:3 * E, 0:CH]).then_inc(s_cTs, 1)

                    def chain(n):
                        return Chain(dve, s_route, n, 28)

                    def finish(n, a):
                        dve.wait_ge(s_dn, n * NE + NE)
                        for h in range(2):
                            nc.vector.tensor_tensor(ys[:, 2 * h:2 * h + 2, :], pA[h][:, :, :], h1[a][:, 2 * h:2 * h + 2, :], ALU.add).then_inc(s_y2, 1)

                    def finish_stats(n):
                        for t in range(NT):
                            dve.wait_ge(s_y2, n * 2 + t // 2 + 1)
                            nc.vector.bn_stats(st6b[:, t, :], ys[:, t, :]).then_inc(s_bn2, 1)
                        for t in range(NT):
                            wait_apart(dve, s_bn2, n * NT + t + 1, s_tick)
                            nc.vector.bn_aggr(mvb[:, t, :], st6b[:, t, :]).then_inc(s_mv2, 1)

                    def finish_out(n):
                        dve.wait_ge(s_rs2, n + 1)
                        dve.wait_ge(s_out, n * 16 + 16)
                        for t in range(NT):
                            nc.vector.tensor_scalar(yo[:, t, :], ys[:, t, :], mvb[:, t, 0:1], rsb[:, t:t + 1],
                                                    ALU.subtract, ALU.mult).then_inc(s_yo, 1)

                    nc.vector.memset(yo[:], 0.0).then_inc(s_out, 16)
                    for h in range(2):
                        ln_stats(0, h)
                        ln_apply(0, 0, h)
                    split(0, 0, 0)
                    split(0, 0, 1)
                    dve.wait_ge(s_cst, 10)
                    dve.wait_ge(s_wl2, 16)
                    c = chain(0)
                    top_groups(0, c)
                    top_experts(0, c)
                    weights(0, c)
                    c.close()
                    combT(0, 0)

                    def chunk(n, a, first=False, final=False):
                        c = chain(n + 1)
                        for e in range(NE):
                            q = n * NE + e
                            dve.wait_ge(s_silu, q + 1)
                            src = sl[e % 2]
                            if e < E:
                                dve.wait_ge(s_C, n * E + e + 1)
                                nc.vector.tensor_tensor(sc_[e % 2][:, :], sl[e % 2][:, :], pC[:, :], ALU.mult).then_inc(s_t1, 1)
                                dve.wait_ge(s_t1, n * E + e + 1)
                                src = sc_[e % 2]
                            dve.wait_ge(s_U, q + 1)
                            if not (first and e < 2):
                                dve.wait_ge(s_pl, q - 1)
                            nc.vector.tensor_tensor(prod[e % 2][:, :], src[:, :], pU[e % 2][:, :], ALU.mult).then_inc(s_prod, 1)
                            if not first:
                                if e == 1:
                                    finish(n - 1, 1 - a)
                                if e == 2:
                                    finish_stats(n - 1)
                                if e == 4:
                                    finish_out(n - 1)
                            if not final:
                                if e in (5, 7):
                                    ln_stats(n + 1, (e - 5) // 2)
                                if e in (6, 8):
                                    ln_apply(n + 1, 1 - a, (e - 6) // 2)
                                if e in (9, 10):
                                    split(n + 1, 1 - a, e - 9)
                                if e == 12:
                                    top_groups(n + 1, c)
                                if e == 13:
                                    top_experts(n + 1, c)
                                if e == 14:
                                    weights(n + 1, c)
                                    c.close()
                                if e == 16:
                                    combT(n + 1, 1 - a)
                    chunk(0, 0, first=True)
                    with dve.Fori(0, NCH // 2 - 1) as i:
                        chunk(i * 2 + 1, 1)
                        chunk(i * 2 + 2, 0)
                    chunk(NCH - 1, 1, final=True)
                    finish(NCH - 1, 1)
                    finish_stats(NCH - 1)
                    finish_out(NCH - 1)
                    linked(link)


def kernel(**inputs):
    import numpy as np
    import concourse.bacc as bacc
    from concourse.bass_utils import run_bass_kernel_spmd

    a = {k: np.asarray(v) for k, v in inputs.items()}
    gate, up, down = a["L0_ffn_gate_w"], a["L0_ffn_up_w"], a["L0_ffn_down_w"]
    gate = np.concatenate([gate, a["L0_ffn_sh_gate_w"].reshape(2, I, C)])
    up = np.concatenate([up, a["L0_ffn_sh_up_w"].reshape(2, I, C)])
    down = np.concatenate([down, a["L0_ffn_sh_down_w"].reshape(C, 2, I).transpose(1, 0, 2)])
    by_c = lambda w: np.ascontiguousarray(w.reshape(NE, I, KC, P).transpose(3, 2, 0, 1))
    arrays = {
        "x": np.ascontiguousarray(a["x"].reshape(B, 3, 2, P, C).transpose(0, 3, 1, 2, 4)),
        "scharr": a["L0_tok_scharr"],
        "qkv_w": a["L0_attn_qkv_w"], "qkv_b": a["L0_attn_qkv_b"],
        "qkv_b_col": np.ascontiguousarray(a["L0_attn_qkv_b"].reshape(6, P).T),
        "proj_w": a["L0_attn_proj_w"],
        "proj_b_col": np.ascontiguousarray(a["L0_attn_proj_b"].reshape(KC, P).T),
        "router_t": np.ascontiguousarray(a["L0_ffn_router_weight"].reshape(E, KC, P).transpose(2, 1, 0)),
        "e_bias": a["L0_ffn_e_bias"],
        "gate_t": by_c(gate), "up_t": by_c(up),
        "down_t": np.ascontiguousarray(down.transpose(2, 0, 1)),
    }
    nc = bacc.Bacc("TRN2", target_bir_lowering=False, num_devices=1)
    args = [nc.dram_tensor(n, v.shape, mybir.dt.from_np(v.dtype), kind="ExternalInput").ap() for n, v in arrays.items()]
    args.append(nc.dram_tensor("out", (B, 256, 256), F32, kind="ExternalOutput").ap())
    build(nc, *args)
    r = run_bass_kernel_spmd(nc, [arrays], core_ids=[0])
    return r.results[0]["out"]
```
